# Optimizing a Trainium2 kernel written in Bass

```python
import numpy as np
import jax
import jax.numpy as jnp

def _softmax(x, axis=-1):
    return jax.nn.softmax(x, axis=axis)

def _gelu(x):
    return jax.nn.gelu(x, approximate=True)

def _silu(x):
    return jax.nn.silu(x)

def _sigmoid(x):
    return jax.nn.sigmoid(x)

def _layernorm(x, axis=-1, eps=1e-05):
    m = jnp.mean(x, axis=axis, keepdims=True)
    v = jnp.var(x, axis=axis, keepdims=True)
    return (x - m) / jnp.sqrt(v + eps)

def _scatter_add(tgt, idx, src, axis=0):
    return tgt.at[idx].add(src)

def _segment_sum(src, seg, n):
    return jax.ops.segment_sum(src, seg, n)
kernel_name = 'mk_perceiver_d2_seqx_r8_c7d524'

def setup_inputs(seed: int=0):
    np.random.seed(seed)
    _w = jnp.asarray

    def _rec_inputs():
        import jax
        import jax.numpy as jnp
        _rk = jax.random.key(seed)
        x = -0.0005146 + 1 * jax.random.normal(jax.random.fold_in(_rk, 1), (32, 32, 128), jnp.float32)
        _lenS = 32 - jax.random.randint(jax.random.fold_in(_rk, 7), (32,), 0, max(1, 32 // 4) + 1, jnp.int32)
        _lenS2 = 257 - jax.random.randint(jax.random.fold_in(_rk, 8), (32,), 0, max(1, 257 // 4) + 1, jnp.int32)
        _ctx_768P = jax.random.normal(jax.random.fold_in(_rk, 11), (32, 16, 96), jnp.float32)
        _ctx_768c = jax.random.dirichlet(jax.random.fold_in(_rk, 511), 0.3 * jnp.ones((16,), jnp.float32), (32, 257))
        _ctx_768t = jnp.einsum('bsk,bkd->bsd', _ctx_768c, _ctx_768P)
        _ctx_768t = _ctx_768t * jax.lax.rsqrt(jnp.mean(jnp.square(_ctx_768t)) + 1e-12) * 0.953939
        ctx_768 = -0.00040386 + 0.999972 * (_ctx_768t + 0.3 * jax.random.normal(jax.random.fold_in(_rk, 611), (32, 257, 96), jnp.float32))
        _validS = jnp.arange(32)[None, :] < _lenS[:, None]
        _validS2 = jnp.arange(257)[None, :] < _lenS2[:, None]
        _causal = jnp.tril(jnp.ones((32, 32), dtype=bool))
        mask_BxS2_bk0 = jnp.logical_not(jnp.broadcast_to(_validS2[:, :], (32, 257)))
        return (x, ctx_768, mask_BxS2_bk0)
    x, ctx_768, mask_BxS2_bk0 = _rec_inputs()

    def _L0_xattn_setup():
        import jax, jax.numpy as jnp
        import numpy as np
        DIM_IN, DIM_LAT, DIM_HEAD = (96, 128, 64)
        INNER = max(DIM_LAT, DIM_IN)
        HEADS = INNER // DIM_HEAD
        SCALE = DIM_HEAD ** (-0.5)
        RMS_EPS = 1e-08
        LN_EPS = 1e-05

        def layernorm(x, g, b):
            mu = jnp.mean(x, axis=-1, keepdims=True)
            var = jnp.mean((x - mu) ** 2, axis=-1, keepdims=True)
            return (x - mu) * jax.lax.rsqrt(var + LN_EPS) * g + b

        def rmsnorm(x, gamma):
            norm = jnp.sqrt(jnp.sum(x * x, axis=-1, keepdims=True)) * x.shape[-1] ** (-0.5)
            return x / jnp.maximum(norm, RMS_EPS) * gamma
        key = jax.random.key(seed)
        ks = jax.random.split(key, 12)
        b, n, m = (4, 512, 64)
        x = jax.random.normal(ks[0], (b, n, DIM_IN), jnp.float32)
        latents = jax.random.normal(ks[1], (b, m, DIM_LAT), jnp.float32)
        mask = jax.random.randint(ks[2], (b, n), 0, 2).astype(bool)
        s = lambda k, sh, fan: jax.random.normal(k, sh, jnp.float32) * fan ** (-0.5)
        return {'x': x, 'latents': latents, 'mask': mask, 'ln_x_g': jnp.ones((DIM_IN,), jnp.float32), 'ln_x_b': jnp.zeros((DIM_IN,), jnp.float32), 'ln_l_g': jnp.ones((DIM_LAT,), jnp.float32), 'ln_l_b': jnp.zeros((DIM_LAT,), jnp.float32), 'qn_g': jnp.ones((DIM_HEAD,), jnp.float32), 'kn_g': jnp.ones((DIM_HEAD,), jnp.float32), 'Wq': s(ks[3], (INNER, DIM_LAT), DIM_LAT), 'Wkv': s(ks[4], (2 * INNER, DIM_IN), DIM_IN), 'Wlkv': s(ks[5], (2 * INNER, DIM_LAT), DIM_LAT), 'Wo': s(ks[6], (DIM_LAT, INNER), INNER), 'bo': jnp.zeros((DIM_LAT,), jnp.float32)}
    _L0_xattn_all = _L0_xattn_setup()
    _L0_xattn_in = {k: v for k, v in _L0_xattn_all.items() if k in ('ln_x_g', 'ln_x_b', 'ln_l_g', 'ln_l_b', 'qn_g', 'kn_g', 'Wq', 'Wkv', 'Wlkv', 'Wo', 'bo')}
    del _L0_xattn_all

    def _L0_attn_setup():
        import jax, jax.numpy as jnp
        import numpy as np
        import math
        NUM_HEADS = 8
        D_HEAD = 128
        DEPTH = 1
        LAMBDA_INIT = 0.8 - 0.6 * math.exp(-0.3 * DEPTH)
        EPS = 1e-05
        key = jax.random.key(seed)
        ks = jax.random.split(key, 10)
        B, N, D = (2, 256, 128)
        s = 0.02
        return {'X': jax.random.normal(ks[0], (B, N, D), jnp.float32), 'Wq': jax.random.normal(ks[1], (2 * D_HEAD * NUM_HEADS, D), jnp.float32) * s, 'Wk': jax.random.normal(ks[2], (2 * D_HEAD * NUM_HEADS, D), jnp.float32) * s, 'Wv': jax.random.normal(ks[3], (2 * D_HEAD * NUM_HEADS, D), jnp.float32) * s, 'Wo': jax.random.normal(ks[4], (D, 2 * D_HEAD * NUM_HEADS), jnp.float32) * s, 'lambda_q1': jax.random.normal(ks[5], (NUM_HEADS, D_HEAD), jnp.float32) * 0.1, 'lambda_k1': jax.random.normal(ks[6], (NUM_HEADS, D_HEAD), jnp.float32) * 0.1, 'lambda_q2': jax.random.normal(ks[7], (NUM_HEADS, D_HEAD), jnp.float32) * 0.1, 'lambda_k2': jax.random.normal(ks[8], (NUM_HEADS, D_HEAD), jnp.float32) * 0.1, 'rms_scale': jnp.ones((2 * D_HEAD,), jnp.float32)}
    _L0_attn_all = _L0_attn_setup()
    _L0_attn_in = {k: v for k, v in _L0_attn_all.items() if k in ('Wq', 'Wk', 'Wv', 'Wo', 'lambda_q1', 'lambda_k1', 'lambda_q2', 'lambda_k2', 'rms_scale')}
    del _L0_attn_all

    def _L0_ffn_setup():
        import jax, jax.numpy as jnp
        import numpy as np
        DIM = 128
        HID = 352
        E = 8
        TOP_K = 2
        EPS = 1e-06

        def _rmsnorm(x, w):
            var = jnp.mean(jnp.square(x), axis=-1, keepdims=True)
            return x * jax.lax.rsqrt(var + EPS) * w
        key = jax.random.key(seed)
        ks = jax.random.split(key, 5)
        x = jax.random.normal(ks[0], (4, 256, DIM), dtype=jnp.float32)
        norm_weight = jnp.ones((DIM,), dtype=jnp.float32)
        router_weight = jax.random.normal(ks[1], (E, DIM), dtype=jnp.float32) * 0.02
        gate_up_weight = jax.random.normal(ks[2], (E, 2 * HID, DIM), dtype=jnp.float32) * (0.02 / np.sqrt(E))
        down_weight = jax.random.normal(ks[3], (E, DIM, HID), dtype=jnp.float32) * (0.02 / np.sqrt(E))
        residual_alpha = jnp.float32(1.0)
        return {'x': x, 'norm_weight': norm_weight, 'router_weight': router_weight, 'gate_up_weight': gate_up_weight, 'down_weight': down_weight, 'residual_alpha': residual_alpha}
    _L0_ffn_all = _L0_ffn_setup()
    _L0_ffn_in = {k: v for k, v in _L0_ffn_all.items() if k in ('norm_weight', 'router_weight', 'gate_up_weight', 'down_weight', 'residual_alpha')}
    del _L0_ffn_all

    def _L1_xattn_setup():
        import jax, jax.numpy as jnp
        import numpy as np
        N_HEADS = 8
        D_EMBED = 128
        D_CROSS = 96
        D_HEAD = D_EMBED // N_HEADS
        key = jax.random.key(seed)
        ks = jax.random.split(key, 10)
        B, Lq, Lkv = (16, 512, 77)
        s_e = 1.0 / np.sqrt(D_EMBED)
        s_c = 1.0 / np.sqrt(D_CROSS)
        return {'x': jax.random.normal(ks[0], (B, Lq, D_EMBED), jnp.float32), 'y': jax.random.normal(ks[1], (B, Lkv, D_CROSS), jnp.float32), 'Wq': jax.random.normal(ks[2], (D_EMBED, D_EMBED), jnp.float32) * s_e, 'bq': jnp.zeros((D_EMBED,), jnp.float32), 'Wk': jax.random.normal(ks[3], (D_CROSS, D_EMBED), jnp.float32) * s_c, 'bk': jnp.zeros((D_EMBED,), jnp.float32), 'Wv': jax.random.normal(ks[4], (D_CROSS, D_EMBED), jnp.float32) * s_c, 'bv': jnp.zeros((D_EMBED,), jnp.float32), 'Wo': jax.random.normal(ks[5], (D_EMBED, D_EMBED), jnp.float32) * s_e, 'bo': jnp.zeros((D_EMBED,), jnp.float32)}
    _L1_xattn_all = _L1_xattn_setup()
    _L1_xattn_in = {k: v for k, v in _L1_xattn_all.items() if k in ('Wq', 'bq', 'Wk', 'bk', 'Wv', 'bv', 'Wo', 'bo')}
    del _L1_xattn_all

    def _L1_attn_setup():
        import jax, jax.numpy as jnp
        import numpy as np
        B, T, D = (4, 256, 128)
        HID = 2 * D
        EPS = 1e-06

        def _rmsnorm(x, w):
            return x * jax.lax.rsqrt(jnp.mean(x * x, axis=-1, keepdims=True) + EPS) * w

        def _ema_scan(v, alpha):

            def step(prev, v_t):
                cur = alpha * v_t + (1.0 - alpha) * prev
                return (cur, cur)
            v_tm = jnp.swapaxes(v, 0, 1)
            _, out = jax.lax.scan(step, jnp.zeros(v.shape[::2], v.dtype), v_tm)
            return jnp.swapaxes(out, 0, 1)

        def _delta_scan(q, k, v, beta):

            def step(S, inp):
                q_t, k_t, v_t, b_t = inp
                Sk = jnp.einsum('bij,bj->bi', S, k_t)
                S = S + b_t[:, None, None] * (v_t - Sk)[:, :, None] * k_t[:, None, :]
                o_t = jnp.einsum('bij,bj->bi', S, q_t)
                return (S, o_t)
            tm = lambda a: jnp.swapaxes(a, 0, 1)
            S0 = jnp.zeros((q.shape[0], q.shape[2], q.shape[2]), q.dtype)
            _, out = jax.lax.scan(step, S0, (tm(q), tm(k), tm(v), tm(beta)))
            return jnp.swapaxes(out, 0, 1)
        key = jax.random.key(seed)
        ks = jax.random.split(key, 12)
        s = 0.02
        return {'x': jax.random.normal(ks[0], (B, T, D), jnp.float32), 'norm1_w': jnp.ones((D,), jnp.float32), 'Wq': jax.random.normal(ks[1], (D, D), jnp.float32) * s, 'Wk': jax.random.normal(ks[2], (D, D), jnp.float32) * s, 'Wv': jax.random.normal(ks[3], (D, D), jnp.float32) * s, 'beta_w': jax.random.normal(ks[4], (D, 1), jnp.float32) * s, 'beta_b': jnp.zeros((1,), jnp.float32), 'Wo': jax.random.normal(ks[5], (D, D), jnp.float32) * s, 'alpha_logit': jnp.full((D,), float(np.log(0.1 / 0.9)), jnp.float32), 'norm2_w': jnp.ones((D,), jnp.float32), 'w_gate': jax.random.normal(ks[6], (D, HID), jnp.float32) * s, 'w_up': jax.random.normal(ks[7], (D, HID), jnp.float32) * s, 'w_down': jax.random.normal(ks[8], (HID, D), jnp.float32) * s}
    _L1_attn_all = _L1_attn_setup()
    _L1_attn_in = {k: v for k, v in _L1_attn_all.items() if k in ('norm1_w', 'Wq', 'Wk', 'Wv', 'beta_w', 'beta_b', 'Wo', 'alpha_logit', 'norm2_w', 'w_gate', 'w_up', 'w_down')}
    del _L1_attn_all

    def _L1_ffn_setup():
        import jax, jax.numpy as jnp
        import numpy as np
        H = 16
        TOP_K = 2
        LN_EPS = 1e-05
        key = jax.random.key(seed)
        ks = jax.random.split(key, 8)
        B, S, E, NE = (2, 128, 128, 8)
        w = lambda k, shp: jax.random.normal(k, shp, dtype=jnp.float32) * 0.02
        return {'x': jax.random.normal(ks[0], (B, S, E), dtype=jnp.float32), 'rW1': w(ks[1], (E // 2, E)), 'rb1': jnp.zeros((E // 2,), jnp.float32), 'ln_g': jnp.ones((E // 2,), jnp.float32), 'ln_b': jnp.zeros((E // 2,), jnp.float32), 'rW2': w(ks[2], (NE, E // 2)), 'rb2': jnp.zeros((NE,), jnp.float32), 'qW': w(ks[3], (NE, E, E)), 'qb': jnp.zeros((NE, E), jnp.float32), 'kW': w(ks[4], (NE, E, E)), 'kb': jnp.zeros((NE, E), jnp.float32), 'vW': w(ks[5], (NE, E, E)), 'vb': jnp.zeros((NE, E), jnp.float32), 'oW': w(ks[6], (NE, E, E)), 'ob': jnp.zeros((NE, E), jnp.float32)}
    _L1_ffn_all = _L1_ffn_setup()
    _L1_ffn_in = {k: v for k, v in _L1_ffn_all.items() if k in ('rW1', 'rb1', 'ln_g', 'ln_b', 'rW2', 'rb2', 'qW', 'qb', 'kW', 'kb', 'vW', 'vb', 'oW', 'ob')}
    del _L1_ffn_all
    return {'x': x, 'ctx_768': ctx_768, 'mask_BxS2_bk0': mask_BxS2_bk0, 'L0_xattn_ln_x_g': _L0_xattn_in['ln_x_g'], 'L0_xattn_ln_x_b': _L0_xattn_in['ln_x_b'], 'L0_xattn_ln_l_g': _L0_xattn_in['ln_l_g'], 'L0_xattn_ln_l_b': _L0_xattn_in['ln_l_b'], 'L0_xattn_qn_g': _L0_xattn_in['qn_g'], 'L0_xattn_kn_g': _L0_xattn_in['kn_g'], 'L0_xattn_Wq': _L0_xattn_in['Wq'], 'L0_xattn_Wkv': _L0_xattn_in['Wkv'], 'L0_xattn_Wlkv': _L0_xattn_in['Wlkv'], 'L0_xattn_Wo': _L0_xattn_in['Wo'], 'L0_xattn_bo': _L0_xattn_in['bo'], 'L0_attn_Wq': _L0_attn_in['Wq'], 'L0_attn_Wk': _L0_attn_in['Wk'], 'L0_attn_Wv': _L0_attn_in['Wv'], 'L0_attn_Wo': _L0_attn_in['Wo'], 'L0_attn_lambda_q1': _L0_attn_in['lambda_q1'], 'L0_attn_lambda_k1': _L0_attn_in['lambda_k1'], 'L0_attn_lambda_q2': _L0_attn_in['lambda_q2'], 'L0_attn_lambda_k2': _L0_attn_in['lambda_k2'], 'L0_attn_rms_scale': _L0_attn_in['rms_scale'], 'L0_ffn_norm_weight': _L0_ffn_in['norm_weight'], 'L0_ffn_router_weight': _L0_ffn_in['router_weight'], 'L0_ffn_gate_up_weight': _L0_ffn_in['gate_up_weight'], 'L0_ffn_down_weight': _L0_ffn_in['down_weight'], 'L0_ffn_residual_alpha': _L0_ffn_in['residual_alpha'], 'L1_xattn_Wq': _L1_xattn_in['Wq'], 'L1_xattn_bq': _L1_xattn_in['bq'], 'L1_xattn_Wk': _L1_xattn_in['Wk'], 'L1_xattn_bk': _L1_xattn_in['bk'], 'L1_xattn_Wv': _L1_xattn_in['Wv'], 'L1_xattn_bv': _L1_xattn_in['bv'], 'L1_xattn_Wo': _L1_xattn_in['Wo'], 'L1_xattn_bo': _L1_xattn_in['bo'], 'L1_attn_norm1_w': _L1_attn_in['norm1_w'], 'L1_attn_Wq': _L1_attn_in['Wq'], 'L1_attn_Wk': _L1_attn_in['Wk'], 'L1_attn_Wv': _L1_attn_in['Wv'], 'L1_attn_beta_w': _L1_attn_in['beta_w'], 'L1_attn_beta_b': _L1_attn_in['beta_b'], 'L1_attn_Wo': _L1_attn_in['Wo'], 'L1_attn_alpha_logit': _L1_attn_in['alpha_logit'], 'L1_attn_norm2_w': _L1_attn_in['norm2_w'], 'L1_attn_w_gate': _L1_attn_in['w_gate'], 'L1_attn_w_up': _L1_attn_in['w_up'], 'L1_attn_w_down': _L1_attn_in['w_down'], 'L1_ffn_rW1': _L1_ffn_in['rW1'], 'L1_ffn_rb1': _L1_ffn_in['rb1'], 'L1_ffn_ln_g': _L1_ffn_in['ln_g'], 'L1_ffn_ln_b': _L1_ffn_in['ln_b'], 'L1_ffn_rW2': _L1_ffn_in['rW2'], 'L1_ffn_rb2': _L1_ffn_in['rb2'], 'L1_ffn_qW': _L1_ffn_in['qW'], 'L1_ffn_qb': _L1_ffn_in['qb'], 'L1_ffn_kW': _L1_ffn_in['kW'], 'L1_ffn_kb': _L1_ffn_in['kb'], 'L1_ffn_vW': _L1_ffn_in['vW'], 'L1_ffn_vb': _L1_ffn_in['vb'], 'L1_ffn_oW': _L1_ffn_in['oW'], 'L1_ffn_ob': _L1_ffn_in['ob']}

def reference(x, ctx_768, mask_BxS2_bk0, L0_xattn_ln_x_g, L0_xattn_ln_x_b, L0_xattn_ln_l_g, L0_xattn_ln_l_b, L0_xattn_qn_g, L0_xattn_kn_g, L0_xattn_Wq, L0_xattn_Wkv, L0_xattn_Wlkv, L0_xattn_Wo, L0_xattn_bo, L0_attn_Wq, L0_attn_Wk, L0_attn_Wv, L0_attn_Wo, L0_attn_lambda_q1, L0_attn_lambda_k1, L0_attn_lambda_q2, L0_attn_lambda_k2, L0_attn_rms_scale, L0_ffn_norm_weight, L0_ffn_router_weight, L0_ffn_gate_up_weight, L0_ffn_down_weight, L0_ffn_residual_alpha, L1_xattn_Wq, L1_xattn_bq, L1_xattn_Wk, L1_xattn_bk, L1_xattn_Wv, L1_xattn_bv, L1_xattn_Wo, L1_xattn_bo, L1_attn_norm1_w, L1_attn_Wq, L1_attn_Wk, L1_attn_Wv, L1_attn_beta_w, L1_attn_beta_b, L1_attn_Wo, L1_attn_alpha_logit, L1_attn_norm2_w, L1_attn_w_gate, L1_attn_w_up, L1_attn_w_down, L1_ffn_rW1, L1_ffn_rb1, L1_ffn_ln_g, L1_ffn_ln_b, L1_ffn_rW2, L1_ffn_rb2, L1_ffn_qW, L1_ffn_qb, L1_ffn_kW, L1_ffn_kb, L1_ffn_vW, L1_ffn_vb, L1_ffn_oW, L1_ffn_ob):
    import jax
    import jax.numpy as jnp

    def _L0_xattn_ref(x, latents, mask, ln_x_g, ln_x_b, ln_l_g, ln_l_b, qn_g, kn_g, Wq, Wkv, Wlkv, Wo, bo):
        import jax, jax.numpy as jnp
        import numpy as np
        DIM_IN, DIM_LAT, DIM_HEAD = (96, 128, 64)
        INNER = max(DIM_LAT, DIM_IN)
        HEADS = INNER // DIM_HEAD
        SCALE = DIM_HEAD ** (-0.5)
        RMS_EPS = 1e-08
        LN_EPS = 1e-05

        def layernorm(x, g, b):
            mu = jnp.mean(x, axis=-1, keepdims=True)
            var = jnp.mean((x - mu) ** 2, axis=-1, keepdims=True)
            return (x - mu) * jax.lax.rsqrt(var + LN_EPS) * g + b

        def rmsnorm(x, gamma):
            norm = jnp.sqrt(jnp.sum(x * x, axis=-1, keepdims=True)) * x.shape[-1] ** (-0.5)
            return x / jnp.maximum(norm, RMS_EPS) * gamma
        b, n, _ = x.shape
        m = latents.shape[1]
        xn = layernorm(x, ln_x_g, ln_x_b)
        ln = layernorm(latents, ln_l_g, ln_l_b)
        q = ln @ Wq.T
        kv = jnp.concatenate([xn @ Wkv.T, ln @ Wlkv.T], axis=1)
        k, v = (kv[..., :INNER], kv[..., INNER:])
        split_heads = lambda t: t.reshape(t.shape[0], t.shape[1], HEADS, DIM_HEAD).transpose(0, 2, 1, 3)
        q, k, v = (split_heads(q), split_heads(k), split_heads(v))
        qn = rmsnorm(q, qn_g) * SCALE
        kn = rmsnorm(k, kn_g)
        attn = jnp.einsum('bhid,bhjd->bhij', qn, kn)
        full_mask = jnp.pad(mask, ((0, 0), (0, m)), constant_values=True)
        attn = jnp.where(full_mask[:, None, None, :], attn, -jnp.finfo(attn.dtype).max)
        attn = jax.nn.softmax(attn, axis=-1)
        out = jnp.einsum('bhij,bhjd->bhid', attn, v)
        out = out.transpose(0, 2, 1, 3).reshape(b, m, INNER)
        return out @ Wo.T + bo

    def _L0_attn_ref(X, Wq, Wk, Wv, Wo, lambda_q1, lambda_k1, lambda_q2, lambda_k2, rms_scale):
        import jax, jax.numpy as jnp
        import numpy as np
        import math
        NUM_HEADS = 8
        D_HEAD = 128
        DEPTH = 1
        LAMBDA_INIT = 0.8 - 0.6 * math.exp(-0.3 * DEPTH)
        EPS = 1e-05
        B, N, D = X.shape
        H, dh = (NUM_HEADS, D_HEAD)

        def proj(W):
            y = jnp.einsum('bnd,ed->bne', X, W)
            return y.reshape(B, N, H, 2 * dh).transpose(0, 2, 1, 3)
        Q = proj(Wq)
        K = proj(Wk)
        V = proj(Wv)
        Q1, Q2 = (Q[..., :dh], Q[..., dh:])
        K1, K2 = (K[..., :dh], K[..., dh:])
        lam1 = jnp.exp(jnp.sum(lambda_q1 * lambda_k1, axis=-1))
        lam2 = jnp.exp(jnp.sum(lambda_q2 * lambda_k2, axis=-1))
        lam = (lam1 - lam2 + LAMBDA_INIT)[None, :, None, None]
        scaling = 1.0 / math.sqrt(dh)
        A1 = jnp.einsum('bhqd,bhkd->bhqk', Q1, K1) * scaling
        A2 = jnp.einsum('bhqd,bhkd->bhqk', Q2, K2) * scaling
        attn = jax.nn.softmax(A1, axis=-1) - lam * jax.nn.softmax(A2, axis=-1)
        O = jnp.einsum('bhqk,bhkd->bhqd', attn, V)
        rms = jnp.sqrt(jnp.mean(O * O, axis=-1, keepdims=True) + EPS)
        O = O / rms * rms_scale
        O = O * (1.0 - LAMBDA_INIT)
        O = O.transpose(0, 2, 1, 3).reshape(B, N, H * 2 * dh)
        return jnp.einsum('bne,de->bnd', O, Wo)

    def _L0_ffn_ref(x, norm_weight, router_weight, gate_up_weight, down_weight, residual_alpha):
        import jax, jax.numpy as jnp
        import numpy as np
        DIM = 128
        HID = 352
        E = 8
        TOP_K = 2
        EPS = 1e-06

        def _rmsnorm(x, w):
            var = jnp.mean(jnp.square(x), axis=-1, keepdims=True)
            return x * jax.lax.rsqrt(var + EPS) * w
        normed = _rmsnorm(x, norm_weight)
        logits = jnp.einsum('bsd,ed->bse', normed, router_weight)
        probs = jax.nn.softmax(logits, axis=-1)
        topk_w, topk_idx = jax.lax.top_k(probs, TOP_K)
        topk_w = topk_w / jnp.sum(topk_w, axis=-1, keepdims=True)
        combine = jnp.sum(jax.nn.one_hot(topk_idx, E, dtype=normed.dtype) * topk_w[..., None], axis=-2)
        moe_out = jnp.zeros_like(x)
        for e in range(E):
            gu = jnp.einsum('bsd,hd->bsh', normed, gate_up_weight[e])
            gate, up = (gu[..., :HID], gu[..., HID:])
            hidden = jax.nn.silu(gate) * up
            out_e = jnp.einsum('bsh,dh->bsd', hidden, down_weight[e])
            moe_out = moe_out + combine[..., e, None] * out_e
        alpha = jnp.clip(residual_alpha, -0.5, 2.0)
        return x + alpha * moe_out

    def _L1_xattn_ref(x, y, Wq, bq, Wk, bk, Wv, bv, Wo, bo):
        import jax, jax.numpy as jnp
        import numpy as np
        N_HEADS = 8
        D_EMBED = 128
        D_CROSS = 96
        D_HEAD = D_EMBED // N_HEADS
        q = jnp.einsum('bqd,de->bqe', x, Wq) + bq
        k = jnp.einsum('bkc,ce->bke', y, Wk) + bk
        v = jnp.einsum('bkc,ce->bke', y, Wv) + bv
        scale = 1.0 / np.sqrt(D_HEAD)
        scores = jnp.einsum('bqe,bke->bqk', q, k) * scale
        attn = jax.nn.softmax(scores, axis=-1)
        out = jnp.einsum('bqk,bke->bqe', attn, v)
        return jnp.einsum('bqe,ef->bqf', out, Wo) + bo

    def _L1_attn_ref(x, norm1_w, Wq, Wk, Wv, beta_w, beta_b, Wo, alpha_logit, norm2_w, w_gate, w_up, w_down):
        import jax, jax.numpy as jnp
        import numpy as np
        B, T, D = (4, 256, 128)
        HID = 2 * D
        EPS = 1e-06

        def _rmsnorm(x, w):
            return x * jax.lax.rsqrt(jnp.mean(x * x, axis=-1, keepdims=True) + EPS) * w

        def _ema_scan(v, alpha):

            def step(prev, v_t):
                cur = alpha * v_t + (1.0 - alpha) * prev
                return (cur, cur)
            v_tm = jnp.swapaxes(v, 0, 1)
            _, out = jax.lax.scan(step, jnp.zeros(v.shape[::2], v.dtype), v_tm)
            return jnp.swapaxes(out, 0, 1)

        def _delta_scan(q, k, v, beta):

            def step(S, inp):
                q_t, k_t, v_t, b_t = inp
                Sk = jnp.einsum('bij,bj->bi', S, k_t)
                S = S + b_t[:, None, None] * (v_t - Sk)[:, :, None] * k_t[:, None, :]
                o_t = jnp.einsum('bij,bj->bi', S, q_t)
                return (S, o_t)
            tm = lambda a: jnp.swapaxes(a, 0, 1)
            S0 = jnp.zeros((q.shape[0], q.shape[2], q.shape[2]), q.dtype)
            _, out = jax.lax.scan(step, S0, (tm(q), tm(k), tm(v), tm(beta)))
            return jnp.swapaxes(out, 0, 1)
        h = _rmsnorm(x, norm1_w)
        q = h @ Wq
        k = h @ Wk
        k = k / jnp.maximum(jnp.linalg.norm(k, axis=-1, keepdims=True), 1e-12)
        v = h @ Wv
        v = _ema_scan(v, jax.nn.sigmoid(alpha_logit))
        beta = jax.nn.sigmoid(h @ beta_w + beta_b)[..., 0]
        attn_out = _delta_scan(q, k, v, beta)
        x = x + attn_out @ Wo
        h2 = _rmsnorm(x, norm2_w)
        mlp = jax.nn.silu(h2 @ w_gate) * (h2 @ w_up) @ w_down
        return x + mlp

    def _L1_ffn_ref(x, rW1, rb1, ln_g, ln_b, rW2, rb2, qW, qb, kW, kb, vW, vb, oW, ob):
        import jax, jax.numpy as jnp
        import numpy as np
        H = 16
        TOP_K = 2
        LN_EPS = 1e-05
        B, S, E = x.shape
        NE = qW.shape[0]
        Dh = E // H
        scale = 1.0 / jnp.sqrt(jnp.asarray(Dh, x.dtype))
        h = x @ rW1.T + rb1
        mu = h.mean(-1, keepdims=True)
        var = ((h - mu) ** 2).mean(-1, keepdims=True)
        h = (h - mu) * jax.lax.rsqrt(var + LN_EPS) * ln_g + ln_b
        h = jax.nn.relu(h)
        logits = h @ rW2.T + rb2
        probs = jax.nn.softmax(logits, axis=-1)
        tp, ti = jax.lax.top_k(probs, TOP_K)
        tp = tp / tp.sum(-1, keepdims=True)
        expert_mask = (jax.nn.one_hot(ti, NE, dtype=probs.dtype) * tp[..., None]).sum(-2)
        gates = jnp.moveaxis(expert_mask, -1, 0)

        def expert_step(acc, params):
            qw, qb_, kw, kb_, vw, vb_, ow, ob_, g = params
            q = (x @ qw.T + qb_).reshape(B, S, H, Dh).transpose(0, 2, 1, 3)
            k = (x @ kw.T + kb_).reshape(B, S, H, Dh).transpose(0, 2, 1, 3)
            v = (x @ vw.T + vb_).reshape(B, S, H, Dh).transpose(0, 2, 1, 3)
            scores = jnp.einsum('bhqd,bhkd->bhqk', q, k) * scale
            p = jax.nn.softmax(scores, axis=-1)
            o = jnp.einsum('bhqk,bhkd->bhqd', p, v)
            o = o.transpose(0, 2, 1, 3).reshape(B, S, E) @ ow.T + ob_
            return (acc + o * g[..., None], None)
        out, _ = jax.lax.scan(expert_step, jnp.zeros_like(x), (qW, qb, kW, kb, vW, vb, oW, ob, gates))
        return out
    x = x + _L0_xattn_ref(ctx_768, _layernorm(x, axis=-1), mask_BxS2_bk0, L0_xattn_ln_x_g, L0_xattn_ln_x_b, L0_xattn_ln_l_g, L0_xattn_ln_l_b, L0_xattn_qn_g, L0_xattn_kn_g, L0_xattn_Wq, L0_xattn_Wkv, L0_xattn_Wlkv, L0_xattn_Wo, L0_xattn_bo)
    x = x + _L0_attn_ref(_layernorm(x, axis=-1), L0_attn_Wq, L0_attn_Wk, L0_attn_Wv, L0_attn_Wo, L0_attn_lambda_q1, L0_attn_lambda_k1, L0_attn_lambda_q2, L0_attn_lambda_k2, L0_attn_rms_scale)
    x = x + _L0_ffn_ref(_layernorm(x, axis=-1), L0_ffn_norm_weight, L0_ffn_router_weight, L0_ffn_gate_up_weight, L0_ffn_down_weight, L0_ffn_residual_alpha)
    x = x + _L1_xattn_ref(_layernorm(x, axis=-1), ctx_768, L1_xattn_Wq, L1_xattn_bq, L1_xattn_Wk, L1_xattn_bk, L1_xattn_Wv, L1_xattn_bv, L1_xattn_Wo, L1_xattn_bo)
    x = x + _L1_attn_ref(_layernorm(x, axis=-1), L1_attn_norm1_w, L1_attn_Wq, L1_attn_Wk, L1_attn_Wv, L1_attn_beta_w, L1_attn_beta_b, L1_attn_Wo, L1_attn_alpha_logit, L1_attn_norm2_w, L1_attn_w_gate, L1_attn_w_up, L1_attn_w_down)
    x = x + _L1_ffn_ref(_layernorm(x, axis=-1), L1_ffn_rW1, L1_ffn_rb1, L1_ffn_ln_g, L1_ffn_ln_b, L1_ffn_rW2, L1_ffn_rb2, L1_ffn_qW, L1_ffn_qb, L1_ffn_kW, L1_ffn_kb, L1_ffn_vW, L1_ffn_vb, L1_ffn_oW, L1_ffn_ob)
    return x

_drawn_inputs = setup_inputs


def setup_inputs(seed=0):
    import zlib

    import numpy as np

    out = dict(_drawn_inputs(seed))
    spreads = {'L0_xattn_ln_x_g': (1.0, 0.2),
     'L0_xattn_ln_x_b': (0.0, 0.1),
     'L0_xattn_ln_l_g': (1.0, 0.2),
     'L0_xattn_ln_l_b': (0.0, 0.1),
     'L0_xattn_qn_g': (1.0, 0.2),
     'L0_xattn_kn_g': (1.0, 0.2),
     'L0_xattn_bo': (0.0, 0.1),
     'L0_attn_rms_scale': (1.0, 0.2),
     'L0_ffn_norm_weight': (1.0, 0.6),
     'L1_xattn_bq': (0.0, 0.1),
     'L1_xattn_bk': (0.0, 2.0),
     'L1_xattn_bv': (0.0, 0.1),
     'L1_xattn_bo': (0.0, 0.1),
     'L1_attn_norm1_w': (1.0, 0.6),
     'L1_attn_alpha_logit': (-2.1972246170043945, 0.6),
     'L1_attn_norm2_w': (1.0, 0.6),
     'L1_ffn_rb1': (0.0, 0.8),
     'L1_ffn_ln_g': (1.0, 0.6),
     'L1_ffn_ln_b': (0.0, 0.8),
     'L1_ffn_rb2': (0.0, 0.344),
     'L1_ffn_qb': (0.0, 0.8),
     'L1_ffn_kb': (0.0, 2.0),
     'L1_ffn_vb': (0.0, 0.8),
     'L1_ffn_ob': (0.0, 2.0)}
    factors = {'L0_attn_lambda_q1': 5.473,
     'L0_attn_lambda_k1': 8.0,
     'L0_attn_lambda_q2': 8.0,
     'L0_attn_lambda_k2': 8.0,
     'L0_ffn_router_weight': 8.0,
     'L0_ffn_gate_up_weight': 8.0,
     'L0_ffn_down_weight': 8.0,
     'L1_attn_Wq': 8.0,
     'L1_attn_Wk': 8.0,
     'L1_attn_Wv': 8.0,
     'L1_attn_beta_w': 8.0,
     'L1_attn_Wo': 8.0,
     'L1_attn_w_gate': 8.0,
     'L1_attn_w_up': 8.0,
     'L1_attn_w_down': 8.0,
     'L1_ffn_rW1': 3.682,
     'L1_ffn_rW2': 3.544,
     'L1_ffn_qW': 8.0,
     'L1_ffn_kW': 8.0,
     'L1_ffn_vW': 8.0,
     'L1_ffn_oW': 7.21}
    for name, (base, spread) in spreads.items():
        noise = np.random.default_rng([zlib.crc32(name.encode()), seed]).standard_normal(out[name].shape)
        drawn = base * np.exp(spread * noise) if base else spread * noise
        out[name] = jnp.asarray(drawn.astype(out[name].dtype))
    for name, factor in factors.items():
        out[name] = (out[name] * factor).astype(out[name].dtype)
    return out
```

```python
from contextlib import ExitStack

import numpy as np
import concourse.bass as bass
from concourse import mybir

F32 = mybir.dt.float32
U8, I32 = mybir.dt.uint8, mybir.dt.int32
ALU = mybir.AluOpType
ACT = mybir.ActivationFunctionType
AX = mybir.AxisListType

B, NQ, D = 32, 32, 128
SC, DC = 257, 96
MASK_WORDS = -(-SC // 4)
TOK = B * NQ
NT = TOK // 128
BT = 128 // NQ
HALF = 512
NH2 = TOK // HALF
KC = 86
NKC = 3
HC, DHC = 2, 64
HD, DHD = 8, 128
EXPERTS = 8
HID = 352
HCH = [128, 128, 96]
HS, DHS = 16, 8
LAMBDA_INIT = 0.8 - 0.6 * float(np.exp(-0.3))
LNS = 1.0e5
NEG = -1.0e30


def columns(parts):
    at, out = 0, {}
    for name, width in parts:
        out[name] = (at, width)
        at += width
    return out, at


CONST, N_CONST = columns([
    ("ident", 128), ("c128", 128), ("j128", 128), ("c96", 96), ("j96", 128), ("heads64", 128),
    ("c64", 64), ("j64", 64), ("ones", 128), ("before", 128), ("upto", 128),
    ("pair1", 128), ("pair2", 128), ("pair4", 128), ("pair8", 128), ("pair16", 128),
    ("rank", 64),
])
VEC, N_VEC = columns([(n, 1) for n in (
    "x_g", "x_b", "l_g", "l_b", "qn_g", "kn_g", "bo0", "ffn_w", "alpha", "bq3", "bo3",
    "norm1", "norm2", "decay", "beta_b", "rb1", "ln_g", "ln_b")]
    + [("rs", 2), ("rb2", 8)])
WTS, N_WTS = columns([
    ("wq0", 128), ("wk0", 128), ("wv0", 128), ("wlk0", 128), ("wlv0", 128), ("wo0", 128),
    ("lq1", 8), ("lk1", 8), ("lq2", 8), ("lk2", 8), ("router2", 8),
    ("wq3", 128), ("wk3", 97), ("wv3", 97), ("wo3", 128),
    ("wq4", 128), ("wk4", 128), ("wv4", 128), ("wo4", 128), ("wb4", 128),
    ("gate4", 256), ("up4", 256), ("down4", 256),
    ("rw1", 64), ("rw2", 8), ("ob", 128),
])


class Shared:
    pass


def block_of(stage, name):
    at, width = (CONST if name in CONST else VEC if name in VEC else WTS)[name]
    tile = stage.const if name in CONST else stage.vec if name in VEC else stage.wts
    return tile[:, at:at + width]


def load_stage(nc, S, dram):
    with nc.Block() as block:

        @block.sync
        def _(sp):
            sp.dma_start(S.xT[:, :], dram["x_t"]).then_inc(S.x_in, 16)
            sp.dma_start(S.const[:, :], dram["const"]).then_inc(S.const_in, 16)
            sp.dma_start(S.vec[:, :], dram["vec"]).then_inc(S.const_in, 16)
            sp.dma_start(S.wts[:, :], dram["wts"]).then_inc(S.wts_in, 16)
            sp.dma_start(S.yT[:, :], dram["y_t"]).then_inc(S.yt_in, 16)
            sp.dma_start(S.mask[:, :], dram["mask"]).then_inc(S.mask_in, 16)
            sp.dma_start(S.ytm[:, :], dram["y_tm"]).then_inc(S.ytm_in, 16)

        @block.gpsimd
        def _(pool):
            pool.wait_ge(S.x_in, 16)
            pool.wait_ge(S.const_in, 32)


def norm_stage(nc, S, name, src, dst, eps, feats=D, centre=None, mean=None, gain=None, shift=None,
               relu=False):
    with ExitStack() as ctx:
        sb = lambda n, s: ctx.enter_context(nc.sbuf_tensor(f"{name}_{n}", s, F32))
        sem = lambda n: S.sem(f"{name}_{n}")
        square = sb("square", [feats, TOK])
        inv = sb("inv", [feats, TOK])
        centred = ctx.enter_context(nc.psum_tensor(f"{name}_centred", [128, NH2, HALF], F32))
        var = ctx.enter_context(nc.psum_tensor(f"{name}_var", [128, NH2, HALF], F32))
        centred_ready, square_ready, var_ready = sem("centred"), sem("squared"), sem("varred")
        log_ready, inv_ready, scaled, done = sem("log"), sem("invd"), sem("scaled"), sem("done")
        relued = sem("relued") if relu else None

        def half(t, h):
            return t[0:feats, h * HALF:(h + 1) * HALF]

        def body(h):
            return half(src, h) if centre is None else centred[0:feats, h, :]

        block = ctx.enter_context(nc.Block())

        @block.tensor
        def _(pe):
            if centre is not None:
                for h in range(NH2):
                    nc.tensor.matmul(centred[0:feats, h, :], centre, half(src, h),
                                     start=True, stop=True).then_inc(centred_ready, 1)
            for h in range(NH2):
                pe.wait_ge(square_ready, h + 1)
                nc.tensor.matmul(var[0:feats, h, :], mean, half(square, h),
                                 start=True, stop=True).then_inc(var_ready, 1)

        @block.scalar
        def _(act):
            nc.scalar.preload_act_table_set("natural_log_exp_and_others")
            for h in range(NH2):
                if centre is not None:
                    act.wait_ge(centred_ready, h + 1)
                nc.scalar.activation(half(square, h), body(h), ACT.Square).then_inc(square_ready, 1)
            for h in range(NH2):
                act.wait_ge(var_ready, h + 1)
                nc.scalar.activation(half(inv, h), var[0:feats, h, :], ACT.Ln,
                                     bias=S.eps(eps)[0:feats, :]).then_inc(log_ready, 1)
                act.wait_ge(log_ready, h + 1)
                nc.scalar.activation(half(inv, h), half(inv, h), ACT.Exp,
                                     scale=-0.5).then_inc(inv_ready, 1)

        @block.vector
        def _(dve):
            for h in range(NH2):
                dve.wait_ge(inv_ready, h + 1)
                if gain is None:
                    nc.vector.tensor_tensor(half(dst, h), body(h), half(inv, h),
                                            ALU.mult).then_inc(done, 1)
                    continue
                nc.vector.tensor_tensor(half(dst, h), body(h), half(inv, h),
                                        ALU.mult).then_inc(scaled, 1)
                dve.wait_ge(scaled, h + 1)
                if relu:
                    nc.vector.tensor_scalar(half(square, h), half(dst, h), gain, shift,
                                            ALU.mult, ALU.add).then_inc(done, 1)
                    dve.wait_ge(done, h + 1)
                    nc.vector.tensor_scalar(half(dst, h), half(square, h), 0.0, None, ALU.max).then_inc(relued, 1)
                elif shift is None:
                    nc.vector.tensor_scalar(half(dst, h), half(dst, h), gain, None,
                                            ALU.mult).then_inc(done, 1)
                else:
                    nc.vector.tensor_scalar(half(dst, h), half(dst, h), gain, shift,
                                            ALU.mult, ALU.add).then_inc(done, 1)


def cross_stage(nc, S):
    with ExitStack() as ctx:
        sb = lambda n, s: ctx.enter_context(nc.sbuf_tensor("c0_" + n, s, F32))
        sem = lambda n: S.sem("c0_" + n)
        C = lambda n: block_of(S, n)
        qblk = sb("qblk", [128, B * HC * NQ])
        qview = qblk[:, :].rearrange("p (b h q) -> p b h q", b=B, h=HC)
        klat = sb("klat", [128, TOK])
        ltm = sb("ltm", [NQ, B * D])
        wkg, wvg, wvc = sb("wkg", [DC, 128]), sb("wvg", [DC, 128]), sb("wvc", [DC, 128])
        bk, gq = sb("bk", [128, 1]), sb("gq", [128, 1])
        bv = sb("bv", [33, 128])
        z = sb("z", [DC, HC, TOK])
        zl = sb("zl", [128, HC, TOK])
        srow = sb("srow", [33, HC, TOK])
        nmask = sb("nmask", [B, SC])

        with ExitStack() as inner:
            isb = lambda n, s: inner.enter_context(nc.sbuf_tensor("c0a_" + n, s, F32))
            ips = lambda n, s: inner.enter_context(nc.psum_tensor("c0a_" + n, s, F32))
            raw, square, inv = isb("raw", [128, 4, HALF]), isb("square", [128, 4, HALF]), isb("inv", [128, 4, HALF])
            raw_ps, ms_ps = ips("raw_ps", [128, 2, HALF]), ips("ms_ps", [128, 2, HALF])
            w_ps, t_ps = ips("w_ps", [128, 2, HALF]), ips("t_ps", [128, 2, HALF])
            wg_ready, bias_ready, wvc_ready, bias_saved = sem("wg"), sem("bias"), sem("wvc"), sem("bias_saved")
            raw_ready, raw_saved, sq_ready, ms_ready = sem("raw"), sem("raws"), sem("sq"), sem("ms")
            clipped, logged, inv_ready, zeroed, gq_ready, done = (
                sem("clip"), sem("log"), sem("inv"), sem("zeroed"), sem("gqr"), sem("done"))
            turned, turn_saved, scaled = sem("turned"), sem("turn_saved"), sem("scaled")
            block = inner.enter_context(nc.Block())

            def mean_square(pe, u):
                pe.wait_ge(sq_ready, u + 1)
                if u >= 2:
                    pe.wait_ge(clipped, u - 1)
                nc.tensor.matmul(ms_ps[:, u % 2, :], C("heads64"), square[:, u, :],
                                 start=True, stop=True).then_inc(ms_ready, 1)

            @block.tensor
            def _(pe):
                pe.wait_ge(S.wts_in, 16)
                nc.tensor.matmul(w_ps[:, 0, 0:1], C("wk0")[0:DC, :], C("x_b")[0:DC, :],
                                 start=True, stop=True)
                nc.tensor.matmul(w_ps[32:33, 1, 0:128], C("x_b")[0:DC, :], C("wv0")[0:DC, :],
                                 start=True, stop=True).then_inc(bias_ready, 1)
                for u in range(4):
                    if u >= 2:
                        pe.wait_ge(raw_saved, u - 1)
                    w = C("wq0") if u < 2 else C("wlk0")
                    nc.tensor.matmul(raw_ps[:, u % 2, :], w, S.xn[:, u % 2 * HALF:(u % 2 + 1) * HALF],
                                     start=True, stop=True).then_inc(raw_ready, 1)
                    if u >= 1:
                        mean_square(pe, u - 1)
                mean_square(pe, 3)
                pe.wait_ge(bias_saved, 2)
                pe.wait_ge(wg_ready, 2)
                nc.tensor.matmul(w_ps[0:DC, 0, 128:256], C("c96")[0:DC, :], wvg[:, :],
                                 start=True, stop=True).then_inc(wvc_ready, 1)
                for g in range(B // 4):
                    if g >= 2:
                        pe.wait_ge(turn_saved, g - 1)
                    for j in range(4):
                        b = 4 * g + j
                        mm = nc.tensor.transpose(t_ps[0:NQ, g % 2, j * 128:(j + 1) * 128],
                                                 S.xn[:, b * NQ:(b + 1) * NQ], C("ident"))
                    mm.then_inc(turned, 1)

            @block.scalar
            def _(act):
                for u in range(4):
                    act.wait_ge(raw_ready, u + 1)
                    nc.scalar.copy(raw[:, u, :], raw_ps[:, u % 2, :]).then_inc(raw_saved, 1)
                for u in range(4):
                    act.wait_ge(clipped, u + 1)
                    nc.scalar.activation(inv[:, u, :], inv[:, u, :], ACT.Ln).then_inc(logged, 1)
                    act.wait_ge(logged, u + 1)
                    nc.scalar.activation(inv[:, u, :], inv[:, u, :], ACT.Exp, scale=-0.5).then_inc(inv_ready, 1)
                for g in range(1, B // 4, 2):
                    act.wait_ge(turned, g + 1)
                    act.wait_ge(turn_saved, g)
                    nc.scalar.copy(ltm[:, g * HALF:(g + 1) * HALF], t_ps[0:NQ, g % 2, :]).then_inc(turn_saved, 1)

            @block.gpsimd
            def _(pool):
                nc.gpsimd.memset(qview[64:128, :, 0, :], 0.0).then_inc(zeroed, 1)
                pool.wait_ge(zeroed, 1)
                nc.gpsimd.memset(qview[0:64, :, 1, :], 0.0).then_inc(zeroed, 1)
                pool.wait_ge(zeroed, 2)
                for u in range(4):
                    pool.wait_ge(raw_saved, u + 1)
                    nc.gpsimd.tensor_tensor(square[:, u, :], raw[:, u, :], raw[:, u, :],
                                            ALU.mult).then_inc(sq_ready, 1)

            @block.vector
            def _(dve):
                dve.wait_ge(S.wts_in, 16)
                nc.vector.tensor_scalar(wkg[:, :], C("wk0")[0:DC, :], C("x_g")[0:DC, :], None,
                                        ALU.mult).then_inc(wg_ready, 1)
                nc.vector.tensor_scalar(wvg[:, :], C("wv0")[0:DC, :], C("x_g")[0:DC, :], None,
                                        ALU.mult).then_inc(wg_ready, 1)
                nc.vector.tensor_scalar(gq[:, :], C("qn_g"), C("kn_g"), DHC ** -0.5,
                                        ALU.mult, ALU.mult).then_inc(gq_ready, 1)
                dve.wait_ge(S.mask_in, 16)
                nc.vector.tensor_scalar(nmask[:, :], S.mask[:, :].bitcast(U8)[:, 0:SC], -1.0, -NEG,
                                        ALU.add, ALU.mult).then_inc(gq_ready, 1)
                dve.wait_ge(bias_ready, 1)
                nc.vector.tensor_copy(bk[:, :], w_ps[:, 0, 0:1]).then_inc(bias_saved, 1)
                nc.vector.tensor_copy(bv[32:33, :], w_ps[32:33, 1, 0:128]).then_inc(bias_saved, 1)
                for u in range(4):
                    dve.wait_ge(ms_ready, u + 1)
                    nc.vector.tensor_scalar(inv[:, u, :], ms_ps[:, u % 2, :], 1e-16, None,
                                            ALU.max).then_inc(clipped, 1)
                for u in range(4):
                    dve.wait_ge(inv_ready, u + 1)
                    h = slice(u % 2 * HALF, (u % 2 + 1) * HALF)
                    if u < 2:
                        dve.wait_ge(gq_ready, 1)
                        for k in range(HC):
                            p = slice(k * DHC, (k + 1) * DHC)
                            by_batch = lambda t: t[p, u, :].rearrange("p (b q) -> p b q", q=NQ)
                            nc.vector.scalar_tensor_tensor(
                                out=qview[p, u * B // 2:(u + 1) * B // 2, k, :], in0=by_batch(raw),
                                scalar=gq[p, :], in1=by_batch(inv),
                                op0=ALU.mult, op1=ALU.mult).then_inc(done, 1)
                    else:
                        nc.vector.tensor_tensor(klat[:, h], raw[:, u, :], inv[:, u, :],
                                                ALU.mult).then_inc(done, 1)
                dve.wait_ge(wvc_ready, 1)
                nc.vector.tensor_copy(wvc[:, :], w_ps[0:DC, 0, 128:256]).then_inc(done, 1)
                for g in range(0, B // 4, 2):
                    dve.wait_ge(turned, g + 1)
                    if g >= 1:
                        dve.wait_ge(turn_saved, g)
                    nc.vector.tensor_copy(ltm[:, g * HALF:(g + 1) * HALF],
                                          t_ps[0:NQ, g % 2, :]).then_inc(turn_saved, 1)

        PAIRS = B // 2
        KEYS = SC + NQ
        with ExitStack() as inner:
            isb = lambda n, s: inner.enter_context(nc.sbuf_tensor("c0b_" + n, s, F32))
            ips = lambda n: inner.enter_context(nc.psum_tensor("c0b_" + n, [128, HALF], F32))
            square, xhat = isb("square", [DC, 2, SC]), isb("xhat", [DC, 2, SC])
            inv = isb("inv", [128, 8, SC])
            kraw, ksq, kinv = isb("kraw", [128, 3, SC]), isb("ksq", [128, 2, SC]), isb("kinv", [128, 2, SC])
            khat = isb("khat", [128, 4, SC])
            p = isb("p", [128, 2, KEYS + 1])
            pt, ptl = isb("pt", [KC, 2, NKC * 128]), isb("ptl", [NQ, 2, 128])
            nmax, total, rtotal = isb("nmax", [128, 2]), isb("total", [128, 2, 3]), isb("rtotal", [128, 2])
            c_ps, v_ps, k_ps, m_ps, s_ps, t_ps, z_ps = (ips(n) for n in "cvkmstz")
            (c_ready, sq_ready, v_ready, log_ready, inv_ready, xhat_ready, k_ready, kraw_ready, ksq_ready,
             m_ready, clip_ready, klog_ready, kinv_ready, khat_ready) = (sem(n) for n in (
                 "c2", "sq2", "v2", "log2", "inv2", "xhat2", "k2", "kraw2", "ksq2", "m2", "clip2",
                 "klog2", "kinv2", "khat2"))
            (s_ready, max_ready, e_ready, sum_ready, rsum_ready, p_ready, t_ready, pt_ready, z_ready,
             z_saved) = (sem(n) for n in (
                 "s3", "max3", "e3", "sum3", "rsum3", "p3", "t3", "pt3", "z3", "zs3"))
            block = inner.enter_context(nc.Block())

            def steps():
                for n in range(B + 8):
                    pair = [(s, (n - lag) // 2) for s, lag in (("z", 7), ("turn", 6), ("score", 5))
                            if (n - lag) % 2 == 0 and 0 <= (n - lag) // 2 < PAIRS]
                    batch = [(s, n - lag) for s, lag in (("ms", 3), ("key", 2), ("var", 1), ("centre", 0))
                             if 0 <= n - lag < B]
                    yield pair + batch

            @block.tensor
            def _(pe):
                pe.wait_ge(S.yt_in, 16)
                pe.wait_ge(S.ytm_in, 16)
                for turn in steps():
                    for step, i in turn:
                        if step == "centre":
                            if i >= 1:
                                pe.wait_ge(xhat_ready, i)
                            nc.tensor.matmul(c_ps[0:DC, 0:SC], C("c96")[0:DC, :], S.yT[0:DC, i * SC:(i + 1) * SC],
                                             start=True, stop=True).then_inc(c_ready, 1)
                        elif step == "var":
                            pe.wait_ge(sq_ready, i + 1)
                            if i >= 1:
                                pe.wait_ge(log_ready, i)
                            nc.tensor.matmul(v_ps[:, 0:SC], C("j96")[0:DC, :], square[:, i % 2, :],
                                             start=True, stop=True).then_inc(v_ready, 1)
                        elif step == "key":
                            pe.wait_ge(xhat_ready, i + 1)
                            if i >= 1:
                                pe.wait_ge(kraw_ready, i)
                            nc.tensor.matmul(k_ps[:, 0:SC], wkg[:, :], xhat[:, i % 2, :],
                                             start=True, stop=True).then_inc(k_ready, 1)
                        elif step == "ms":
                            pe.wait_ge(ksq_ready, i + 1)
                            if i >= 1:
                                pe.wait_ge(clip_ready, i)
                            nc.tensor.matmul(m_ps[:, 0:SC], C("heads64"), ksq[:, i % 2, :],
                                             start=True, stop=True).then_inc(m_ready, 1)
                        elif step == "score":
                            pe.wait_ge(khat_ready, 2 * i + 2)
                            if i >= 1:
                                pe.wait_ge(e_ready, 2 * i)
                            for j in range(2):
                                b = 2 * i + j
                                q = qblk[:, b * 64:b * 64 + 64]
                                o = s_ps[64 * j:64 * j + 64, :]
                                nc.tensor.matmul(o[:, 0:SC], q, khat[:, b % 4, :], start=True, stop=False)
                                nc.tensor.matmul(o[:, 0:SC], C("ident")[0:B, b:b + 1].to_broadcast([B, 64]),
                                                 nmask[:, :], start=False, stop=True)
                                mm = nc.tensor.matmul(o[:, SC:KEYS], q, klat[:, b * NQ:(b + 1) * NQ],
                                                      start=True, stop=True)
                            mm.then_inc(s_ready, 1)
                        elif step == "turn":
                            pe.wait_ge(p_ready, 3 * i + 3)
                            if i >= 1:
                                pe.wait_ge(pt_ready, 3 * i)
                            for c in range(NKC):
                                nc.tensor.transpose(t_ps[0:KC, c * 128:(c + 1) * 128],
                                                    p[:, i % 2, c * KC:(c + 1) * KC], C("ident"))
                            nc.tensor.transpose(t_ps[0:NQ + 1, 384:512], p[:, i % 2, SC:KEYS + 1],
                                                C("ident")).then_inc(t_ready, 1)
                        else:
                            pe.wait_ge(pt_ready, 3 * i + 3)
                            if i >= 1:
                                pe.wait_ge(z_saved, 2 * i)
                            for j in range(2):
                                b = 2 * i + j
                                for c in range(NKC):
                                    at = (b * NKC + c) * (DC + 1)
                                    nc.tensor.matmul(z_ps[0:DC, 64 * j:64 * j + 64], S.ytm[:, at:at + DC],
                                                     pt[:, i % 2, c * 128 + 64 * j:c * 128 + 64 * j + 64],
                                                     start=(c == 0), stop=(c == NKC - 1))
                                mm = nc.tensor.matmul(z_ps[:, 128 + 64 * j:192 + 64 * j],
                                                      ltm[:, b * D:(b + 1) * D],
                                                      ptl[:, i % 2, 64 * j:64 * j + 64], start=True, stop=True)
                            mm.then_inc(z_ready, 1)

            @block.scalar
            def _(act):
                for turn in steps():
                    for step, i in turn:
                        if step == "centre":
                            act.wait_ge(c_ready, i + 1)
                            if i >= 2:
                                act.wait_ge(v_ready, i - 1)
                            nc.scalar.activation(square[:, i % 2, :], c_ps[0:DC, 0:SC],
                                                 ACT.Square).then_inc(sq_ready, 1)
                        elif step == "var":
                            act.wait_ge(v_ready, i + 1)
                            if i >= 8:
                                act.wait_ge(p_ready, 3 * ((i - 8) // 2) + 3)
                            r = inv[:, i % 8, :]
                            nc.scalar.activation(r, v_ps[:, 0:SC], ACT.Ln, bias=S.eps(1e-5)).then_inc(log_ready, 1)
                            act.wait_ge(log_ready, i + 1)
                            nc.scalar.activation(r, r, ACT.Exp, scale=-0.5).then_inc(inv_ready, 1)
                        elif step == "ms":
                            act.wait_ge(clip_ready, i + 1)
                            r = kinv[:, i % 2, :]
                            nc.scalar.activation(r, r, ACT.Ln).then_inc(klog_ready, 1)
                            act.wait_ge(klog_ready, i + 1)
                            nc.scalar.activation(r, r, ACT.Exp, scale=-0.5).then_inc(kinv_ready, 1)
                        elif step == "score":
                            act.wait_ge(max_ready, i + 1)
                            if i >= 2:
                                act.wait_ge(t_ready, i - 1)
                            nc.scalar.activation(p[:, i % 2, 0:SC], s_ps[:, 0:SC], ACT.Exp,
                                                 bias=nmax[:, i % 2:i % 2 + 1],
                                                 accum_out=total[:, i % 2, 0:1]).then_inc(e_ready, 1)
                            nc.scalar.activation(p[:, i % 2, SC:KEYS], s_ps[:, SC:KEYS], ACT.Exp,
                                                 bias=nmax[:, i % 2:i % 2 + 1],
                                                 accum_out=total[:, i % 2, 1:2]).then_inc(e_ready, 1)
                        elif step == "z":
                            act.wait_ge(z_ready, i + 1)
                            t = slice(2 * i * NQ, (2 * i + 2) * NQ)
                            for out, rows, at in ((z, DC, 0), (zl, 128, 128)):
                                nc.scalar.copy(
                                    out[:, :, t].rearrange("c h (b q) -> c b h q", b=2),
                                    z_ps[0:rows, at:at + 128].rearrange("c (b h q) -> c b h q", b=2, h=HC),
                                ).then_inc(z_saved, 1)

            @block.gpsimd
            def _(pool):
                for turn in steps():
                    for step, i in turn:
                        if step == "key":
                            pool.wait_ge(kraw_ready, i + 1)
                            if i >= 2:
                                pool.wait_ge(m_ready, i - 1)
                            nc.gpsimd.tensor_tensor(ksq[:, i % 2, :], kraw[:, i % 3, :], kraw[:, i % 3, :],
                                                    ALU.mult).then_inc(ksq_ready, 1)
                        elif step == "ms":
                            pool.wait_ge(kinv_ready, i + 1)
                            if i >= 4:
                                pool.wait_ge(s_ready, (i - 4) // 2 + 1)
                            nc.gpsimd.tensor_tensor(khat[:, i % 4, :], kraw[:, i % 3, :], kinv[:, i % 2, :],
                                                    ALU.mult).then_inc(khat_ready, 1)

            @block.vector
            def _(dve):
                for turn in steps():
                    for step, i in turn:
                        if step == "var":
                            dve.wait_ge(inv_ready, i + 1)
                            if i >= 2:
                                dve.wait_ge(k_ready, i - 1)
                            nc.vector.tensor_tensor(xhat[:, i % 2, :], c_ps[0:DC, 0:SC], inv[0:DC, i % 8, :],
                                                    ALU.mult).then_inc(xhat_ready, 1)
                        elif step == "key":
                            dve.wait_ge(k_ready, i + 1)
                            if i >= 3:
                                dve.wait_ge(khat_ready, i - 2)
                            nc.vector.tensor_scalar(kraw[:, i % 3, :], k_ps[:, 0:SC], bk[:, 0:1], None,
                                                    ALU.add).then_inc(kraw_ready, 1)
                        elif step == "ms":
                            dve.wait_ge(m_ready, i + 1)
                            if i >= 2:
                                dve.wait_ge(khat_ready, i - 1)
                            nc.vector.tensor_scalar(kinv[:, i % 2, :], m_ps[:, 0:SC], 1e-16, None,
                                                    ALU.max).then_inc(clip_ready, 1)
                        elif step == "score":
                            dve.wait_ge(s_ready, i + 1)
                            if i >= 2:
                                dve.wait_ge(e_ready, 2 * i - 2)
                            nc.vector.tensor_reduce(nmax[:, i % 2:i % 2 + 1], s_ps[:, 0:KEYS], AX.X, ALU.max,
                                                    negate=True).then_inc(max_ready, 1)
                            dve.wait_ge(e_ready, 2 * i + 2)
                            t = total[:, i % 2, :]
                            nc.vector.tensor_tensor(t[:, 2:3], t[:, 0:1], t[:, 1:2], ALU.add).then_inc(sum_ready, 1)
                            dve.wait_ge(sum_ready, i + 1)
                            r = rtotal[:, i % 2:i % 2 + 1]
                            nc.vector.reciprocal(r, t[:, 2:3]).then_inc(rsum_ready, 1)
                            dve.wait_ge(rsum_ready, i + 1)
                            for j in range(2):
                                h = slice(64 * j, 64 * j + 64)
                                nc.vector.scalar_tensor_tensor(
                                    out=p[h, i % 2, 0:SC], in0=p[h, i % 2, 0:SC], scalar=rtotal[h, i % 2:i % 2 + 1],
                                    in1=inv[h, (2 * i + j) % 8, :], op0=ALU.mult, op1=ALU.mult).then_inc(p_ready, 1)
                            nc.vector.tensor_scalar(p[:, i % 2, SC:KEYS], p[:, i % 2, SC:KEYS], r, None, ALU.mult)
                            nc.vector.tensor_tensor(p[:, i % 2, KEYS:KEYS + 1], t[:, 0:1], r,
                                                    ALU.mult).then_inc(p_ready, 1)
                        elif step == "turn":
                            dve.wait_ge(t_ready, i + 1)
                            if i >= 2:
                                dve.wait_ge(z_ready, i - 1)
                            nc.vector.tensor_copy(pt[:, i % 2, :], t_ps[0:KC, 0:384]).then_inc(pt_ready, 1)
                            nc.vector.tensor_copy(ptl[:, i % 2, :], t_ps[0:NQ, 384:512]).then_inc(pt_ready, 1)
                            t = slice(2 * i * NQ, (2 * i + 2) * NQ)
                            nc.vector.tensor_copy(
                                srow[32:33, :, t].rearrange("c h (b q) -> c b h q", b=2),
                                t_ps[32:33, 384:512].rearrange("c (b h q) -> c b h q", b=2, h=HC),
                            ).then_inc(pt_ready, 1)

        with ExitStack() as inner:
            o_sb = inner.enter_context(nc.sbuf_tensor("c0c_o", [128, TOK], F32))
            o_ps = inner.enter_context(nc.psum_tensor("c0c_o_ps", [128, NH2, HALF], F32))
            y_ps = inner.enter_context(nc.psum_tensor("c0c_y_ps", [128, NH2, HALF], F32))
            o_ready, o_saved, y_ready, added = sem("o4"), sem("os4"), sem("y4"), sem("add4")
            block = inner.enter_context(nc.Block())

            @block.tensor
            def _(pe):
                for h in range(NH2):
                    t = slice(h * HALF, (h + 1) * HALF)
                    for k in range(HC):
                        w = slice(k * DHC, (k + 1) * DHC)
                        o = o_ps[w, h, :]
                        nc.tensor.matmul(o, wvc[:, w], z[:, k, t], start=True, stop=False)
                        nc.tensor.matmul(o, C("wlv0")[:, w], zl[:, k, t], start=False, stop=False)
                        mm = nc.tensor.matmul(o, bv[32:33, w], srow[32:33, k, t], start=False, stop=True)
                    mm.then_inc(o_ready, 1)
                for h in range(NH2):
                    pe.wait_ge(o_saved, h + 1)
                    nc.tensor.matmul(y_ps[:, h, :], C("wo0"), o_sb[:, h * HALF:(h + 1) * HALF],
                                     start=True, stop=True).then_inc(y_ready, 1)

            @block.scalar
            def _(act):
                for h in range(NH2):
                    act.wait_ge(o_ready, h + 1)
                    nc.scalar.copy(o_sb[:, h * HALF:(h + 1) * HALF], o_ps[:, h, :]).then_inc(o_saved, 1)

            @block.vector
            def _(dve):
                for h in range(NH2):
                    dve.wait_ge(y_ready, h + 1)
                    x = S.xT[:, h * HALF:(h + 1) * HALF]
                    nc.vector.scalar_tensor_tensor(out=x, in0=y_ps[:, h, :], scalar=C("bo0"), in1=x,
                                                   op0=ALU.add, op1=ALU.add).then_inc(added, 1)


def diff_stage(nc, S, dram):
    HH = 2 * HD
    with ExitStack() as ctx:
        sb = lambda n, s: ctx.enter_context(nc.sbuf_tensor("d1_" + n, s, F32))
        sem = lambda n: S.sem("d1_" + n)
        C = lambda n: block_of(S, n)
        wd = sb("wd", [128, 5 * 2048])
        wq, wk, wvt, wv, wo = (wd[:, n * 2048:(n + 1) * 2048] for n in range(5))
        wkq = sb("wkq", [128, HH, 128])
        wvo = sb("wvo", [128, HD, 128])
        xtm = sb("xtm", [128, NT, 128])
        prod, nlam = sb("prod", [128, 2, HD]), sb("nlam", [128, HD])
        at = sb("at", [128, 2, HD * 128])

        with ExitStack() as inner:
            w_ps = [inner.enter_context(nc.psum_tensor(f"d1a_w{n}", [128, 4, 128], F32)) for n in range(8)]
            elam = inner.enter_context(nc.sbuf_tensor("d1a_elam", [128, 2, HD], F32))
            kq_ready, kq_saved, vo_ready, t_ready, all_saved = (
                sem("kq"), sem("kqs"), sem("vo"), sem("t"), sem("alls"))
            prod_ready, lam_ready, elam_ready, scaled, lam_done, zeroed = (
                sem("prod"), sem("lam"), sem("elam"), sem("scaled"), sem("lamd"), sem("zero"))
            block = inner.enter_context(nc.Block())

            @block.sync
            def _(sp):
                sp.dma_start(wd[:, :], dram["wd"]).then_inc(S.wd_in, 16)

            @block.tensor
            def _(pe):
                for g in range(2):
                    for j in range(4):
                        t = 4 * g + j
                        mm = nc.tensor.transpose(w_ps[6 + g][:, j, :], S.xn[:, t * 128:(t + 1) * 128], C("ident"))
                    mm.then_inc(t_ready, 1)
                pe.wait_ge(S.wd_in, 16)
                for g in range(4):
                    for j in range(4):
                        e = slice((4 * g + j) * 128, (4 * g + j + 1) * 128)
                        mm = nc.tensor.matmul(w_ps[g][:, j, :], wk[:, e], wq[:, e], start=True, stop=True)
                    mm.then_inc(kq_ready, 1)
                pe.wait_ge(scaled, 2)
                for g in range(2):
                    for j in range(4):
                        for c in range(2):
                            k = 2 * (4 * g + j) + c
                            e = slice(k * 128, (k + 1) * 128)
                            mm = nc.tensor.matmul(w_ps[4 + g][:, j, :], wv[:, e], wo[:, e],
                                                  start=(c == 0), stop=(c == 1))
                    mm.then_inc(vo_ready, 1)
                pe.wait_ge(t_ready, 2)
                pe.wait_ge(all_saved, 1)
                pe.wait_ge(prod_ready, 2)
                nc.tensor.matmul(w_ps[6][:, 0, 0:2 * HD], C("ones"), prod[:, :, :], start=True, stop=True).then_inc(lam_ready, 1)

            @block.scalar
            def _(act):
                for g in range(4):
                    act.wait_ge(kq_ready, g + 1)
                    nc.scalar.copy(wkq[:, 4 * g:4 * g + 4, :], w_ps[g][:, :, :]).then_inc(kq_saved, 1)
                act.wait_ge(lam_ready, 1)
                nc.scalar.activation(elam[:, :, :], w_ps[6][:, 0, 0:2 * HD].rearrange("p (a h) -> p a h", a=2),
                                     ACT.Exp).then_inc(elam_ready, 1)

            @block.gpsimd
            def _(pool):
                nc.gpsimd.memset(at[:, :, :], 0.0).then_inc(zeroed, 1)

            @block.vector
            def _(dve):
                nc.vector.tensor_tensor(prod[:, 0, :], C("lq1"), C("lk1"), ALU.mult).then_inc(prod_ready, 1)
                nc.vector.tensor_tensor(prod[:, 1, :], C("lq2"), C("lk2"), ALU.mult).then_inc(prod_ready, 1)
                for g in range(2):
                    dve.wait_ge(t_ready, g + 1)
                    nc.vector.tensor_copy(xtm[:, 4 * g:4 * g + 4, :], w_ps[6 + g][:, :, :]).then_inc(all_saved, 1)
                dve.wait_ge(S.wd_in, 16)
                by_half = wo.rearrange("p (h c n) -> p h c n", h=HD, c=2)
                for c in range(2):
                    nc.vector.tensor_scalar(by_half[:, :, c, :], by_half[:, :, c, :], C("rs")[:, c:c + 1],
                                            1.0 - LAMBDA_INIT, ALU.mult, ALU.mult).then_inc(scaled, 1)
                for g in range(2):
                    dve.wait_ge(vo_ready, g + 1)
                    nc.vector.tensor_copy(wvo[:, 4 * g:4 * g + 4, :], w_ps[4 + g][:, :, :]).then_inc(all_saved, 1)
                dve.wait_ge(elam_ready, 1)
                nc.vector.scalar_tensor_tensor(out=nlam[:, :], in0=elam[:, 1, :], scalar=LAMBDA_INIT, in1=elam[:, 0, :],
                                               op0=ALU.subtract, op1=ALU.subtract).then_inc(lam_done, 1)

        with ExitStack() as inner:
            isb = lambda n, s: inner.enter_context(nc.sbuf_tensor("d1b_" + n, s, F32))
            ips = lambda n: inner.enter_context(nc.psum_tensor(f"d1b_{n}_ps", [128, HALF], F32))
            r_sb = isb("r", [128, 2, HH * 128])
            e_sb, nmax, sums, rsum = isb("e", [128, HH, NQ]), isb("nmax", [128, HH]), isb("sums", [128, HH]), isb("rsum", [128, HH])
            attn = isb("attn", [128, HD, NQ])
            z_sb = isb("z", [128, 2, HD * 128])
            junk, ssq, rms = isb("junk", [128, HD, 2 * DHD]), isb("ssq", [128, 2, HD]), isb("rms", [128, 2, HD])
            acc = isb("acc", [128, 2, 128])
            r_ps, o_ps = [ips("r0"), ips("r1")], [ips("o0"), ips("o1")]
            s_ps, z_ps, y_ps, x_ps = ips("s"), ips("z"), ips("y"), ips("x")
            (r_ready, r_act, r_dve, s_ready, max_ready, sub_ready, e_ready, sum_ready, rsum_ready, nl_ready,
             p_ready, a_ready, at_ready, z_ready, z_act, z_dve, o_ready, ssq_ready, rlog, rms_ready, y_ready,
             acc_ready, x_ready, added) = (sem(n) for n in (
                 "r", "ra", "rd", "s", "max", "sub", "e", "sum", "rsum", "nl", "p", "a", "at", "z", "za",
                 "zd", "o", "ssq", "rlog", "rms", "y", "acc", "x", "added"))
            block = inner.enter_context(nc.Block())
            by_half = lambda t: t[:, :].rearrange("p (h s) -> p h s", s=2)

            def steps():
                for n in range(NT + 5):
                    yield [(s, n - lag) for s, lag in (("out", 5), ("y", 4), ("o", 3), ("z", 2), ("score", 1), ("r", 0))
                           if 0 <= n - lag < NT]

            @block.tensor
            def _(pe):
                for turn in steps():
                    for step, t in turn:
                        if step == "r":
                            for g in range(4):
                                if t or g >= 2:
                                    pe.wait_ge((r_act, r_dve)[g % 2], 2 * t + g // 2)
                                for j in range(4):
                                    mm = nc.tensor.matmul(r_ps[g % 2][:, j * 128:(j + 1) * 128], wkq[:, 4 * g + j, :],
                                                          S.xn[:, t * 128:(t + 1) * 128], start=True, stop=True)
                                mm.then_inc(r_ready, 1)
                        elif step == "score":
                            pe.wait_ge(r_act, 2 * t + 2)
                            pe.wait_ge(r_dve, 2 * t + 2)
                            if t:
                                pe.wait_ge(sub_ready, t)
                            keys = r_sb[:, t % 2, :].rearrange("p (h b k) -> p h b k", h=HH, b=BT)
                            for b in range(BT):
                                at_b = t * 128 + b * NQ
                                mm = nc.tensor.matmul(s_ps[b * NQ:(b + 1) * NQ, :], S.xn[:, at_b:at_b + NQ],
                                                      keys[:, :, b, :], start=True, stop=True)
                            mm.then_inc(s_ready, 1)
                        elif step == "z":
                            pe.wait_ge(at_ready, BT * (t + 1))
                            for g in range(2):
                                if t or g:
                                    pe.wait_ge(z_act, t + g)
                                if t:
                                    pe.wait_ge(z_dve, t)
                                nc.tensor.matmul(z_ps[:, :], xtm[:, t, :], at[:, t % 2, g * HALF:(g + 1) * HALF],
                                                 start=True, stop=True).then_inc(z_ready, 1)
                        elif step == "o":
                            pe.wait_ge(z_act, t + 1)
                            pe.wait_ge(z_dve, t + 1)
                            for h in range(HD):
                                if t or h >= 4:
                                    pe.wait_ge(ssq_ready, HD * t + h // 2 * 2 - 2)
                                mm = nc.tensor.matmul(o_ps[h // 2 % 2][:, h % 2 * 256:h % 2 * 256 + 256],
                                                      z_sb[:, t % 2, h * 128:(h + 1) * 128], wvt[:, h * 256:(h + 1) * 256],
                                                      start=True, stop=True)
                                if h % 2:
                                    mm.then_inc(o_ready, 1)
                        elif step == "y":
                            for g in range(2):
                                if t or g:
                                    pe.wait_ge(acc_ready, HD * t + 4 * g)
                                for j in range(4):
                                    h = 4 * g + j
                                    mm = nc.tensor.matmul(y_ps[:, j * 128:(j + 1) * 128],
                                                          z_sb[:, t % 2, h * 128:(h + 1) * 128], wvo[:, h, :],
                                                          start=True, stop=True)
                                mm.then_inc(y_ready, 1)
                        else:
                            pe.wait_ge(acc_ready, HD * (t + 1))
                            if t:
                                pe.wait_ge(added, t)
                            nc.tensor.transpose(x_ps[:, 0:128], acc[:, t % 2, :], C("ident")).then_inc(x_ready, 1)

            @block.scalar
            def _(act):
                for turn in steps():
                    for step, t in turn:
                        if step == "r":
                            for g in (0, 2):
                                act.wait_ge(r_ready, 4 * t + g + 1)
                                if t >= 2:
                                    act.wait_ge(s_ready, t - 1)
                                nc.scalar.copy(r_sb[:, t % 2, g * HALF:(g + 1) * HALF], r_ps[0][:, :]).then_inc(r_act, 1)
                        elif step == "score":
                            act.wait_ge(sub_ready, t + 1)
                            nc.scalar.activation(e_sb[:, :, :], e_sb[:, :, :], ACT.Exp, scale=DHD ** -0.5).then_inc(e_ready, 1)
                        elif step == "z":
                            act.wait_ge(z_ready, 2 * t + 1)
                            if t >= 2:
                                act.wait_ge(y_ready, 2 * t - 2)
                            nc.scalar.copy(z_sb[:, t % 2, 0:HALF], z_ps[:, :]).then_inc(z_act, 1)
                        elif step == "o":
                            if t >= 2:
                                act.wait_ge(rms_ready, t - 1)
                            for h in range(HD):
                                if h % 2 == 0:
                                    act.wait_ge(o_ready, 4 * t + h // 2 + 1)
                                nc.scalar.activation(junk[:, h, :], o_ps[h // 2 % 2][:, h % 2 * 256:h % 2 * 256 + 256], ACT.Square,
                                                     accum_out=ssq[:, t % 2, h:h + 1]).then_inc(ssq_ready, 1)
                            act.wait_ge(ssq_ready, HD * (t + 1))
                            if t >= 2:
                                act.wait_ge(acc_ready, HD * (t - 1))
                            nc.scalar.activation(rms[:, t % 2, :], ssq[:, t % 2, :], ACT.Ln, scale=1.0 / (2 * DHD),
                                                 bias=S.eps(1e-5)).then_inc(rlog, 1)
                            act.wait_ge(rlog, t + 1)
                            nc.scalar.activation(rms[:, t % 2, :], rms[:, t % 2, :], ACT.Exp, scale=-0.5).then_inc(rms_ready, 1)

            @block.vector
            def _(dve):
                for turn in steps():
                    for step, t in turn:
                        if step == "r":
                            for g in (1, 3):
                                dve.wait_ge(r_ready, 4 * t + g + 1)
                                if t >= 2:
                                    dve.wait_ge(s_ready, t - 1)
                                nc.vector.tensor_copy(r_sb[:, t % 2, g * HALF:(g + 1) * HALF], r_ps[1][:, :]).then_inc(r_dve, 1)
                        elif step == "score":
                            dve.wait_ge(s_ready, t + 1)
                            s = s_ps[:, :].rearrange("p (h k) -> p h k", k=NQ)
                            nc.vector.tensor_reduce(nmax[:, :], s, AX.X, ALU.max).then_inc(max_ready, 1)
                            dve.wait_ge(max_ready, t + 1)
                            nc.vector.tensor_tensor(e_sb[:, :, :], s, nmax[:, :].unsqueeze(2).to_broadcast([128, HH, NQ]),
                                                    ALU.subtract).then_inc(sub_ready, 1)
                            dve.wait_ge(e_ready, t + 1)
                            nc.vector.tensor_reduce(sums[:, :], e_sb[:, :, :], AX.X, ALU.add).then_inc(sum_ready, 1)
                            dve.wait_ge(sum_ready, t + 1)
                            nc.vector.reciprocal(rsum[:, :], sums[:, :]).then_inc(rsum_ready, 1)
                            dve.wait_ge(rsum_ready, t + 1)
                            nc.vector.tensor_tensor(by_half(rsum)[:, :, 1], by_half(rsum)[:, :, 1], nlam[:, :],
                                                    ALU.mult).then_inc(nl_ready, 1)
                            dve.wait_ge(nl_ready, t + 1)
                            nc.vector.tensor_tensor(e_sb[:, :, :], e_sb[:, :, :],
                                                    rsum[:, :].unsqueeze(2).to_broadcast([128, HH, NQ]),
                                                    ALU.mult).then_inc(p_ready, 1)
                            dve.wait_ge(p_ready, t + 1)
                            both = e_sb[:, :, :].rearrange("p (h s) k -> p h s k", s=2)
                            nc.vector.tensor_tensor(attn[:, :, :], both[:, :, 0, :], both[:, :, 1, :], ALU.add).then_inc(a_ready, 1)
                            dve.wait_ge(a_ready, t + 1)
                            if t >= 2:
                                dve.wait_ge(z_ready, 2 * t - 2)
                            for b in range(BT):
                                p = slice(b * NQ, (b + 1) * NQ)
                                nc.vector.transpose(
                                    at[p, t % 2, :].rearrange("p (h q) -> p h q", h=HD)[:, :, b * NQ:(b + 1) * NQ],
                                    attn[p, :, :]).then_inc(at_ready, 1)
                        elif step == "z":
                            dve.wait_ge(z_ready, 2 * t + 2)
                            if t >= 2:
                                dve.wait_ge(y_ready, 2 * t - 2)
                            nc.vector.tensor_copy(z_sb[:, t % 2, HALF:2 * HALF], z_ps[:, :]).then_inc(z_dve, 1)
                        elif step == "y":
                            dve.wait_ge(rms_ready, t + 1)
                            if t >= 2:
                                dve.wait_ge(x_ready, t - 1)
                            for h in range(HD):
                                if h % 4 == 0:
                                    dve.wait_ge(y_ready, 2 * t + h // 4 + 1)
                                y = y_ps[:, h % 4 * 128:h % 4 * 128 + 128]
                                r = rms[:, t % 2, h:h + 1]
                                if h == 0:
                                    nc.vector.tensor_scalar(acc[:, t % 2, :], y, r, None, ALU.mult).then_inc(acc_ready, 1)
                                else:
                                    dve.wait_ge(acc_ready, HD * t + h)
                                    nc.vector.scalar_tensor_tensor(out=acc[:, t % 2, :], in0=y, scalar=r, in1=acc[:, t % 2, :],
                                                                   op0=ALU.mult, op1=ALU.add).then_inc(acc_ready, 1)
                        elif step == "out":
                            dve.wait_ge(x_ready, t + 1)
                            x = S.xT[:, t * 128:(t + 1) * 128]
                            nc.vector.tensor_tensor(x, x_ps[:, 0:128], x, ALU.add).then_inc(added, 1)


class Chain:

    def __init__(self, engine, semaphore):
        self.engine, self.semaphore, self.count = engine, semaphore, 0

    def __call__(self, instruction):
        self.count += 1
        instruction.then_inc(self.semaphore, 1)
        self.engine.wait_ge(self.semaphore, self.count)


def top_two(nc, S, name, logits, gates, sb, block, logits_ready, bias=None):
    sem = lambda n: S.sem(f"{name}_{n}")
    shape = [128, NT, EXPERTS]
    p, key, first, second, rest = (sb(n, shape) for n in ("p", "key", "first", "second", "rest"))
    top, row = sb("top", [128, NT]), sb("row", [128, NT])
    chain_sem, shifted, exp_ready = sem("chain"), sem("shifted"), sem("exp")
    wide = lambda t: t[:, :].unsqueeze(2).to_broadcast(shape)
    rank = block_of(S, "rank").rearrange("p (t e) -> p t e", e=EXPERTS)

    @block.scalar
    def _(act):
        act.wait_ge(shifted, 1)
        nc.scalar.activation(p[:, :, :], p[:, :, :], ACT.Exp).then_inc(exp_ready, 1)

    @block.vector
    def _(dve):
        step = Chain(dve, chain_sem)
        tt = lambda *a: step(nc.vector.tensor_tensor(*a))
        dve.wait_ge(logits_ready, 1)
        source = logits
        if bias is not None:
            tt(key[:, :, :], logits, bias, ALU.add)
            source = key[:, :, :]
        step(nc.vector.tensor_reduce(top[:, :], source, AX.X, ALU.max))
        nc.vector.tensor_tensor(p[:, :, :], source, wide(top), ALU.subtract).then_inc(shifted, 1)
        dve.wait_ge(exp_ready, 1)
        step(nc.vector.tensor_reduce(row[:, :], p[:, :, :], AX.X, ALU.add))
        step(nc.vector.reciprocal(row[:, :], row[:, :]))
        tt(p[:, :, :], p[:, :, :], wide(row), ALU.mult)

        def select(out, src):
            step(nc.vector.tensor_reduce(top[:, :], src[:, :, :], AX.X, ALU.max))
            tt(key[:, :, :], src[:, :, :], wide(top), ALU.is_ge)
            tt(key[:, :, :], key[:, :, :], rank, ALU.mult)
            step(nc.vector.tensor_reduce(top[:, :], key[:, :, :], AX.X, ALU.max))
            tt(out[:, :, :], key[:, :, :], wide(top), ALU.is_equal)

        select(first, p)
        step(nc.vector.scalar_tensor_tensor(out=rest[:, :, :], in0=first[:, :, :], scalar=-2.0, in1=p[:, :, :],
                                            op0=ALU.mult, op1=ALU.add))
        select(second, rest)
        tt(first[:, :, :], first[:, :, :], second[:, :, :], ALU.add)
        tt(p[:, :, :], p[:, :, :], first[:, :, :], ALU.mult)
        step(nc.vector.tensor_reduce(row[:, :], p[:, :, :], AX.X, ALU.add))
        step(nc.vector.reciprocal(row[:, :], row[:, :]))
        tt(gates[:, :, :], p[:, :, :], wide(row), ALU.mult)


def ffn_stage(nc, S, dram):
    with ExitStack() as ctx:
        sb = lambda n, s: ctx.enter_context(nc.sbuf_tensor("f2_" + n, s, F32))
        sem = lambda n: S.sem("f2_" + n)
        C = lambda n: block_of(S, n)
        xr = sb("xr", [128, TOK])
        gates = sb("gates", [128, NT, EXPERTS])
        acc = sb("acc", [128, NT, 128])
        norm_stage(nc, S, "f2n", S.xn, xr, 1e-6, mean=C("j128"), gain=C("ffn_w"))

        with ExitStack() as inner:
            isb = lambda n, s: inner.enter_context(nc.sbuf_tensor("f2a_" + n, s, F32))
            l_ps = inner.enter_context(nc.psum_tensor("f2a_l", [128, NT, EXPERTS], F32))
            l_ready = sem("l")
            block = inner.enter_context(nc.Block())

            @block.tensor
            def _(pe):
                for t in range(NT):
                    mm = nc.tensor.matmul(l_ps[:, t, :], xr[:, t * 128:(t + 1) * 128], C("router2"), start=True, stop=True)
                mm.then_inc(l_ready, 1)

            top_two(nc, S, "f2t", l_ps[:, :, :], gates, isb, block, l_ready)

        with ExitStack() as inner:
            isb = lambda n, s: inner.enter_context(nc.sbuf_tensor("f2b_" + n, s, F32))
            ips = lambda n: inner.enter_context(nc.psum_tensor(f"f2b_{n}_ps", [128, HALF], F32))
            gu_w, down_w = isb("gu_w", [128, 2, 2 * HID]), isb("down_w", [128, 2, 3 * 128])
            sil, hid = isb("sil", [128, 2, HALF]), isb("hid", [128, NH2, 3, HALF])
            g_ps, u_ps, d_ps = [ips("g0"), ips("g1")], [ips("u0"), ips("u1")], [ips("d0"), ips("d1")]
            w_in = [sem("w_in0"), sem("w_in1")]
            gu_ready, sil_ready, hid_ready, d_ready, acc_ready = (sem(n) for n in ("gu", "sil", "hid", "d", "acc"))
            block = inner.enter_context(nc.Block())
            UNITS = 3 * NH2
            FREE = 2

            @block.sync
            def _(sp):
                def load(e, k):
                    sp.dma_start(gu_w[:, k, :], dram["gate_up"][e, :, :]).then_inc(w_in[k], 16)
                    sp.dma_start(down_w[:, k, :], dram["down"][e, :, :]).then_inc(w_in[k], 16)

                for k in range(2):
                    load(k, k)
                with sp.Fori(1, EXPERTS // 2) as i:
                    for k in range(2):
                        sp.wait_ge(d_ready, i * 4 + (2 * k - 2))
                        load_at = i * 2 + k
                        sp.dma_start(gu_w[:, k, :], dram["gate_up"][bass.ds(load_at, 1), :, :]).then_inc(w_in[k], 16)
                        sp.dma_start(down_w[:, k, :], dram["down"][bass.ds(load_at, 1), :, :]).then_inc(w_in[k], 16)

            @block.tensor
            def _(pe):
                with pe.Fori(0, EXPERTS // 2) as i:
                    for k in range(2):
                        pe.wait_ge(w_in[k], i * 32 + 32)
                        for h in range(NH2):
                            for c, m in enumerate(HCH):
                                u = UNITS * k + 3 * h + c
                                pe.wait_ge(hid_ready, i * (2 * UNITS) + (u - 1 + FREE))
                                x = xr[:, h * HALF:(h + 1) * HALF]
                                nc.tensor.matmul(g_ps[u % 2][0:m, :], gu_w[:, k, c * 128:c * 128 + m], x, start=True, stop=True)
                                nc.tensor.matmul(u_ps[u % 2][0:m, :], gu_w[:, k, HID + c * 128:HID + c * 128 + m], x,
                                                 start=True, stop=True).then_inc(gu_ready, 1)
                        for h in range(NH2):
                            pe.wait_ge(hid_ready, i * (2 * UNITS) + (UNITS * k + 3 * h + 3 + FREE))
                            pe.wait_ge(acc_ready, i * (2 * NT) + (NT * k + 4 * h + 4))
                            for j in range(4):
                                for c, m in enumerate(HCH):
                                    mm = nc.tensor.matmul(d_ps[h][:, j * 128:(j + 1) * 128],
                                                          hid[0:m, h, c, j * 128:(j + 1) * 128],
                                                          down_w[0:m, k, c * 128:(c + 1) * 128],
                                                          start=(c == 0), stop=(c == 2))
                            mm.then_inc(d_ready, 1)

            @block.scalar
            def _(act):
                with act.Fori(0, EXPERTS // 2) as i:
                    for u in range(2 * UNITS):
                        m = HCH[u % 3]
                        act.wait_ge(gu_ready, i * (2 * UNITS) + (u + 1))
                        nc.scalar.activation(sil[0:m, u % 2, :], g_ps[u % 2][0:m, :], ACT.Silu).then_inc(sil_ready, 1)

            @block.vector
            def _(dve):
                nc.vector.memset(acc[:, 0:4, :], 0.0).then_inc(hid_ready, 1)
                nc.vector.memset(acc[:, 4:8, :], 0.0).then_inc(hid_ready, 1)
                dve.wait_ge(hid_ready, FREE)
                for t in range(NT):
                    nc.vector.memset(acc[:, t, 0:1], 0.0).then_inc(acc_ready, 1)
                with dve.Fori(0, EXPERTS // 2) as i:
                    for k in range(2):
                        for h in range(NH2):
                            for c, m in enumerate(HCH):
                                u = UNITS * k + 3 * h + c
                                dve.wait_ge(sil_ready, i * (2 * UNITS) + (u + 1))
                                nc.vector.tensor_tensor(hid[0:m, h, c, :], sil[0:m, u % 2, :], u_ps[u % 2][0:m, :],
                                                        ALU.mult).then_inc(hid_ready, 1)
                        for t in range(NT):
                            h, j = t // 4, t % 4
                            if j == 0:
                                dve.wait_ge(d_ready, i * 4 + (2 * k + h + 1))
                            dve.wait_ge(acc_ready, i * (2 * NT) + (NT * k + t + 1))
                            nc.vector.scalar_tensor_tensor(
                                out=acc[:, t, :], in0=d_ps[h][:, j * 128:(j + 1) * 128],
                                scalar=gates[:, t, bass.ds(i * 2 + k, 1)], in1=acc[:, t, :],
                                op0=ALU.mult, op1=ALU.add).then_inc(acc_ready, 1)

        with ExitStack() as inner:
            t_ps = inner.enter_context(nc.psum_tensor("f2c_t", [128, NH2, HALF], F32))
            moe = inner.enter_context(nc.sbuf_tensor("f2c_moe", [128, TOK], F32))
            alpha = inner.enter_context(nc.sbuf_tensor("f2c_alpha", [128, 1], F32))
            turned, alpha_ready, moe_ready, added = sem("turned"), sem("alpha"), sem("moe"), sem("added")
            block = inner.enter_context(nc.Block())

            @block.tensor
            def _(pe):
                for h in range(NH2):
                    for j in range(4):
                        mm = nc.tensor.transpose(t_ps[:, h, j * 128:(j + 1) * 128], acc[:, 4 * h + j, :], C("ident"))
                    mm.then_inc(turned, 1)

            @block.vector
            def _(dve):
                nc.vector.tensor_scalar(alpha[:, :], C("alpha"), -0.5, 2.0, ALU.max, ALU.min).then_inc(alpha_ready, 1)
                dve.wait_ge(alpha_ready, 1)
                for h in range(NH2):
                    t = slice(h * HALF, (h + 1) * HALF)
                    dve.wait_ge(turned, h + 1)
                    nc.vector.scalar_tensor_tensor(out=moe[:, t], in0=t_ps[:, h, :], scalar=alpha[:, 0:1],
                                                   in1=S.xn[:, t], op0=ALU.mult, op1=ALU.add).then_inc(moe_ready, 1)
                    dve.wait_ge(moe_ready, h + 1)
                    nc.vector.tensor_tensor(S.xT[:, t], S.xT[:, t], moe[:, t], ALU.add).then_inc(added, 1)


def context_stage(nc, S):
    DA = DC + 1
    with ExitStack() as ctx:
        sb = lambda n, s: ctx.enter_context(nc.sbuf_tensor("x3_" + n, s, F32))
        sem = lambda n: S.sem("x3_" + n)
        C = lambda n: block_of(S, n)
        q, qk = sb("q", [128, TOK]), sb("qk", [DA, TOK])
        vo = sb("vo", [DA, 128])
        z = sb("z", [DA, TOK])

        with ExitStack() as inner:
            ips = lambda n, s: inner.enter_context(nc.psum_tensor("x3a_" + n, s, F32))
            q_ps, k_ps, v_ps = ips("q_ps", [128, NH2, HALF]), ips("k_ps", [128, NH2, HALF]), ips("v_ps", [128, 128])
            q_ready, q_saved, k_ready, k_saved, v_ready, v_saved = (
                sem(n) for n in ("q", "qs", "k", "ks", "v", "vs"))
            block = inner.enter_context(nc.Block())

            @block.tensor
            def _(pe):
                for h in range(NH2):
                    nc.tensor.matmul(q_ps[:, h, :], C("wq3"), S.xn[:, h * HALF:(h + 1) * HALF],
                                     start=True, stop=True).then_inc(q_ready, 1)
                nc.tensor.matmul(v_ps[0:DA, :], C("wv3"), C("wo3"), start=True, stop=True).then_inc(v_ready, 1)
                for h in range(NH2):
                    pe.wait_ge(q_saved, h + 1)
                    nc.tensor.matmul(k_ps[0:DA, h, :], C("wk3"), q[:, h * HALF:(h + 1) * HALF],
                                     start=True, stop=True).then_inc(k_ready, 1)

            @block.scalar
            def _(act):
                act.wait_ge(v_ready, 1)
                nc.scalar.copy(vo[:, :], v_ps[0:DA, :]).then_inc(v_saved, 1)
                act.wait_ge(k_ready, 1)
                nc.scalar.copy(qk[:, 0:HALF], k_ps[0:DA, 0, :]).then_inc(k_saved, 1)

            @block.vector
            def _(dve):
                for h in range(NH2):
                    dve.wait_ge(q_ready, h + 1)
                    nc.vector.tensor_scalar(q[:, h * HALF:(h + 1) * HALF], q_ps[:, h, :], C("bq3"), (D // 8) ** -0.5,
                                            ALU.add, ALU.mult).then_inc(q_saved, 1)
                dve.wait_ge(k_ready, 2)
                nc.vector.tensor_copy(qk[:, HALF:TOK], k_ps[0:DA, 1, :]).then_inc(k_saved, 1)

        with ExitStack() as inner:
            isb = lambda n, s: inner.enter_context(nc.sbuf_tensor("x3b_" + n, s, F32))
            ips = lambda n: inner.enter_context(nc.psum_tensor(f"x3b_{n}_ps", [128, HALF], F32))
            p, pt = isb("p", [128, 2, NKC * KC]), isb("pt", [KC, 2, NKC * 128])
            nmax, total, rtotal = isb("nmax", [128, 2]), isb("total", [128, 2]), isb("rtotal", [128, 2])
            s_ps, t_ps, z_ps = [ips("s0"), ips("s1")], [ips("t0"), ips("t1")], [ips("z0"), ips("z1")]
            (s_ready, max_ready, e_ready, r_ready, p_ready, t_ready, pt_ready, z_ready, z_saved, padded) = (
                sem(n) for n in ("s", "max", "e", "r", "p", "t", "pt", "z", "zs", "pad"))
            block = inner.enter_context(nc.Block())

            def steps():
                for n in range(NT + 2):
                    yield [(s, n - lag) for s, lag in (("z", 2), ("turn", 1), ("score", 0)) if 0 <= n - lag < NT]

            @block.tensor
            def _(pe):
                for turn in steps():
                    for step, t in turn:
                        if step == "score":
                            if t >= 2:
                                pe.wait_ge(e_ready, t - 1)
                            for j in range(BT):
                                b = BT * t + j
                                mm = nc.tensor.matmul(s_ps[t % 2][j * NQ:(j + 1) * NQ, 0:SC], qk[:, b * NQ:(b + 1) * NQ],
                                                      S.yT[:, b * SC:(b + 1) * SC], start=True, stop=True)
                            mm.then_inc(s_ready, 1)
                        elif step == "turn":
                            pe.wait_ge(p_ready, t + 1)
                            if t == 0:
                                pe.wait_ge(padded, 2)
                            if t >= 2:
                                pe.wait_ge(pt_ready, t - 1)
                            for c in range(NKC):
                                mm = nc.tensor.transpose(t_ps[t % 2][0:KC, c * 128:(c + 1) * 128],
                                                         p[:, t % 2, c * KC:(c + 1) * KC], C("ident"))
                            mm.then_inc(t_ready, 1)
                        else:
                            pe.wait_ge(pt_ready, t + 1)
                            if t >= 2:
                                pe.wait_ge(z_saved, t - 1)
                            for j in range(BT):
                                for c in range(NKC):
                                    at = ((BT * t + j) * NKC + c) * DA
                                    mm = nc.tensor.matmul(z_ps[t % 2][0:DA, j * NQ:(j + 1) * NQ], S.ytm[:, at:at + DA],
                                                          pt[:, t % 2, c * 128 + j * NQ:c * 128 + (j + 1) * NQ],
                                                          start=(c == 0), stop=(c == NKC - 1))
                            mm.then_inc(z_ready, 1)

            @block.scalar
            def _(act):
                for turn in steps():
                    for step, t in turn:
                        if step == "score":
                            act.wait_ge(max_ready, t + 1)
                            if t >= 2:
                                act.wait_ge(t_ready, t - 1)
                            nc.scalar.activation(p[:, t % 2, 0:SC], s_ps[t % 2][:, 0:SC], ACT.Exp,
                                                 bias=nmax[:, t % 2:t % 2 + 1],
                                                 accum_out=total[:, t % 2:t % 2 + 1]).then_inc(e_ready, 1)
                        elif step == "z":
                            act.wait_ge(z_ready, t + 1)
                            nc.scalar.copy(z[:, t * 128:(t + 1) * 128], z_ps[t % 2][0:DA, 0:128]).then_inc(z_saved, 1)

            @block.vector
            def _(dve):
                for k in range(2):
                    nc.vector.memset(p[:, k, SC:NKC * KC], 0.0).then_inc(padded, 1)
                for turn in steps():
                    for step, t in turn:
                        if step == "score":
                            dve.wait_ge(s_ready, t + 1)
                            nc.vector.tensor_reduce(nmax[:, t % 2:t % 2 + 1], s_ps[t % 2][:, 0:SC], AX.X, ALU.max,
                                                    negate=True).then_inc(max_ready, 1)
                            dve.wait_ge(e_ready, t + 1)
                            r = rtotal[:, t % 2:t % 2 + 1]
                            nc.vector.reciprocal(r, total[:, t % 2:t % 2 + 1]).then_inc(r_ready, 1)
                            dve.wait_ge(r_ready, t + 1)
                            nc.vector.tensor_scalar(p[:, t % 2, 0:SC], p[:, t % 2, 0:SC], r, None,
                                                    ALU.mult).then_inc(p_ready, 1)
                        elif step == "turn":
                            dve.wait_ge(t_ready, t + 1)
                            if t >= 2:
                                dve.wait_ge(z_ready, t - 1)
                            nc.vector.tensor_copy(pt[:, t % 2, :], t_ps[t % 2][0:KC, 0:NKC * 128]).then_inc(pt_ready, 1)

        with ExitStack() as inner:
            y_ps = inner.enter_context(nc.psum_tensor("x3c_y", [128, NH2, HALF], F32))
            y_ready, added = sem("y"), sem("added")
            block = inner.enter_context(nc.Block())

            @block.tensor
            def _(pe):
                for h in range(NH2):
                    nc.tensor.matmul(y_ps[:, h, :], vo[:, :], z[:, h * HALF:(h + 1) * HALF],
                                     start=True, stop=True).then_inc(y_ready, 1)

            @block.vector
            def _(dve):
                for h in range(NH2):
                    dve.wait_ge(y_ready, h + 1)
                    x = S.xT[:, h * HALF:(h + 1) * HALF]
                    nc.vector.scalar_tensor_tensor(out=x, in0=y_ps[:, h, :], scalar=C("bo3"), in1=x,
                                                   op0=ALU.add, op1=ALU.add).then_inc(added, 1)


def delta_stage(nc, S):
    with ExitStack() as ctx:
        sb = lambda n, s: ctx.enter_context(nc.sbuf_tensor("r4_" + n, s, F32))
        sem = lambda n: S.sem("r4_" + n)
        C = lambda n: block_of(S, n)
        half = lambda t, h: t[:, h * HALF:(h + 1) * HALF]
        x1, h1 = sb("x1", [128, TOK]), sb("h1", [128, TOK])
        q, k, v, beta = (sb(n, [128, TOK]) for n in ("q", "k", "v", "beta"))
        norm_stage(nc, S, "r4n", S.xn, h1, 1e-6, mean=C("j128"), gain=C("norm1"))

        with ExitStack() as inner:
            isb = lambda n, s: inner.enter_context(nc.sbuf_tensor("r4a_" + n, s, F32))
            p_ps = [inner.enter_context(nc.psum_tensor(f"r4a_p{n}", [128, HALF], F32)) for n in range(8)]
            keep = isb("keep", [128, 3])
            decay, ksq, kinv = isb("decay", [128, B, NQ]), isb("ksq", [128, TOK]), isb("kinv", [128, TOK])
            p_ready, k_saved, v_saved, q_saved, sq_ready, ss_ready = (
                sem(n) for n in ("p", "ks", "vs", "qs", "sq", "ss"))
            clipped, logged, kinv_ready, e_ready, ea_ready = (sem(n) for n in ("clip", "log", "kinv", "e", "ea"))
            chain_sem, done = sem("chain"), sem("done")
            block = inner.enter_context(nc.Block())
            ORDER = ("wk4", "wb4", "wv4", "wq4")

            @block.tensor
            def _(pe):
                for n, w in enumerate(ORDER):
                    for h in range(NH2):
                        nc.tensor.matmul(p_ps[2 * n + h][:, :], C(w), half(h1, h), start=True, stop=True).then_inc(p_ready, 1)
                for h in range(NH2):
                    pe.wait_ge(k_saved, h + 1)
                    pe.wait_ge(sq_ready, h + 1)
                    nc.tensor.matmul(p_ps[h][:, :], C("ones"), half(ksq, h), start=True, stop=True).then_inc(ss_ready, 1)

            @block.scalar
            def _(act):
                nc.scalar.activation(keep[:, 0:1], C("decay"), ACT.Exp, scale=-1.0).then_inc(ea_ready, 1)
                for h in range(NH2):
                    act.wait_ge(p_ready, h + 1)
                    nc.scalar.copy(half(k, h), p_ps[h][:, :]).then_inc(k_saved, 1)
                act.wait_ge(ea_ready, 3)
                for h in range(NH2):
                    act.wait_ge(p_ready, 2 + h + 1)
                    nc.scalar.activation(half(beta, h), p_ps[2 + h][:, :], ACT.Exp, scale=-1.0,
                                         bias=keep[:, 2:3]).then_inc(e_ready, 1)
                for h in range(NH2):
                    act.wait_ge(clipped, h + 1)
                    nc.scalar.activation(half(kinv, h), half(kinv, h), ACT.Ln).then_inc(logged, 1)
                    act.wait_ge(logged, h + 1)
                    nc.scalar.activation(half(kinv, h), half(kinv, h), ACT.Exp, scale=-0.5).then_inc(kinv_ready, 1)
                for h in range(NH2):
                    act.wait_ge(p_ready, 6 + h + 1)
                    nc.scalar.copy(half(q, h), p_ps[6 + h][:, :]).then_inc(q_saved, 1)

            @block.gpsimd
            def _(pool):
                for h in range(NH2):
                    pool.wait_ge(k_saved, h + 1)
                    nc.gpsimd.tensor_tensor(half(ksq, h), half(k, h), half(k, h), ALU.mult).then_inc(sq_ready, 1)

            @block.vector
            def _(dve):
                step = Chain(dve, chain_sem)
                nc.vector.tensor_scalar(keep[:, 2:3], C("beta_b"), -1.0, None, ALU.mult).then_inc(ea_ready, 1)
                dve.wait_ge(ea_ready, 2)
                step(nc.vector.tensor_scalar(keep[:, 1:2], keep[:, 0:1], 1.0, None, ALU.add))
                step(nc.vector.reciprocal(keep[:, 1:2], keep[:, 1:2]))
                nc.vector.tensor_scalar(keep[:, 0:1], keep[:, 1:2], -1.0, 1.0, ALU.mult, ALU.add).then_inc(ea_ready, 1)
                step(nc.vector.memset(decay[:, :, :], 1.0))
                dve.wait_ge(ea_ready, 3)
                step(nc.vector.tensor_scalar(decay[:, :, :], decay[:, :, :], keep[:, 0:1], None, ALU.mult))
                step(nc.vector.memset(decay[:, :, 0:1], 0.0))
                for h in range(NH2):
                    dve.wait_ge(ss_ready, h + 1)
                    nc.vector.tensor_scalar(half(kinv, h), p_ps[h][:, :], 1e-24, LNS, ALU.max, ALU.mult).then_inc(clipped, 1)
                for h in range(NH2):
                    dve.wait_ge(p_ready, 4 + h + 1)
                    step(nc.vector.tensor_scalar(half(v, h), p_ps[4 + h][:, :], keep[:, 1:2], None, ALU.mult))
                    flat = decay[:, :, :].rearrange("p b t -> p (b t)")
                    step(nc.vector.tensor_tensor_scan(half(v, h), half(flat, h), half(v, h), 0.0, ALU.mult, ALU.add))
                for h in range(NH2):
                    dve.wait_ge(e_ready, h + 1)
                    step(nc.vector.tensor_scalar(half(beta, h), half(beta, h), 1.0, None, ALU.add))
                    step(nc.vector.reciprocal(half(beta, h), half(beta, h)))
                    step(nc.vector.tensor_tensor(half(v, h), half(v, h), half(beta, h), ALU.mult))
                for h in range(NH2):
                    dve.wait_ge(kinv_ready, h + 1)
                    nc.vector.scalar_tensor_tensor(out=half(k, h), in0=half(kinv, h), scalar=LNS ** 0.5, in1=half(k, h),
                                                   op0=ALU.mult, op1=ALU.mult).then_inc(done, 1)

        o = sb("o", [128, TOK])
        with ExitStack() as inner:
            isb = lambda n: inner.enter_context(nc.sbuf_tensor(f"r4b_{n}", [128, TOK], F32))
            bt, qk, vt, inv, invt, x, u, low = (isb(n) for n in ("bt", "qk", "vt", "inv", "invt", "x", "u", "low"))
            LEVELS = (2, 4, 8, 16)
            m = [isb(f"m{n}") for n in LEVELS]
            a_ps, b_ps, c_ps, d_ps = ([inner.enter_context(nc.psum_tensor(f"r4b_{n}{h}", [128, HALF], F32))
                                       for h in range(NH2)] for n in "abcd")
            mm_done, dve_done, m_ready = ([sem(f"{n}{h}") for h in range(NH2)] for n in ("mm", "dv", "mr"))
            o_saved = sem("os")
            block = inner.enter_context(nc.Block())
            wide = lambda n: C(n).unsqueeze(1).to_broadcast([128, 4, 128])
            four = lambda t, h: half(t, h).rearrange("p (t n) -> p t n", t=4)
            bank = lambda p: p[:, :].rearrange("p (t n) -> p t n", t=4)
            MM_GRAM, MM_QK, MM_V, MM_TURN = 1, 2, 3, 4
            MM_X = lambda l: 5 + 3 * l
            MM_NEXT = lambda l: 7 + 3 * l if l < 3 else 15
            MM_U, MM_O = 16, 17
            DV_BT, DV_QK, DV_V, DV_INVT, DV_INV = 2, 3, 4, 6, 7
            DV_X = lambda l: 8 + 3 * l
            DV_LEVEL = lambda l: 10 + 3 * l if l < 3 else 18
            DV_U = 19

            def products(h, out, left, right):
                for j in range(4):
                    t = slice((4 * h + j) * 128, (4 * h + j + 1) * 128)
                    mm = nc.tensor.matmul(out[:, j * 128:(j + 1) * 128], left[:, t], right[:, t], start=True, stop=True)
                mm.then_inc(mm_done[h], 1)

            def turns(h, out, src):
                for j in range(4):
                    t = slice((4 * h + j) * 128, (4 * h + j + 1) * 128)
                    mm = nc.tensor.transpose(out[:, j * 128:(j + 1) * 128], src[:, t], C("ident"))
                mm.then_inc(mm_done[h], 1)

            @block.tensor
            def _(pe):
                for h in range(NH2):
                    products(h, a_ps[h], k, k)
                    products(h, b_ps[h], k, q)
                    turns(h, c_ps[h], v)
                for h in range(NH2):
                    pe.wait_ge(dve_done[h], DV_INVT)
                    turns(h, d_ps[h], invt)
                for l in range(len(LEVELS)):
                    for h in range(NH2):
                        pe.wait_ge(dve_done[h], DV_INV if l == 0 else DV_LEVEL(l - 1))
                        pe.wait_ge(m_ready[h], l + 1)
                        products(h, a_ps[h], m[l], inv)
                    for h in range(NH2):
                        pe.wait_ge(dve_done[h], DV_X(l))
                        products(h, b_ps[h], x, invt)
                        if l < 3:
                            products(h, c_ps[h], invt, x)
                for h in range(NH2):
                    pe.wait_ge(dve_done[h], DV_LEVEL(3))
                    products(h, a_ps[h], invt, vt)
                for h in range(NH2):
                    pe.wait_ge(dve_done[h], DV_U)
                    products(h, d_ps[h], u, qk)

            @block.scalar
            def _(act):
                for h in range(NH2):
                    act.wait_ge(mm_done[h], MM_O)
                    nc.scalar.copy(half(o, h), d_ps[h][:, :]).then_inc(o_saved, 1)

            @block.gpsimd
            def _(pool):
                for l, n in enumerate(LEVELS):
                    for h in range(NH2):
                        pool.wait_ge(dve_done[h], DV_BT)
                        nc.gpsimd.tensor_tensor(four(m[l], h), four(bt, h), wide(f"pair{n}"), ALU.mult).then_inc(m_ready[h], 1)

            @block.vector
            def _(dve):
                count = [0, 0]

                def step(h, instruction):
                    count[h] += 1
                    instruction.then_inc(dve_done[h], 1)

                def after(h, products_done=None):
                    if products_done:
                        dve.wait_ge(mm_done[h], products_done)
                    if count[h]:
                        dve.wait_ge(dve_done[h], count[h])

                for h in range(NH2):
                    after(h, MM_GRAM)
                    step(h, nc.vector.tensor_tensor(four(low, h), bank(a_ps[h]), wide("before"), ALU.mult))
                    after(h)
                    step(h, nc.vector.tensor_tensor(half(bt, h), half(low, h), half(beta, h), ALU.mult))
                    after(h, MM_QK)
                    step(h, nc.vector.tensor_tensor(four(qk, h), bank(b_ps[h]), wide("upto"), ALU.mult))
                    after(h, MM_V)
                    step(h, nc.vector.tensor_copy(half(vt, h), c_ps[h][:, :]))
                    step(h, nc.vector.tensor_tensor(four(x, h), four(bt, h), wide("pair1"), ALU.mult))
                    after(h)
                    step(h, nc.vector.tensor_tensor(four(invt, h), wide("ident"), four(x, h), ALU.subtract))
                for h in range(NH2):
                    after(h, MM_TURN)
                    step(h, nc.vector.tensor_copy(half(inv, h), d_ps[h][:, :]))
                for l in range(len(LEVELS)):
                    for h in range(NH2):
                        after(h, MM_X(l))
                        step(h, nc.vector.tensor_copy(half(x, h), a_ps[h][:, :]))
                    for h in range(NH2):
                        after(h, MM_NEXT(l))
                        step(h, nc.vector.tensor_tensor(half(invt, h), half(invt, h), b_ps[h][:, :], ALU.subtract))
                        if l < 3:
                            step(h, nc.vector.tensor_tensor(half(inv, h), half(inv, h), c_ps[h][:, :], ALU.subtract))
                for h in range(NH2):
                    after(h, MM_U)
                    step(h, nc.vector.tensor_copy(half(u, h), a_ps[h][:, :]))

        with ExitStack() as inner:
            y_ps = inner.enter_context(nc.psum_tensor("r4c_y", [128, NH2, HALF], F32))
            y_ready, x1_ready = sem("y"), sem("x1r")
            block = inner.enter_context(nc.Block())

            @block.tensor
            def _(pe):
                for h in range(NH2):
                    nc.tensor.matmul(y_ps[:, h, :], C("wo4"), half(o, h), start=True, stop=True).then_inc(y_ready, 1)

            @block.vector
            def _(dve):
                for h in range(NH2):
                    dve.wait_ge(y_ready, h + 1)
                    nc.vector.tensor_tensor(half(x1, h), half(S.xn, h), y_ps[:, h, :], ALU.add).then_inc(x1_ready, 1)

        norm_stage(nc, S, "r4m", x1, h1, 1e-6, mean=C("j128"), gain=C("norm2"))
        with ExitStack() as inner:
            isb = lambda n, s: inner.enter_context(nc.sbuf_tensor("r4d_" + n, s, F32))
            ips = lambda n: inner.enter_context(nc.psum_tensor(f"r4d_{n}_ps", [128, HALF], F32))
            sil, hid = isb("sil", [128, 4, HALF]), isb("hid", [128, 4, HALF])
            g_ps, u_ps, d_ps = [ips("g0"), ips("g1")], [ips("u0"), ips("u1")], [ips("d0"), ips("d1")]
            gu_ready, sil_ready, hid_ready, d_ready, res_ready, added = (
                sem(n) for n in ("gu", "sil", "hid", "d", "res", "add"))
            block = inner.enter_context(nc.Block())

            @block.tensor
            def _(pe):
                for n in range(4):
                    h, c = n // 2, n % 2
                    if n >= 2:
                        pe.wait_ge(hid_ready, n - 1)
                    w = slice(c * 128, (c + 1) * 128)
                    nc.tensor.matmul(g_ps[c][:, :], C("gate4")[:, w], half(h1, h), start=True, stop=True)
                    nc.tensor.matmul(u_ps[c][:, :], C("up4")[:, w], half(h1, h), start=True, stop=True).then_inc(gu_ready, 1)
                for h in range(NH2):
                    pe.wait_ge(hid_ready, 2 * h + 2)
                    for c in range(2):
                        mm = nc.tensor.matmul(d_ps[h][:, :], C("down4")[:, c * 128:(c + 1) * 128], hid[:, 2 * h + c, :],
                                              start=(c == 0), stop=(c == 1))
                    mm.then_inc(d_ready, 1)

            @block.scalar
            def _(act):
                for n in range(4):
                    act.wait_ge(gu_ready, n + 1)
                    nc.scalar.activation(sil[:, n, :], g_ps[n % 2][:, :], ACT.Silu).then_inc(sil_ready, 1)

            @block.vector
            def _(dve):
                for n in range(4):
                    dve.wait_ge(sil_ready, n + 1)
                    nc.vector.tensor_tensor(hid[:, n, :], sil[:, n, :], u_ps[n % 2][:, :], ALU.mult).then_inc(hid_ready, 1)
                for h in range(NH2):
                    nc.vector.tensor_tensor(half(S.xT, h), half(S.xT, h), half(x1, h), ALU.add).then_inc(res_ready, 1)
                for h in range(NH2):
                    dve.wait_ge(d_ready, h + 1)
                    dve.wait_ge(res_ready, h + 1)
                    nc.vector.tensor_tensor(half(S.xT, h), half(S.xT, h), d_ps[h][:, :], ALU.add).then_inc(added, 1)


def experts_stage(nc, S, dram):
    with ExitStack() as ctx:
        sb = lambda n, s: ctx.enter_context(nc.sbuf_tensor("e5_" + n, s, F32))
        sem = lambda n: S.sem("e5_" + n)
        C = lambda n: block_of(S, n)
        half = lambda t, h: t[:, h * HALF:(h + 1) * HALF]
        NR = D // 2
        gates, gates_t = sb("gates", [128, NT, EXPERTS]), sb("gates_t", [EXPERTS, TOK])
        acc = sb("acc", [128, NT, 128])
        vblk = sb("vblk", [128, 4, B, (DHS + 1) * 4])
        by_group = vblk[:, :, :, :].rearrange("p j n (d g) -> p j n d g", g=4)

        def values(j, b, h):
            return vblk[j * NQ:(j + 1) * NQ, j, :, 0:4 * DHS].rearrange(
                "p (h t b) c -> p h t b c", h=2, b=BT)[:, h, :, b, :]


        hr, hn = sb("hr", [NR, TOK]), sb("hn", [NR, TOK])
        with ExitStack() as inner:
            h_ps = inner.enter_context(nc.psum_tensor("e5a_h", [128, NH2, HALF], F32))
            h_ready, h_saved, ones_set = sem("h"), sem("hs"), sem("ones")
            block = inner.enter_context(nc.Block())

            @block.tensor
            def _(pe):
                for h in range(NH2):
                    nc.tensor.matmul(h_ps[0:NR, h, :], C("rw1"), half(S.xn, h), start=True, stop=True).then_inc(h_ready, 1)

            @block.gpsimd
            def _(pool):
                nc.gpsimd.memset(vblk[:, :, :, :], 0.0).then_inc(ones_set, 1)
                pool.wait_ge(ones_set, 1)
                for j in range(4):
                    nc.gpsimd.memset(vblk[j * NQ:(j + 1) * NQ, j, :, 4 * DHS:], 1.0).then_inc(ones_set, 1)

            @block.vector
            def _(dve):
                for h in range(NH2):
                    dve.wait_ge(h_ready, h + 1)
                    nc.vector.tensor_scalar(half(hr, h), h_ps[0:NR, h, :], C("rb1")[0:NR, :], None,
                                            ALU.add).then_inc(h_saved, 1)

        norm_stage(nc, S, "e5n", hr, hn, 1e-5, feats=NR, centre=C("c64")[0:NR, :], mean=C("j64")[0:NR, :],
                   gain=C("ln_g")[0:NR, :], shift=C("ln_b")[0:NR, :], relu=True)
        with ExitStack() as inner:
            isb = lambda n, s: inner.enter_context(nc.sbuf_tensor("e5b_" + n, s, F32))
            l_ps = inner.enter_context(nc.psum_tensor("e5b_l", [128, NT, EXPERTS], F32))
            l_ready = sem("l")
            block = inner.enter_context(nc.Block())

            @block.tensor
            def _(pe):
                for t in range(NT):
                    mm = nc.tensor.matmul(l_ps[:, t, :], hn[:, t * 128:(t + 1) * 128], C("rw2")[0:NR, :], start=True, stop=True)
                mm.then_inc(l_ready, 1)

            top_two(nc, S, "e5t", l_ps[:, :, :], gates, isb, block, l_ready,
                    bias=C("rb2").unsqueeze(1).to_broadcast([128, NT, EXPERTS]))
        with ExitStack() as inner:
            g_ps = inner.enter_context(nc.psum_tensor("e5c_g", [128, NH2, HALF], F32))
            x_ps = inner.enter_context(nc.psum_tensor("e5c_x", [128, NH2, HALF], F32))
            g_ready, g_saved, x_ready = sem("g"), sem("gs"), sem("x")
            block = inner.enter_context(nc.Block())

            @block.tensor
            def _(pe):
                for t in range(NT):
                    mm = nc.tensor.transpose(g_ps[0:EXPERTS, t // 4, t % 4 * 128:(t % 4 + 1) * 128],
                                             gates[:, t, :], C("ident"))
                mm.then_inc(g_ready, 1)
                for t in range(NT):
                    tok = slice(t * 128, (t + 1) * 128)
                    x = x_ps[:, t // 4, t % 4 * 128:(t % 4 + 1) * 128]
                    nc.tensor.matmul(x, S.xT[:, tok], C("ident"), start=True, stop=False)
                    pe.wait_ge(g_saved, t // 4 + 1)
                    nc.tensor.matmul(x, gates_t[:, tok], C("ob")[0:EXPERTS, :],
                                     start=False, stop=True).then_inc(x_ready, 1)

            @block.vector
            def _(dve):
                dve.wait_ge(g_ready, 1)
                for h in range(NH2):
                    nc.vector.tensor_copy(half(gates_t, h), g_ps[0:EXPERTS, h, :]).then_inc(g_saved, 1)
                for h in range(NH2):
                    dve.wait_ge(x_ready, 4 * h + 4)
                    nc.vector.tensor_copy(acc[:, 4 * h:4 * h + 4, :].rearrange("p t d -> p (t d)"), x_ps[:, h, :])

        with ExitStack() as inner:
            isb = lambda n, s: inner.enter_context(nc.sbuf_tensor("e5d_" + n, s, F32))
            ips = lambda n: inner.enter_context(nc.psum_tensor(f"e5d_{n}_ps", [128, HALF], F32))
            w_qkv = isb("w_qkv", [128, 3 * 128 + 2])
            w_next, w_o = isb("w_next", [128, 129]), isb("w_o", [128, 129])
            qt, kt = isb("qt", [128, TOK]), isb("kt", [128, TOK])
            kblk = isb("kblk", [128, HS, TOK])
            p, pt = isb("p", [128, 2, HS, NQ]), isb("pt", [128, 2, 4, 128])
            nmax, rsum = isb("nmax", [128, 2, HS]), isb("rsum", [128, HS])
            on, ot = isb("on", [128, 2, 128]), isb("ot", [128, 2, 128])
            qk_ps, v_ps, s_ps = ips("qk"), ips("v"), [ips("s0"), ips("s1")]
            t_ps, o_ps, ot_ps, y_ps = ips("t"), ips("o"), ips("ot"), ips("y")
            qkv_in, next_in, wo_ready = sem("qkv_in"), sem("next_in"), sem("wo")
            k_ready, k_saved, k_spread, q_ready, q_saved = sem("k"), sem("ks"), sem("kspread"), sem("q"), sem("qs")
            v_ready, v_spread_dve, v_spread_act = sem("v"), sem("vsd"), sem("vsa")
            s_ready, max_ready, sub_ready, e_ready = sem("s"), sem("max"), sem("sub"), sem("e")
            t_ready, pt_saved, o_ready, rsum_ready = sem("t"), sem("pts"), sem("o"), sem("rsum")
            on_ready, ot_ready, ot_saved, y_ready, acc_ready = sem("on"), sem("ot"), sem("ots"), sem("y"), sem("acc")
            zeroed = sem("zero")
            block = inner.enter_context(nc.Block())
            ROUND = range(NT // 2, NT + NT // 2)

            def reach(engine, semaphore, value):
                if not isinstance(value, int) or value > 0:
                    engine.wait_ge(semaphore, value)

            def live(e, t):
                return not isinstance(e, int) or 0 <= e * NT + t < EXPERTS * NT

            def coming(e):
                return not isinstance(e, int) or e + 1 < EXPERTS

            @block.gpsimd
            def _(pool):
                nc.gpsimd.dma_start(w_qkv[:, :], dram["qkvo"][0, :, 0:386]).then_inc(qkv_in, 16)
                nc.gpsimd.dma_start(w_next[:, :], dram["qkvo"][0, :, 386:515]).then_inc(next_in, 16)
                nc.gpsimd.memset(kblk[:, :, :], 0.0).then_inc(zeroed, 1)
                with pool.Fori(1, EXPERTS) as e:
                    pool.wait_ge(q_saved, e * 2)
                    pool.wait_ge(v_ready, e * 2)
                    nc.gpsimd.dma_start(w_qkv[:, :], dram["qkvo"][bass.ds(e, 1), :, 0:386]).then_inc(qkv_in, 16)
                    pool.wait_ge(wo_ready, e * 1)
                    nc.gpsimd.dma_start(w_next[:, :], dram["qkvo"][bass.ds(e, 1), :, 386:515]).then_inc(next_in, 16)

            @block.sync
            def _(sp):

                def spread(e):
                    for h in range(2):
                        k = slice(h * HALF, (h + 1) * HALF)
                        sp.wait_ge(k_saved, e * 2 + (h + 3))
                        for head in range(HS):
                            r = slice(head * DHS, (head + 1) * DHS)
                            sp.dma_start(kblk[r, head, k], kt[r, k]).then_inc(k_spread, 16)

                sp.wait_ge(zeroed, 1)
                spread(-1)
                with sp.Fori(0, EXPERTS - 1) as e:
                    spread(e)
                out = dram["out"].rearrange("(t p) d -> p t d", p=128)
                for h in range(2):
                    sp.wait_ge(acc_ready, 1 + (EXPERTS - 1) * NT + 4 * h + 4)
                    sp.dma_start(out[:, 4 * h:4 * h + 4, :], acc[:, 4 * h:4 * h + 4, :]).then_inc(S.stored, 16)
                sp.wait_ge(S.stored, 32)

            @block.tensor
            def _(pe):

                def rounds(e):
                    for n in ROUND:
                        h = n // 4 - 1
                        if live(e, n):
                            t = n
                            if t % 4 == 0:
                                pe.wait_ge(q_saved, e * 2 + (t // 4 + 1))
                                pe.wait_ge(k_spread, e * (32 * HS) + 16 * HS * (t // 4 + 1))
                            reach(pe, sub_ready, e * NT + (t - 1))
                            for b in range(BT):
                                at = t % NT * 128 + b * NQ
                                mm = nc.tensor.matmul(s_ps[t % 2][b * NQ:(b + 1) * NQ, :], qt[:, at:at + NQ],
                                                      kblk[:, :, at:at + NQ], start=True, stop=True)
                            mm.then_inc(s_ready, 1)
                        if live(e, n - 4):
                            t = n - 4
                            if t % NT == 0:
                                pe.wait_ge(wo_ready, e + (t // NT + 1))
                            pe.wait_ge(ot_saved, e * NT + (t + 1))
                            pe.wait_ge(acc_ready, e * NT + (t + 1))
                            nc.tensor.matmul(y_ps[:, 0:128], ot[:, t % 2, :], w_o[:, 0:128],
                                             start=True, stop=True).then_inc(y_ready, 1)
                        if live(e, n - 3):
                            t = n - 3
                            pe.wait_ge(on_ready, e * NT + (t + 1))
                            reach(pe, ot_saved, e * NT + t)
                            nc.tensor.transpose(ot_ps[:, 0:128], on[:, t % 2, :], C("ident")).then_inc(ot_ready, 1)
                        if live(e, n - 2):
                            t = n - 2
                            if t % 4 == 0:
                                pe.wait_ge(v_spread_dve, e * 2 + (t // 4 + 1))
                                pe.wait_ge(v_spread_act, e * 2 + (t // 4 + 1))
                            pe.wait_ge(pt_saved, e * NT + (t + 1))
                            reach(pe, on_ready, e * NT + t)
                            for g in range(4):
                                for b in range(BT):
                                    mm = nc.tensor.matmul(
                                        o_ps[b * NQ:(b + 1) * NQ, g * 36:(g + 1) * 36],
                                        pt[:, t % 2, g, b * NQ:(b + 1) * NQ],
                                        by_group[:, :, t % NT * BT + b, :, g], start=True, stop=True)
                            mm.then_inc(o_ready, 1)
                        if coming(e) and n % 4 == 0:
                            if h == 0:
                                pe.wait_ge(qkv_in, e * 16 + 32)
                            reach(pe, q_saved, e * 2 + (h + 2))
                            nc.tensor.matmul(qk_ps[:, :], w_qkv[:, 128:256], half(S.xn, h),
                                             start=True, stop=True).then_inc(k_ready, 1)
                        if coming(e) and n % 4 == 1:
                            pe.wait_ge(k_saved, e * 2 + (h + 3))
                            nc.tensor.matmul(qk_ps[:, :], w_qkv[:, 0:128], half(S.xn, h),
                                             start=True, stop=True).then_inc(q_ready, 1)
                            reach(pe, v_spread_dve, e * 2 + (h + 2))
                            reach(pe, v_spread_act, e * 2 + (h + 2))
                            for t in range(4):
                                at = h * HALF + t * 128
                                mm = nc.tensor.matmul(v_ps[:, t * 128:(t + 1) * 128], S.xn[:, at:at + 128],
                                                      w_qkv[:, 256:384], start=True, stop=True)
                            mm.then_inc(v_ready, 1)
                        if live(e, n - 1):
                            t = n - 1
                            pe.wait_ge(e_ready, e * NT + (t + 1))
                            reach(pe, pt_saved, e * NT + t)
                            for g in range(4):
                                mm = nc.tensor.transpose(t_ps[:, g * 128:(g + 1) * 128],
                                                         p[:, t % 2, 4 * g:4 * g + 4, :].rearrange("p h k -> p (h k)"),
                                                         C("ident"))
                            mm.then_inc(t_ready, 1)

                rounds(-1)
                with pe.Fori(0, EXPERTS - 1) as e:
                    rounds(e)
                rounds(EXPERTS - 1)

            @block.scalar
            def _(act):

                def rounds(e):
                    for n in ROUND:
                        h = n // 4 - 1
                        if live(e, n - 3):
                            t = n - 3
                            if t % NT == 0:
                                act.wait_ge(next_in, e * 16 + 16 * (t // NT + 1))
                                reach(act, y_ready, e * NT + t)
                                nc.scalar.copy(w_o[:, :], w_next[:, :]).then_inc(wo_ready, 1)
                                act.wait_ge(wo_ready, e + (t // NT + 1))
                            act.wait_ge(ot_ready, e * NT + (t + 1))
                            reach(act, acc_ready, e * NT + t)
                            nc.scalar.activation(ot[:, t % 2, :], ot_ps[:, 0:128], ACT.Identity,
                                                 bias=w_o[:, 128:129]).then_inc(ot_saved, 1)
                        if live(e, n):
                            t = n
                            act.wait_ge(sub_ready, e * NT + (t + 1))
                            nc.scalar.activation(p[:, t % 2, :, :], p[:, t % 2, :, :], ACT.Exp,
                                                 scale=DHS ** -0.5).then_inc(e_ready, 1)
                        if coming(e) and n % 4 == 0:
                            act.wait_ge(k_ready, e * 2 + (h + 3))
                            reach(act, k_spread, e * (32 * HS) + 16 * HS * (h + 1))
                            nc.scalar.activation(half(kt, h), qk_ps[:, :], ACT.Identity,
                                                 bias=w_qkv[:, 385:386]).then_inc(k_saved, 1)
                        if coming(e) and n % 4 == 1:
                            act.wait_ge(q_ready, e * 2 + (h + 3))
                            nc.scalar.activation(half(qt, h), qk_ps[:, :], ACT.Identity,
                                                 bias=w_qkv[:, 384:385]).then_inc(q_saved, 1)
                        if coming(e) and n % 4 == 2:
                            act.wait_ge(v_ready, e * 2 + (h + 3))
                            for j in range(4):
                                for b in (2, 3):
                                    mm = nc.scalar.copy(values(j, b, h), v_ps[b * NQ:(b + 1) * NQ, :].rearrange(
                                        "p (t j c) -> p t j c", t=4, j=4)[:, :, j, :])
                            mm.then_inc(v_spread_act, 1)
                        if live(e, n - 1):
                            t = n - 1
                            act.wait_ge(t_ready, e * NT + (t + 1))
                            reach(act, o_ready, e * NT + (t - 1))
                            nc.scalar.copy(pt[:, t % 2, :, :].rearrange("p g q -> p (g q)"), t_ps[:, :]).then_inc(pt_saved, 1)

                rounds(-1)
                with act.Fori(0, EXPERTS - 1) as e:
                    rounds(e)
                rounds(EXPERTS - 1)

            @block.vector
            def _(dve):
                nc.vector.memset(rsum[:, :], 0.0).then_inc(acc_ready, 1)

                def rounds(e):
                    for n in ROUND:
                        h = n // 4 - 1
                        if live(e, n):
                            t = n
                            dve.wait_ge(s_ready, e * NT + (t + 1))
                            s = s_ps[t % 2][:, :].rearrange("p (h k) -> p h k", h=HS)
                            nc.vector.tensor_reduce(nmax[:, t % 2, :], s, AX.X, ALU.max).then_inc(max_ready, 1)
                            dve.wait_ge(max_ready, e * NT + (t + 1))
                            reach(dve, t_ready, e * NT + (t - 1))
                            nc.vector.tensor_tensor(p[:, t % 2, :, :], s,
                                                    nmax[:, t % 2, :].unsqueeze(2).to_broadcast([128, HS, NQ]),
                                                    ALU.subtract).then_inc(sub_ready, 1)
                        if live(e, n - 4):
                            t = n - 4
                            dve.wait_ge(y_ready, e * NT + (t + 1))
                            dve.wait_ge(acc_ready, e * NT + (t + 1))
                            gate = e if t < NT else e + 1
                            gate = slice(gate, gate + 1) if isinstance(e, int) else bass.ds(gate, 1)
                            nc.vector.scalar_tensor_tensor(
                                out=acc[:, t % NT, :], in0=y_ps[:, 0:128], scalar=gates[:, t % NT, gate],
                                in1=acc[:, t % NT, :], op0=ALU.mult, op1=ALU.add).then_inc(acc_ready, 1)
                        if live(e, n - 2):
                            t = n - 2
                            dve.wait_ge(o_ready, e * NT + (t + 1))
                            o = o_ps[:, 0:HS * (DHS + 1)].rearrange("p (h d) -> p h d", h=HS)
                            nc.vector.reciprocal(rsum[:, :], o[:, :, DHS]).then_inc(rsum_ready, 1)
                            dve.wait_ge(rsum_ready, e * NT + (t + 1))
                            reach(dve, ot_ready, e * NT + (t - 1))
                            nc.vector.tensor_tensor(on[:, t % 2, :].rearrange("p (h d) -> p h d", h=HS), o[:, :, 0:DHS],
                                                    rsum[:, :].unsqueeze(2).to_broadcast([128, HS, DHS]),
                                                    ALU.mult).then_inc(on_ready, 1)
                        if coming(e) and n % 4 == 2:
                            dve.wait_ge(v_ready, e * 2 + (h + 3))
                            for j in range(4):
                                for b in (0, 1):
                                    mm = nc.vector.tensor_copy(values(j, b, h), v_ps[b * NQ:(b + 1) * NQ, :].rearrange(
                                        "p (t j c) -> p t j c", t=4, j=4)[:, :, j, :])
                            mm.then_inc(v_spread_dve, 1)

                rounds(-1)
                with dve.Fori(0, EXPERTS - 1) as e:
                    rounds(e)
                rounds(EXPERTS - 1)


EPS = (1e-5, 1e-6)


def program(nc, dram):
    with ExitStack() as ctx:
        S = Shared()
        sb = lambda n, s, dt=F32: ctx.enter_context(nc.sbuf_tensor(n, s, dt))
        S.sem = lambda n: ctx.enter_context(nc.semaphore(n))
        S.xT, S.xn = sb("xT", [D, TOK]), sb("xn", [D, TOK])
        S.const, S.vec, S.wts = sb("const", [128, N_CONST]), sb("vec", [128, N_VEC]), sb("wts", [128, N_WTS])
        S.epst = sb("epst", [128, len(EPS)])
        S.eps = lambda e: S.epst[:, EPS.index(e):EPS.index(e) + 1]
        S.x_in, S.const_in, S.wts_in = S.sem("x_in"), S.sem("const_in"), S.sem("wts_in")
        S.yt_in, S.ytm_in, S.mask_in = S.sem("yt_in"), S.sem("ytm_in"), S.sem("mask_in")
        S.wd_in, S.stored = S.sem("wd_in"), S.sem("stored")
        context = ExitStack()
        csb = lambda n, s, dt=F32: context.enter_context(nc.sbuf_tensor(n, s, dt))
        S.yT, S.ytm = csb("yT", [DC + 1, B * SC]), csb("ytm", [KC, B * NKC * (DC + 1)])
        S.mask = csb("mask", [B, MASK_WORDS], I32)
        eps_set = S.sem("eps_set")
        with nc.Block() as block:

            @block.scalar
            def _(act):
                nc.scalar.preload_act_table_set("natural_log_exp_and_others")

            @block.vector
            def _(dve):
                for n, e in enumerate(EPS):
                    nc.vector.memset(S.epst[:, n:n + 1], e).then_inc(eps_set, 1)

            @block.gpsimd
            def _(pool):
                pool.wait_ge(eps_set, len(EPS))
        load_stage(nc, S, dram)
        stage_sems = []

        def stage_sem(name):
            stage_sems.append(nc.alloc_semaphore(name=name))
            return stage_sems[-1]

        def recycle():
            nc.clear_and_free_semaphores(list(stage_sems))
            nc.all_engine_barrier()
            stage_sems.clear()

        S.sem = stage_sem
        C = lambda n: block_of(S, n)
        norm_stage(nc, S, "n0", S.xT, S.xn, 1e-5, centre=C("c128"), mean=C("j128"))
        norm_stage(nc, S, "n0l", S.xn, S.xn, 1e-5, centre=C("c128"), mean=C("j128"),
                   gain=C("l_g"), shift=C("l_b"))
        cross_stage(nc, S)
        norm_stage(nc, S, "n1", S.xT, S.xn, 1e-5, centre=C("c128"), mean=C("j128"))
        diff_stage(nc, S, dram)
        norm_stage(nc, S, "n2", S.xT, S.xn, 1e-5, centre=C("c128"), mean=C("j128"))
        ffn_stage(nc, S, dram)
        recycle()
        norm_stage(nc, S, "n3", S.xT, S.xn, 1e-5, centre=C("c128"), mean=C("j128"))
        context_stage(nc, S)
        context.close()
        norm_stage(nc, S, "n4", S.xT, S.xn, 1e-5, centre=C("c128"), mean=C("j128"))
        delta_stage(nc, S)
        recycle()
        norm_stage(nc, S, "n5", S.xT, S.xn, 1e-5, centre=C("c128"), mean=C("j128"))
        experts_stage(nc, S, dram)


def constants():
    p = np.arange(128)
    c = np.zeros((128, N_CONST), np.float32)

    def put(name, a):
        at, width = CONST[name]
        c[:a.shape[0], at:at + width] = a

    same = p[:, None] // NQ == p[None, :] // NQ
    put("ident", np.eye(128))
    for n in (128, 96, 64):
        put(f"c{n}", np.eye(n) - 1.0 / n)
    put("j128", np.full((128, 128), 1 / 128))
    put("j96", np.full((96, 128), 1 / 96))
    put("j64", np.full((64, 64), 1 / 64))
    put("heads64", (p[:, None] // 64 == p[None, :] // 64) / 64)
    put("ones", np.ones((128, 128)))
    put("before", same & (p[:, None] < p[None, :]))
    put("upto", same & (p[:, None] <= p[None, :]))
    for n in (1, 2, 4, 8, 16):
        put(f"pair{n}", (p[:, None] // (2 * n) == p[None, :] // (2 * n))
            & (p[:, None] // n % 2 == 0) & (p[None, :] // n % 2 == 1))
    put("rank", np.broadcast_to(8.0 - np.arange(64) % 8, (128, 64)))
    return c


def laid_out(i):
    i = {k: np.asarray(v) for k, v in i.items()}
    f = np.float32

    def pack(where, total, items):
        a = np.zeros((128, total), f)
        for name, v in items.items():
            at, width = where[name]
            a[:v.shape[0], at:at + width] = v
        return a

    col = lambda v: v.reshape(-1, 1)
    rep = lambda v: np.broadcast_to(v.reshape(1, -1), (128, v.size))
    ctx = i["ctx_768"]
    vec = pack(VEC, N_VEC, {
        "x_g": col(i["L0_xattn_ln_x_g"]), "x_b": col(i["L0_xattn_ln_x_b"]),
        "l_g": col(i["L0_xattn_ln_l_g"]), "l_b": col(i["L0_xattn_ln_l_b"]),
        "qn_g": col(np.tile(i["L0_xattn_qn_g"], HC)), "kn_g": col(np.tile(i["L0_xattn_kn_g"], HC)),
        "bo0": col(i["L0_xattn_bo"]), "ffn_w": col(i["L0_ffn_norm_weight"]),
        "alpha": rep(i["L0_ffn_residual_alpha"]), "bq3": col(i["L1_xattn_bq"]), "bo3": col(i["L1_xattn_bo"]),
        "norm1": col(i["L1_attn_norm1_w"]), "norm2": col(i["L1_attn_norm2_w"]),
        "decay": col(i["L1_attn_alpha_logit"]), "beta_b": rep(i["L1_attn_beta_b"]),
        "rb1": col(i["L1_ffn_rb1"]), "ln_g": col(i["L1_ffn_ln_g"]), "ln_b": col(i["L1_ffn_ln_b"]),
        "rs": i["L0_attn_rms_scale"].reshape(2, 128).T, "rb2": rep(i["L1_ffn_rb2"]),
    })
    wkv, wlkv = i["L0_xattn_Wkv"], i["L0_xattn_Wlkv"]
    wts = pack(WTS, N_WTS, {
        "wq0": i["L0_xattn_Wq"].T, "wk0": wkv[:128].T, "wv0": wkv[128:].T,
        "wlk0": wlkv[:128].T, "wlv0": wlkv[128:].T, "wo0": i["L0_xattn_Wo"].T,
        "lq1": i["L0_attn_lambda_q1"].T, "lk1": i["L0_attn_lambda_k1"].T,
        "lq2": i["L0_attn_lambda_q2"].T, "lk2": i["L0_attn_lambda_k2"].T,
        "router2": i["L0_ffn_router_weight"].T,
        "wq3": i["L1_xattn_Wq"],
        "wk3": np.concatenate([i["L1_xattn_Wk"].T, col(i["L1_xattn_bk"])], 1),
        "wv3": np.concatenate([i["L1_xattn_Wv"].T, col(i["L1_xattn_bv"])], 1),
        "wo3": i["L1_xattn_Wo"],
        "wq4": i["L1_attn_Wq"], "wk4": i["L1_attn_Wk"], "wv4": i["L1_attn_Wv"], "wo4": i["L1_attn_Wo"],
        "wb4": np.broadcast_to(i["L1_attn_beta_w"], (128, 128)),
        "gate4": i["L1_attn_w_gate"], "up4": i["L1_attn_w_up"],
        "down4": i["L1_attn_w_down"].reshape(2, 128, 128).transpose(1, 0, 2).reshape(128, 256),
        "rw1": i["L1_ffn_rW1"].T, "rw2": i["L1_ffn_rW2"].T, "ob": i["L1_ffn_ob"],
    })
    y_tm = np.zeros((B, NKC * KC, DC + 1), f)
    y_tm[:, :SC, :DC] = ctx
    y_tm[:, :SC, DC] = 1.0
    y_t = np.ones((DC + 1, B * SC), f)
    y_t[:DC] = ctx.reshape(B * SC, DC).T
    rows = lambda w: w.reshape(16, 128, 128).transpose(1, 0, 2).reshape(128, 2048)
    wd = np.concatenate([
        rows(i["L0_attn_Wq"]), rows(i["L0_attn_Wk"]), i["L0_attn_Wv"].T, rows(i["L0_attn_Wv"]),
        rows(np.ascontiguousarray(i["L0_attn_Wo"].T))], 1)
    down = np.zeros((EXPERTS, 3 * 128, 128), f)
    down[:, :HID] = i["L0_ffn_down_weight"].transpose(0, 2, 1)
    w = {n: i[f"L1_ffn_{n}W"].transpose(0, 2, 1) for n in "qkvo"}
    w["v"] = w["v"].reshape(EXPERTS, 128, 4, 4, DHS).transpose(0, 1, 3, 4, 2).reshape(EXPERTS, 128, 128)
    bias = {n: i[f"L1_ffn_{n}b"][:, :, None] for n in "qkv"}
    qkvo = np.concatenate([w["q"], w["k"], w["v"], bias["q"], bias["k"], w["o"], bias["v"]], 2)
    mask = np.zeros((B, 4 * MASK_WORDS), bool)
    mask[:, :SC] = i["mask_BxS2_bk0"]
    return {
        "x_t": i["x"].reshape(TOK, D).T, "y_t": y_t,
        "y_tm": y_tm.reshape(B, NKC, KC, DC + 1).transpose(2, 0, 1, 3).reshape(KC, -1),
        "mask": mask.view(np.int32), "const": constants(), "vec": vec, "wts": wts,
        "wd": wd, "gate_up": i["L0_ffn_gate_up_weight"].transpose(0, 2, 1),
        "down": down.reshape(EXPERTS, 3, 128, 128).transpose(0, 2, 1, 3).reshape(EXPERTS, 128, 384),
        "qkvo": qkvo,
    }


def kernel(**inputs):
    import numpy as _np
    import concourse.bacc as _bacc
    from concourse.bass_utils import run_bass_kernel_spmd as _run

    nc = _bacc.Bacc("TRN2", target_bir_lowering=False, num_devices=1)
    arrays, dram = {}, {}
    for name, a in laid_out(inputs).items():
        a = _np.ascontiguousarray(a)
        arrays[f"in_{name}"] = a
        dram[name] = nc.dram_tensor(f"in_{name}", a.shape, mybir.dt.from_np(a.dtype), kind="ExternalInput").ap()
    dram["out"] = nc.dram_tensor("out_0", (TOK, D), F32, kind="ExternalOutput").ap()
    program(nc, dram)
    r = _run(nc, [arrays], core_ids=[0])
    return r.results[0]["out_0"].reshape(B, NQ, D)
```

```python
from itertools import islice
from contextlib import ExitStack

import numpy as np
import concourse.bass as bass
from concourse import mybir

F32 = mybir.dt.float32
U8, I32 = mybir.dt.uint8, mybir.dt.int32
ALU = mybir.AluOpType
ACT = mybir.ActivationFunctionType
AX = mybir.AxisListType

B, NQ, D = 32, 32, 128
SC, DC = 257, 96
MASK_WORDS = -(-SC // 4)
TOK = B * NQ
NT = TOK // 128
BT = 128 // NQ
HALF = 512
NH2 = TOK // HALF
KC = 86
NKC = 3
HC, DHC = 2, 64
HD, DHD = 8, 128
EXPERTS = 8
HID = 352
HCH = [128, 128, 96]
HS, DHS = 16, 8
LAMBDA_INIT = 0.8 - 0.6 * float(np.exp(-0.3))
LNS = 1.0e5
NEG = -1.0e30


def columns(parts):
    at, out = 0, {}
    for name, width in parts:
        out[name] = (at, width)
        at += width
    return out, at


CONST, N_CONST = columns([
    ("ident", 128), ("c128", 128), ("j128", 128), ("c96", 96), ("j96", 128), ("heads64", 128), ("headq", 64),
    ("c64", 64), ("j64", 64), ("ones", 128), ("before", 128), ("upto", 128),
    ("pair1", 128), ("pair2", 128), ("pair4", 128), ("pair8", 128), ("pair16", 128),
    ("rank", 64),
])
VEC, N_VEC = columns([(n, 1) for n in (
    "x_g", "x_b", "l_g", "l_b", "qn_g", "kn_g", "bo0", "ffn_w", "alpha", "bq3", "bo3",
    "norm1", "norm2", "decay", "beta_b", "rb1", "ln_g", "ln_b")]
    + [("rs", 2), ("rb2", 8)])
WTS, N_WTS = columns([
    ("wq0", 128), ("wk0", 128), ("wv0", 128), ("wlk0", 128), ("wlv0", 128), ("wo0", 128),
    ("lq1", 8), ("lk1", 8), ("lq2", 8), ("lk2", 8), ("router2", 8),
    ("wq3", 128), ("wk3", 97), ("wv3", 97), ("wo3", 128),
    ("wq4", 128), ("wk4", 128), ("wv4", 128), ("wo4", 128), ("wb4", 128),
    ("gate4", 256), ("up4", 256), ("down4", 256),
    ("rw1", 64), ("rw2", 8), ("ob", 128),
])


class Shared:
    pass


def block_of(stage, name):
    at, width = (CONST if name in CONST else VEC if name in VEC else WTS)[name]
    tile = stage.const if name in CONST else stage.vec if name in VEC else stage.wts
    return tile[:, at:at + width]


def load_stage(nc, S, dram):
    with nc.Block() as block:

        @block.sync
        def _(sp):
            sp.dma_start(S.xT[:, :], dram["x_t"]).then_inc(S.x_in, 16)
            sp.dma_start(S.const[:, :], dram["const"]).then_inc(S.const_in, 16)
            sp.dma_start(S.vec[:, :], dram["vec"]).then_inc(S.const_in, 16)
            quarter = B * NKC * (DC + 1) // 4
            sp.dma_start(S.ytm[:, 0:quarter], dram["y_tm"][:, 0:quarter]).then_inc(S.ytm_in, 16)
            sp.dma_start(S.wts[:, :], dram["wts"]).then_inc(S.wts_in, 16)
            by_pair = dram["mask"].rearrange("(i j) w -> j i w", j=2)
            for j in range(2):
                sp.dma_start(S.mask[64 * j:64 * j + 64, :].rearrange("p (i w) -> p i w", i=B // 2),
                             by_pair[j].partition_broadcast(64)).then_inc(S.mask_in, 16)
            sp.dma_start(S.ytm[:, quarter:], dram["y_tm"][:, quarter:]).then_inc(S.ytm_rest_in, 16)
            sp.dma_start(S.wd[:, :], dram["wd"]).then_inc(S.wd_in, 16)

        @block.gpsimd
        def _(pool):
            pool.wait_ge(S.x_in, 16)
            pool.wait_ge(S.const_in, 32)


def norm_stage(nc, S, name, src, dst, eps, feats=D, centre=None, mean=None, gain=None, shift=None,
               relu=False, tables=False, before=None, within=None, ready=None, banks=None):
    with ExitStack() as own:
        ctx = own if within is None else within[0]
        sb = lambda n, s: ctx.enter_context(nc.sbuf_tensor(f"{name}_{n}", s, F32))
        sem = lambda n: S.sem(f"{name}_{n}")
        square = sb("square", [feats, TOK])
        inv = sb("inv", [feats, TOK])
        centred = None
        if banks is not None:
            centred, var = banks
        elif centre is not None:
            centred = ctx.enter_context(nc.psum_tensor(f"{name}_centred", [128, NH2, HALF], F32))
        if banks is None:
            var = ctx.enter_context(nc.psum_tensor(f"{name}_var", [128, NH2, HALF], F32))
        centred_ready, square_ready, var_ready = sem("centred"), sem("squared"), sem("varred")
        log_ready, inv_ready, scaled, done = sem("log"), sem("invd"), sem("scaled"), sem("done")
        relued = sem("relued") if relu else None

        def half(t, h):
            return t[0:feats, h * HALF:(h + 1) * HALF]

        def body(h):
            return half(src, h) if centre is None else centred[0:feats, h, :]

        block = ctx.enter_context(nc.Block()) if within is None else within[1]

        @block.tensor
        def _(pe):
            if centre is not None:
                for h in range(NH2):
                    if ready is not None:
                        pe.wait_ge(ready, h + 1)
                    nc.tensor.matmul(centred[0:feats, h, :], centre, half(src, h),
                                     start=True, stop=True).then_inc(centred_ready, 1)
            for h in range(NH2):
                pe.wait_ge(square_ready, h + 1)
                nc.tensor.matmul(var[0:feats, h, :], mean, half(square, h),
                                 start=True, stop=True).then_inc(var_ready, 1)

        @block.scalar
        def _(act):
            if tables:
                nc.scalar.preload_act_table_set("natural_log_exp_and_others")
            for h in range(NH2):
                if centre is not None:
                    act.wait_ge(centred_ready, h + 1)
                elif ready is not None:
                    act.wait_ge(ready, h + 1)
                nc.scalar.activation(half(square, h), body(h), ACT.Square).then_inc(square_ready, 1)
            for h in range(NH2):
                act.wait_ge(var_ready, h + 1)
                nc.scalar.activation(half(inv, h), var[0:feats, h, :], ACT.Ln,
                                     bias=S.eps(eps)[0:feats, :]).then_inc(log_ready, 1)
                act.wait_ge(log_ready, h + 1)
                nc.scalar.activation(half(inv, h), half(inv, h), ACT.Exp,
                                     scale=-0.5).then_inc(inv_ready, 1)

        @block.vector
        def _(dve):
            if before is not None:
                before(dve)
            for h in range(NH2):
                dve.wait_ge(inv_ready, h + 1)
                if centre is None and ready is not None:
                    dve.wait_ge(ready, h + 1)
                if gain is None:
                    nc.vector.tensor_tensor(half(dst, h), body(h), half(inv, h),
                                            ALU.mult).then_inc(done, 1)
                    continue
                nc.vector.tensor_tensor(half(dst, h), body(h), half(inv, h),
                                        ALU.mult).then_inc(scaled, 1)
                dve.wait_ge(scaled, h + 1)
                if relu:
                    nc.vector.tensor_scalar(half(square, h), half(dst, h), gain, shift,
                                            ALU.mult, ALU.add).then_inc(done, 1)
                    dve.wait_ge(done, h + 1)
                    nc.vector.tensor_scalar(half(dst, h), half(square, h), 0.0, None, ALU.max).then_inc(relued, 1)
                elif shift is None:
                    nc.vector.tensor_scalar(half(dst, h), half(dst, h), gain, None,
                                            ALU.mult).then_inc(done, 1)
                else:
                    nc.vector.tensor_scalar(half(dst, h), half(dst, h), gain, shift,
                                            ALU.mult, ALU.add).then_inc(done, 1)
    return relued if relu else done


def cross_stage(nc, S):
    with ExitStack() as ctx:
        sb = lambda n, s: ctx.enter_context(nc.sbuf_tensor("c0_" + n, s, F32))
        sem = lambda n: S.sem("c0_" + n)
        C = lambda n: block_of(S, n)
        qblk = sb("qblk", [128, B * HC * NQ])
        qview = qblk[:, :].rearrange("p (b h q) -> p b h q", b=B, h=HC)
        klat = sb("klat", [128, TOK])
        ltm = sb("ltm", [NQ, B * D])
        wkg = sb("wkg", [DC, 128])
        wvg = sb("wvg", [DC + 1, 128])
        bk, gq = sb("bk", [128, 1]), sb("gq", [128, 1])
        z = sb("z", [DC + 1, HC, TOK])
        zl = sb("zl", [128, HC, TOK])
        nmask = sb("nmask", [128, B // 2, SC])
        CHUNKS = B * NKC
        ctx_tm = S.ytm[:, :].rearrange("p (n c) -> p n c", n=CHUNKS)
        GROUPS = 4
        GROUP = CHUNKS // GROUPS
        stats = sb("stats", [KC, CHUNKS, 6])
        mean, dev, m2 = sb("mean", [KC, CHUNKS]), sb("dev", [KC, CHUNKS]), sb("m2", [KC, CHUNKS])
        stats_ready, sum_ready, mean_ready, dev_ready, m2_ready, var_ready = (
            sem("stats"), sem("msum"), sem("mean"), sem("dev"), sem("m2"), sem("var"))
        dev_log, dev_inv, normed, shift_ready, normed_act = (
            sem(n) for n in ("devlog", "devinv", "normed", "shift", "normeda"))
        shift = sb("shift", [KC, CHUNKS])
        BY_ACT = (1,)

        def statistics(n):
            nc.vector.bn_stats(stats[:, n, :], ctx_tm[:, n, 0:DC]).then_inc(stats_ready, 1)

        def moments(dve, k):
            g = slice(k * GROUP, (k + 1) * GROUP)
            dve.wait_ge(stats_ready, (k + 1) * GROUP)
            nc.vector.tensor_tensor(mean[:, g], stats[:, g, 1], stats[:, g, 4], ALU.add).then_inc(sum_ready, 1)
            nc.vector.tensor_tensor(dev[:, g], stats[:, g, 1], stats[:, g, 4], ALU.subtract).then_inc(dev_ready, 1)
            nc.vector.tensor_tensor(m2[:, g], stats[:, g, 2], stats[:, g, 5], ALU.add).then_inc(m2_ready, 1)
            dve.wait_ge(sum_ready, k + 1)
            nc.vector.tensor_scalar(mean[:, g], mean[:, g], 0.5, None, ALU.mult).then_inc(mean_ready, 1)
            dve.wait_ge(dev_ready, 2 * k + 1)
            nc.vector.tensor_tensor(dev[:, g], dev[:, g], dev[:, g], ALU.mult).then_inc(dev_ready, 1)
            dve.wait_ge(dev_ready, 2 * k + 2)
            dve.wait_ge(m2_ready, k + 1)
            nc.vector.scalar_tensor_tensor(out=dev[:, g], in0=dev[:, g], scalar=DC / 4.0, in1=m2[:, g],
                                           op0=ALU.mult, op1=ALU.add).then_inc(var_ready, 1)

        def deviation(act, k):
            d = dev[:, k * GROUP:(k + 1) * GROUP]
            act.wait_ge(var_ready, k + 1)
            nc.scalar.activation(d, d, ACT.Ln, scale=1.0 / DC, bias=S.eps(1e-5)[0:KC, :]).then_inc(dev_log, 1)
            act.wait_ge(dev_log, k + 1)
            nc.scalar.activation(d, d, ACT.Exp, scale=-0.5).then_inc(dev_inv, 1)

        def on_act(n):
            return n >= GROUP and n % NKC in BY_ACT

        def normalise_on_act(act, n):
            if n % GROUP == BY_ACT[0]:
                act.wait_ge(shift_ready, n // GROUP)
            nc.scalar.activation(ctx_tm[:, n, 0:DC], ctx_tm[:, n, 0:DC], ACT.Identity, scale=dev[:, n:n + 1],
                                 bias=shift[:, n:n + 1]).then_inc(normed_act, 1)

        def normalise(dve, n):
            if n % GROUP == 0:
                dve.wait_ge(dev_inv, n // GROUP + 1)
                dve.wait_ge(mean_ready, n // GROUP + 1)
                if n:
                    g = slice(n, n + GROUP)
                    nc.vector.scalar_tensor_tensor(out=shift[:, g], in0=mean[:, g], scalar=-1.0, in1=dev[:, g],
                                                   op0=ALU.mult, op1=ALU.mult).then_inc(shift_ready, 1)
            nc.vector.tensor_scalar(ctx_tm[:, n, 0:DC], ctx_tm[:, n, 0:DC], mean[:, n:n + 1],
                                    dev[:, n:n + 1], ALU.subtract, ALU.mult).then_inc(normed, 1)

        def first_moments(dve):
            dve.wait_ge(S.ytm_in, 16)
            for n in range(GROUP):
                statistics(n)
            moments(dve, 0)

        with ExitStack() as inner:
            block = inner.enter_context(nc.Block())
            ready = norm_stage(nc, S, "n0", S.xT, S.xn, 1e-5, centre=C("c128"), mean=C("j128"), within=(inner, block))
            norm_stage(nc, S, "n0l", S.xn, S.xn, 1e-5, centre=C("c128"), mean=C("j128"), gain=C("l_g"), shift=C("l_b"),
                       before=first_moments, within=(inner, block), ready=ready)

        with ExitStack() as inner:
            isb = lambda n, s: inner.enter_context(nc.sbuf_tensor("c0a_" + n, s, F32))
            ips = lambda n, s: inner.enter_context(nc.psum_tensor("c0a_" + n, s, F32))
            raw, square, inv = isb("raw", [128, 4, HALF]), isb("square", [128, 4, HALF]), isb("inv", [128, 4, HALF])
            raw_ps, ms_ps = ips("raw_ps", [128, 2, HALF]), ips("ms_ps", [128, 2, HALF])
            t_ps = ips("t_ps", [128, 4, HALF])
            w_ps = t_ps[:, 2:4, :]
            wg_ready, bias_ready, bias_saved = sem("wg"), sem("bias"), sem("bias_saved")
            raw_ready, raw_saved, sq_ready, ms_ready = sem("raw"), sem("raws"), sem("sq"), sem("ms")
            clipped, logged, inv_ready, zeroed, gq_ready, done = (
                sem("clip"), sem("log"), sem("inv"), sem("zeroed"), sem("gqr"), sem("done"))
            turned, turn_saved = sem("turned"), [sem("turn_saved0"), sem("turn_saved1")]
            block = inner.enter_context(nc.Block())

            def mean_square(pe, u):
                pe.wait_ge(sq_ready, u + 1)
                if u >= 2:
                    pe.wait_ge(clipped, u - 1)
                nc.tensor.matmul(ms_ps[:, u % 2, :], C("heads64"), square[:, u, :],
                                 start=True, stop=True).then_inc(ms_ready, 1)

            def turn(pe, g):
                if g == 2:
                    pe.wait_ge(bias_saved, 2)
                if g >= 4:
                    pe.wait_ge(turn_saved[g % 2], (g - 4) // 2 + 1)
                for j in range(4):
                    b = 4 * g + j
                    mm = nc.tensor.transpose(t_ps[0:NQ, g % 4, j * 128:(j + 1) * 128],
                                             S.xn[:, b * NQ:(b + 1) * NQ], C("ident"))
                mm.then_inc(turned, 1)

            @block.tensor
            def _(pe):
                pe.wait_ge(S.wts_in, 16)
                nc.tensor.matmul(w_ps[:, 0, 0:1], C("wk0")[0:DC, :], C("x_b")[0:DC, :],
                                 start=True, stop=True)
                nc.tensor.matmul(w_ps[DC:DC + 1, 1, 0:128], C("x_b")[0:DC, :], C("wv0")[0:DC, :],
                                 start=True, stop=True).then_inc(bias_ready, 1)
                for u in range(4):
                    if u >= 2:
                        pe.wait_ge(sq_ready, u - 1)
                    w = C("wq0") if u < 2 else C("wlk0")
                    nc.tensor.matmul(raw_ps[:, u % 2, :], w, S.xn[:, u % 2 * HALF:(u % 2 + 1) * HALF],
                                     start=True, stop=True).then_inc(raw_ready, 1)
                    if u == 1:
                        for g in range(4):
                            turn(pe, g)
                    if u >= 1:
                        mean_square(pe, u - 1)
                mean_square(pe, 3)
                for g in range(4, B // 4):
                    turn(pe, g)

            @block.scalar
            def _(act):
                def save_turned(g):
                    act.wait_ge(turned, g + 1)
                    nc.scalar.copy(ltm[:, g * HALF:(g + 1) * HALF], t_ps[0:NQ, g % 4, :]).then_inc(turn_saved[1], 1)

                deviation(act, 0)
                for u in range(4):
                    act.wait_ge(raw_ready, u + 1)
                    nc.scalar.copy(raw[:, u, :], raw_ps[:, u % 2, :]).then_inc(raw_saved, 1)
                    nc.scalar.activation(square[:, u, :], raw_ps[:, u % 2, :], ACT.Square).then_inc(sq_ready, 1)
                save_turned(1)
                save_turned(3)
                for u in range(4):
                    act.wait_ge(clipped, u + 1)
                    nc.scalar.activation(inv[:, u, :], inv[:, u, :], ACT.Ln).then_inc(logged, 1)
                    act.wait_ge(logged, u + 1)
                    nc.scalar.activation(inv[:, u, :], inv[:, u, :], ACT.Exp, scale=-0.5).then_inc(inv_ready, 1)
                save_turned(5)
                save_turned(7)

            @block.gpsimd
            def _(pool):
                nc.gpsimd.memset(qview[64:128, :, 0, :], 0.0).then_inc(zeroed, 1)
                pool.wait_ge(zeroed, 1)
                nc.gpsimd.memset(qview[0:64, :, 1, :], 0.0).then_inc(zeroed, 1)
                pool.wait_ge(zeroed, 2)
                pool.wait_ge(S.mask_in, 32)
                nc.gpsimd.tensor_scalar(nmask[:, :, :], S.mask[:, :].bitcast(U8).rearrange(
                    "p (i w) -> p i w", i=B // 2)[:, :, 0:SC], -1.0, -NEG, ALU.add, ALU.mult).then_inc(gq_ready, 1)

            @block.vector
            def _(dve):
                dve.wait_ge(S.wts_in, 16)
                nc.vector.tensor_scalar(wkg[:, :], C("wk0")[0:DC, :], C("x_g")[0:DC, :], None,
                                        ALU.mult).then_inc(wg_ready, 1)
                nc.vector.tensor_scalar(wvg[0:DC, :], C("wv0")[0:DC, :], C("x_g")[0:DC, :], None,
                                        ALU.mult).then_inc(wg_ready, 1)
                nc.vector.tensor_scalar(gq[:, :], C("qn_g"), C("kn_g"), DHC ** -0.5,
                                        ALU.mult, ALU.mult).then_inc(gq_ready, 1)
                dve.wait_ge(bias_ready, 1)
                nc.vector.tensor_copy(bk[:, :], w_ps[:, 0, 0:1]).then_inc(bias_saved, 1)
                nc.vector.tensor_copy(wvg[DC:DC + 1, :], w_ps[DC:DC + 1, 1, 0:128]).then_inc(bias_saved, 1)
                for n in range(GROUP):
                    normalise(dve, n)
                for u in range(4):
                    dve.wait_ge(ms_ready, u + 1)
                    nc.vector.tensor_scalar(inv[:, u, :], ms_ps[:, u % 2, :], 1e-16, None,
                                            ALU.max).then_inc(clipped, 1)
                for g in range(0, B // 4, 2):
                    dve.wait_ge(turned, g + 1)
                    nc.vector.tensor_copy(ltm[:, g * HALF:(g + 1) * HALF],
                                          t_ps[0:NQ, g % 4, :]).then_inc(turn_saved[0], 1)
                for u in range(4):
                    dve.wait_ge(inv_ready, u + 1)
                    h = slice(u % 2 * HALF, (u % 2 + 1) * HALF)
                    if u < 2:
                        dve.wait_ge(gq_ready, 1)
                        for k in range(HC):
                            p = slice(k * DHC, (k + 1) * DHC)
                            by_batch = lambda t: t[p, u, :].rearrange("p (b q) -> p b q", q=NQ)
                            nc.vector.scalar_tensor_tensor(
                                out=qview[p, u * B // 2:(u + 1) * B // 2, k, :], in0=by_batch(raw),
                                scalar=gq[p, :], in1=by_batch(inv),
                                op0=ALU.mult, op1=ALU.mult).then_inc(done, 1)
                    else:
                        nc.vector.tensor_tensor(klat[:, h], raw[:, u, :], inv[:, u, :],
                                                ALU.mult).then_inc(done, 1)

        PAIRS = B // 2
        KEYS = SC + NQ
        TURNS = PAIRS // GROUPS
        ACT_SHARE = 1
        SHARE = 2 * GROUP // TURNS
        with ExitStack() as inner:
            isb = lambda n, s: inner.enter_context(nc.sbuf_tensor("c0b_" + n, s, F32))
            ips = lambda n: inner.enter_context(nc.psum_tensor("c0b_" + n, [128, HALF], F32))
            xh, kraw, ksq = isb("xh", [DC, 4, SC]), isb("kraw", [128, 6, SC]), isb("ksq", [128, 4, SC])
            kinv, p = isb("kinv", [128, 2, KEYS]), isb("p", [128, 2, KEYS])
            pt, ptl = isb("pt", [KC, 2, NKC * 128]), isb("ptl", [NQ, 2, 128])
            zt = isb("zt", [128, 2, DC + 1 + D])
            nmax, total, rtotal = isb("nmax", [128, 2]), isb("total", [128, 2]), isb("rtotal", [128, 2])
            x_ps, k_ps, m_ps, s_ps, t_ps, z_ps, w_ps = (
                ips("x"), [ips("k0"), ips("k1")], ips("m"), ips("s"), ips("t"), ips("z"), ips("w"))
            x_ready, xh_ready, k_ready, kraw_ready, ksq_ready, m_ready, clip_ready, klog_ready, kinv_ready, ones_set = (
                sem(n) for n in ("x2", "xh2", "k2", "kraw2", "ksq2", "m2b", "clip2", "klog2", "kinv2", "ones2"))
            (s_ready, scaled, masked, max_ready, e_ready, rsum_ready, t_ready, pt_ready, z_ready, zt_ready,
             w_ready, w_act, w_dve) = (sem(n) for n in (
                 "s3", "scaled3", "masked3", "max3", "e3", "rsum3", "t3", "pt3", "z3", "zt3", "w3", "wa3", "wd3"))
            block = inner.enter_context(nc.Block())
            by_head = lambda out, i: out[:, :, 2 * i * NQ:(2 * i + 2) * NQ].rearrange("c h (b q) -> c b h q", b=2)
            of_pair = lambda x: x.rearrange("c (b h q) -> c b h q", b=2, h=HC)

            LAGS = (("key0", 1), ("score", 3), ("untwist", 6), ("turn0", 0), ("key1", 1), ("norm", 2), ("max", 3), 
                    ("turn", 4), ("turn1", 0), ("z", 5))

            def steps():
                for n in range(PAIRS + 6):
                    yield [(s, n - lag) for s, lag in LAGS if 0 <= n - lag < PAIRS]

            @block.tensor
            def _(pe):
                for turn in steps():
                    for step, i in turn:
                        if step in ("turn0", "turn1"):
                            b = 2 * i + int(step[-1])
                            by_act = sum(on_act(m) for m in range((b + 1) * NKC))
                            pe.wait_ge(normed, (b + 1) * NKC - by_act)
                            if by_act:
                                pe.wait_ge(normed_act, by_act)
                            if b >= 1:
                                pe.wait_ge(xh_ready, b)
                            for c in range(NKC):
                                mm = nc.tensor.transpose(x_ps[0:DC, c * KC:(c + 1) * KC], ctx_tm[:, b * NKC + c, 0:DC],
                                                         C("ident")[0:KC, 0:KC])
                            mm.then_inc(x_ready, 1)
                        elif step in ("key0", "key1"):
                            b = 2 * i + int(step[-1])
                            pe.wait_ge(xh_ready, b + 1)
                            if b >= 2:
                                pe.wait_ge(kraw_ready, b - 1)
                            nc.tensor.matmul(k_ps[b % 2][:, 0:SC], wkg[:, :], xh[:, b % 4, :],
                                             start=True, stop=True).then_inc(k_ready, 1)
                        elif step == "norm":
                            pe.wait_ge(ksq_ready, 2 * i + 2)
                            if i >= 1:
                                pe.wait_ge(clip_ready, i)
                            for j in range(2):
                                mm = nc.tensor.matmul(m_ps[64 * j:64 * j + 64, 0:SC], C("headq"),
                                                      ksq[:, (2 * i + j) % 4, :], start=True, stop=True)
                            mm.then_inc(m_ready, 1)
                        elif step == "score":
                            pe.wait_ge(kraw_ready, 2 * i + 2)
                            if i >= 1:
                                pe.wait_ge(scaled, i)
                            for j in range(2):
                                b = 2 * i + j
                                q = qblk[:, b * 64:b * 64 + 64]
                                o = s_ps[64 * j:64 * j + 64, :]
                                nc.tensor.matmul(o[:, 0:SC], q, kraw[:, b % 6, :], start=True, stop=True)
                                mm = nc.tensor.matmul(o[:, SC:KEYS], q, klat[:, b * NQ:(b + 1) * NQ],
                                                      start=True, stop=True)
                            mm.then_inc(s_ready, 1)
                        elif step == "turn":
                            pe.wait_ge(e_ready, i + 1)
                            if i >= 1:
                                pe.wait_ge(pt_ready, 2 * i)
                            for c in range(NKC):
                                nc.tensor.transpose(t_ps[0:KC, c * 128:(c + 1) * 128],
                                                    p[:, i % 2, c * KC:(c + 1) * KC], C("ident"))
                            nc.tensor.transpose(t_ps[0:NQ, 384:512], p[:, i % 2, SC:KEYS],
                                                C("ident")).then_inc(t_ready, 1)
                        elif step == "z":
                            pe.wait_ge(pt_ready, 2 * i + 2)
                            if i >= 1:
                                pe.wait_ge(zt_ready, i)
                            for c in range(NKC):
                                for j in range(2):
                                    rows = slice(64 * j, 64 * j + 64)
                                    nc.tensor.matmul(z_ps[rows, 0:DC + 1], pt[:, i % 2, c * 128 + 64 * j:c * 128 + 64 * j + 64],
                                                     ctx_tm[:, (2 * i + j) * NKC + c, :], start=(c == 0), stop=(c == NKC - 1))
                            for j in range(2):
                                b = 2 * i + j
                                mm = nc.tensor.matmul(z_ps[64 * j:64 * j + 64, DC + 1:DC + 1 + D],
                                                      ptl[:, i % 2, 64 * j:64 * j + 64], ltm[:, b * D:(b + 1) * D],
                                                      start=True, stop=True)
                            mm.then_inc(z_ready, 1)
                        elif step == "untwist":
                            pe.wait_ge(zt_ready, i + 1)
                            if i >= 1:
                                pe.wait_ge(w_act, i)
                                pe.wait_ge(w_dve, i)
                            nc.tensor.transpose(w_ps[0:DC + 1, 0:128], zt[:, i % 2, 0:DC + 1], C("ident"))
                            nc.tensor.transpose(w_ps[:, 128:256], zt[:, i % 2, DC + 1:DC + 1 + D],
                                                C("ident")).then_inc(w_ready, 1)

            @block.scalar
            def _(act):
                for n, turn in enumerate(steps()):
                    k = n // TURNS + 1
                    chunks = iter(range(0))
                    if k < GROUPS and n % TURNS >= TURNS // 2:
                        if n % TURNS == TURNS // 2:
                            deviation(act, k)
                        first = k * GROUP + n % (TURNS // 2) * SHARE
                        chunks = iter([m for m in range(first, first + SHARE) if on_act(m)])
                    for place, (step, i) in enumerate(turn):
                        if place >= 2:
                            for chunk in islice(chunks, ACT_SHARE):
                                normalise_on_act(act, chunk)
                        if step in ("turn0", "turn1"):
                            b = 2 * i + int(step[-1])
                            act.wait_ge(x_ready, b + 1)
                            if b >= 4:
                                act.wait_ge(k_ready, b - 3)
                            nc.scalar.copy(xh[:, b % 4, :], x_ps[0:DC, 0:SC]).then_inc(xh_ready, 1)
                        elif step in ("key0", "key1"):
                            b = 2 * i + int(step[-1])
                            act.wait_ge(k_ready, b + 1)
                            if i >= 3:
                                act.wait_ge(s_ready, i - 2)
                            nc.scalar.activation(kraw[:, b % 6, :], k_ps[b % 2][:, 0:SC], ACT.Identity,
                                                 bias=bk[:, 0:1]).then_inc(kraw_ready, 1)
                        elif step == "norm":
                            act.wait_ge(clip_ready, i + 1)
                            r = kinv[:, i % 2, 0:SC]
                            nc.scalar.activation(r, r, ACT.Ln).then_inc(klog_ready, 1)
                            act.wait_ge(klog_ready, i + 1)
                            nc.scalar.activation(r, r, ACT.Exp, scale=-0.5).then_inc(kinv_ready, 1)
                        elif step == "max":
                            act.wait_ge(max_ready, i + 1)
                            nc.scalar.activation(p[:, i % 2, :], p[:, i % 2, :], ACT.Exp, bias=nmax[:, i % 2:i % 2 + 1],
                                                 accum_out=total[:, i % 2:i % 2 + 1]).then_inc(e_ready, 1)
                        elif step == "z":
                            act.wait_ge(z_ready, i + 1)
                            act.wait_ge(rsum_ready, i + 1)
                            if i >= 2:
                                act.wait_ge(w_ready, i - 1)
                            nc.scalar.activation(zt[:, i % 2, :], z_ps[:, 0:DC + 1 + D], ACT.Identity,
                                                 scale=rtotal[:, i % 2:i % 2 + 1]).then_inc(zt_ready, 1)
                        elif step == "untwist":
                            act.wait_ge(w_ready, i + 1)
                            nc.scalar.copy(by_head(z, i), of_pair(w_ps[0:DC + 1, 0:128])).then_inc(w_act, 1)
                    for chunk in chunks:
                        normalise_on_act(act, chunk)

            @block.gpsimd
            def _(pool):
                for turn in steps():
                    for step, i in turn:
                        if step in ("key0", "key1"):
                            b = 2 * i + int(step[-1])
                            pool.wait_ge(kraw_ready, b + 1)
                            if i >= 2:
                                pool.wait_ge(m_ready, i - 1)
                            nc.gpsimd.tensor_tensor(ksq[:, b % 4, :], kraw[:, b % 6, :], kraw[:, b % 6, :],
                                                    ALU.mult).then_inc(ksq_ready, 1)
                        elif step == "score":
                            pool.wait_ge(scaled, i + 1)
                            s = p[:, i % 2, 0:SC]
                            nc.gpsimd.tensor_tensor(s, s, nmask[:, i, :], ALU.add).then_inc(masked, 1)

            @block.vector
            def _(dve):
                nc.vector.memset(kinv[:, :, SC:KEYS], 1.0).then_inc(ones_set, 1)
                dve.wait_ge(S.ytm_rest_in, 16)
                for n, turn in enumerate(steps()):
                    k = n // TURNS + 1
                    chunks = iter(range(0))
                    if k < GROUPS:
                        first = k * GROUP + n % (TURNS // 2) * SHARE
                        chunks = iter([m for m in range(first, first + SHARE) if n % TURNS < TURNS // 2 or not on_act(m)])
                    for step, i in turn:
                        if step == "norm":
                            dve.wait_ge(m_ready, i + 1)
                            if i >= 2:
                                dve.wait_ge(scaled, i - 1)
                            nc.vector.tensor_scalar(kinv[:, i % 2, 0:SC], m_ps[:, 0:SC], 1e-16, None,
                                                    ALU.max).then_inc(clip_ready, 1)
                        elif step == "score":
                            dve.wait_ge(s_ready, i + 1)
                            dve.wait_ge(kinv_ready, i + 1)
                            if i == 0:
                                dve.wait_ge(ones_set, 1)
                            if i >= 2:
                                dve.wait_ge(t_ready, i - 1)
                            nc.vector.tensor_tensor(p[:, i % 2, :], s_ps[:, 0:KEYS], kinv[:, i % 2, :],
                                                    ALU.mult).then_inc(scaled, 1)
                        elif step == "max":
                            dve.wait_ge(masked, i + 1)
                            nc.vector.tensor_reduce(nmax[:, i % 2:i % 2 + 1], p[:, i % 2, :], AX.X, ALU.max,
                                                    negate=True).then_inc(max_ready, 1)
                        elif step == "turn":
                            dve.wait_ge(e_ready, i + 1)
                            if i >= 2:
                                dve.wait_ge(zt_ready, i - 1)
                            nc.vector.reciprocal(rtotal[:, i % 2:i % 2 + 1], total[:, i % 2:i % 2 + 1]).then_inc(rsum_ready, 1)
                            dve.wait_ge(t_ready, i + 1)
                            if i >= 2:
                                dve.wait_ge(z_ready, i - 1)
                            nc.vector.tensor_copy(pt[:, i % 2, :], t_ps[0:KC, 0:384]).then_inc(pt_ready, 1)
                            nc.vector.tensor_copy(ptl[:, i % 2, :], t_ps[0:NQ, 384:512]).then_inc(pt_ready, 1)
                        elif step == "untwist":
                            dve.wait_ge(w_act, i + 1)
                            nc.vector.tensor_copy(by_head(zl, i), of_pair(w_ps[:, 128:256])).then_inc(w_dve, 1)
                        for chunk in islice(chunks, 1):
                            if n % TURNS < TURNS // 2:
                                statistics(chunk)
                            else:
                                normalise(dve, chunk)
                    for chunk in chunks:
                        if n % TURNS < TURNS // 2:
                            statistics(chunk)
                        else:
                            normalise(dve, chunk)
                    if k < GROUPS and n % TURNS == TURNS // 2 - 1:
                        moments(dve, k)

        with ExitStack() as inner:
            o_sb = inner.enter_context(nc.sbuf_tensor("c0c_o", [128, TOK], F32))
            o_ps = inner.enter_context(nc.psum_tensor("c0c_o_ps", [128, NH2, HALF], F32))
            y_ps = inner.enter_context(nc.psum_tensor("c0c_y_ps", [128, NH2, HALF], F32))
            o_ready, o_saved, y_ready, added = sem("o4"), sem("os4"), sem("y4"), sem("add4")
            block = inner.enter_context(nc.Block())

            @block.tensor
            def _(pe):
                for h in range(NH2):
                    t = slice(h * HALF, (h + 1) * HALF)
                    for k in range(HC):
                        w = slice(k * DHC, (k + 1) * DHC)
                        o = o_ps[w, h, :]
                        nc.tensor.matmul(o, wvg[:, w], z[:, k, t], start=True, stop=False)
                        mm = nc.tensor.matmul(o, C("wlv0")[:, w], zl[:, k, t], start=False, stop=True)
                    mm.then_inc(o_ready, 1)
                for h in range(NH2):
                    pe.wait_ge(o_saved, h + 1)
                    nc.tensor.matmul(y_ps[:, h, :], C("wo0"), o_sb[:, h * HALF:(h + 1) * HALF],
                                     start=True, stop=True).then_inc(y_ready, 1)

            @block.scalar
            def _(act):
                for h in range(NH2):
                    act.wait_ge(o_ready, h + 1)
                    nc.scalar.copy(o_sb[:, h * HALF:(h + 1) * HALF], o_ps[:, h, :]).then_inc(o_saved, 1)

            @block.vector
            def _(dve):
                for h in range(NH2):
                    dve.wait_ge(y_ready, h + 1)
                    x = S.xT[:, h * HALF:(h + 1) * HALF]
                    nc.vector.scalar_tensor_tensor(out=x, in0=y_ps[:, h, :], scalar=C("bo0"), in1=x,
                                                   op0=ALU.add, op1=ALU.add).then_inc(added, 1)

            norm_stage(nc, S, "n1", S.xT, S.xn, 1e-5, centre=C("c128"), mean=C("j128"),
                       within=(inner, block), ready=added)


def diff_stage(nc, S, dram):
    HH = 2 * HD
    with ExitStack() as ctx:
        sb = lambda n, s: ctx.enter_context(nc.sbuf_tensor("d1_" + n, s, F32))
        sem = lambda n: S.sem("d1_" + n)
        C = lambda n: block_of(S, n)
        wd = S.wd
        wq, wk, wvt, wv, wo = (wd[:, n * 2048:(n + 1) * 2048] for n in range(5))
        wkq = sb("wkq", [128, HH, 128])
        wvo = sb("wvo", [128, HD, 128])
        xtm = sb("xtm", [128, NT, 128])
        prod, nlam = sb("prod", [128, 2, HD]), sb("nlam", [128, HD])
        at = sb("at", [128, 2, HD * 128])
        acc = sb("acc", [128, 2, NT, 128])

        with ExitStack() as inner:
            w_ps = [inner.enter_context(nc.psum_tensor(f"d1a_w{n}", [128, 4, 128], F32)) for n in range(8)]
            elam = inner.enter_context(nc.sbuf_tensor("d1a_elam", [128, 2, HD], F32))
            kq_ready, kq_saved, vo_ready, t_ready, all_saved = (
                sem("kq"), sem("kqs"), sem("vo"), sem("t"), sem("alls"))
            prod_ready, lam_ready, elam_ready, scaled, lam_done, zeroed = (
                sem("prod"), sem("lam"), sem("elam"), sem("scaled"), sem("lamd"), sem("zero"))
            block = inner.enter_context(nc.Block())

            @block.tensor
            def _(pe):
                for g in range(2):
                    for j in range(4):
                        t = 4 * g + j
                        mm = nc.tensor.transpose(w_ps[6 + g][:, j, :], S.xn[:, t * 128:(t + 1) * 128], C("ident"))
                    mm.then_inc(t_ready, 1)
                pe.wait_ge(S.wd_in, 16)
                for g in range(4):
                    for j in range(4):
                        e = slice((4 * g + j) * 128, (4 * g + j + 1) * 128)
                        mm = nc.tensor.matmul(w_ps[g][:, j, :], wk[:, e], wq[:, e], start=True, stop=True)
                    mm.then_inc(kq_ready, 1)
                pe.wait_ge(scaled, 2)
                for g in range(2):
                    for j in range(4):
                        for c in range(2):
                            k = 2 * (4 * g + j) + c
                            e = slice(k * 128, (k + 1) * 128)
                            mm = nc.tensor.matmul(w_ps[4 + g][:, j, :], wv[:, e], wo[:, e],
                                                  start=(c == 0), stop=(c == 1))
                    mm.then_inc(vo_ready, 1)
                pe.wait_ge(t_ready, 2)
                pe.wait_ge(all_saved, 1)
                pe.wait_ge(prod_ready, 2)
                nc.tensor.matmul(w_ps[6][:, 0, 0:2 * HD], C("ones"), prod[:, :, :], start=True, stop=True).then_inc(lam_ready, 1)

            @block.scalar
            def _(act):
                for g in range(4):
                    act.wait_ge(kq_ready, g + 1)
                    nc.scalar.copy(wkq[:, 4 * g:4 * g + 4, :], w_ps[g][:, :, :]).then_inc(kq_saved, 1)
                act.wait_ge(lam_ready, 1)
                nc.scalar.activation(elam[:, :, :], w_ps[6][:, 0, 0:2 * HD].rearrange("p (a h) -> p a h", a=2),
                                     ACT.Exp).then_inc(elam_ready, 1)

            @block.gpsimd
            def _(pool):
                nc.gpsimd.memset(at[:, :, :], 0.0).then_inc(zeroed, 1)

            @block.vector
            def _(dve):
                nc.vector.tensor_tensor(prod[:, 0, :], C("lq1"), C("lk1"), ALU.mult).then_inc(prod_ready, 1)
                nc.vector.tensor_tensor(prod[:, 1, :], C("lq2"), C("lk2"), ALU.mult).then_inc(prod_ready, 1)
                for g in range(2):
                    dve.wait_ge(t_ready, g + 1)
                    nc.vector.tensor_copy(xtm[:, 4 * g:4 * g + 4, :], w_ps[6 + g][:, :, :]).then_inc(all_saved, 1)
                dve.wait_ge(S.wd_in, 16)
                by_half = wo.rearrange("p (h c n) -> p h c n", h=HD, c=2)
                for c in range(2):
                    nc.vector.tensor_scalar(by_half[:, :, c, :], by_half[:, :, c, :], C("rs")[:, c:c + 1],
                                            1.0 - LAMBDA_INIT, ALU.mult, ALU.mult).then_inc(scaled, 1)
                for g in range(2):
                    dve.wait_ge(vo_ready, g + 1)
                    nc.vector.tensor_copy(wvo[:, 4 * g:4 * g + 4, :], w_ps[4 + g][:, :, :]).then_inc(all_saved, 1)
                dve.wait_ge(elam_ready, 1)
                nc.vector.scalar_tensor_tensor(out=nlam[:, :], in0=elam[:, 1, :], scalar=LAMBDA_INIT, in1=elam[:, 0, :],
                                               op0=ALU.subtract, op1=ALU.subtract).then_inc(lam_done, 1)

        with ExitStack() as inner:
            isb = lambda n, s: inner.enter_context(nc.sbuf_tensor("d1b_" + n, s, F32))
            ips = lambda n: inner.enter_context(nc.psum_tensor(f"d1b_{n}_ps", [128, HALF], F32))
            r_sb = isb("r", [128, 2, HH * 128])
            e_sb, nmax, sums, rsum = isb("e", [128, HH, NQ]), isb("nmax", [128, HH]), isb("sums", [128, HH]), isb("rsum", [128, HH])
            attn = isb("attn", [128, HD, NQ])
            part = isb("part", [128, 4, 128])
            z_sb = isb("z", [128, 2, HD * 128])
            junk, ssq, rms = isb("junk", [128, HD, 2 * DHD]), isb("ssq", [128, 2, HD]), isb("rms", [128, 2, HD])
            r_ps, o_ps = [ips("r0"), ips("r1")], [ips("o0"), ips("o1")]
            s_ps, y_ps = ips("s"), [ips("y0"), ips("y1")]
            z_ps = [ips("z"), y_ps[0]]
            (r_ready, r_act, r_dve, s_ready, max_ready, sub_ready, e_ready, sum_ready, rsum_ready, nl_ready,
             p_ready, a_ready, at_ready, z_ready, z_act, z_dve, o_ready, ssq_ready, rlog, rms_ready, y_ready,
             acc_dve, acc_pool, part_ready) = (sem(n) for n in (
                 "r", "ra", "rd", "s", "max", "sub", "e", "sum", "rsum", "nl", "p", "a", "at", "z", "za",
                 "zd", "o", "ssq", "rlog", "rms", "y", "accd", "accp", "part"))
            block = inner.enter_context(nc.Block())
            by_half = lambda t: t[:, :].rearrange("p (h s) -> p h s", s=2)

            def steps():
                for n in range(NT + 4):
                    yield [(s, n - lag) for s, lag in (("at", 2), ("y", 4), ("o", 3), ("score", 1),  ("z", 2), ("r", 0))
                           if 0 <= n - lag < NT]

            @block.tensor
            def _(pe):
                for turn in steps():
                    for step, t in turn:
                        if step == "r":
                            for g in range(4):
                                if t or g >= 2:
                                    pe.wait_ge((r_act, r_dve)[g % 2], 2 * t + g // 2)
                                for j in range(4):
                                    mm = nc.tensor.matmul(r_ps[g % 2][:, j * 128:(j + 1) * 128], wkq[:, 4 * g + j, :],
                                                          S.xn[:, t * 128:(t + 1) * 128], start=True, stop=True)
                                mm.then_inc(r_ready, 1)
                        elif step == "score":
                            pe.wait_ge(r_act, 2 * t + 2)
                            pe.wait_ge(r_dve, 2 * t + 2)
                            if t:
                                pe.wait_ge(sub_ready, t)
                            keys = r_sb[:, t % 2, :].rearrange("p (h b k) -> p h b k", h=HH, b=BT)
                            for b in range(BT):
                                at_b = t * 128 + b * NQ
                                mm = nc.tensor.matmul(s_ps[b * NQ:(b + 1) * NQ, :], S.xn[:, at_b:at_b + NQ],
                                                      keys[:, :, b, :], start=True, stop=True)
                            mm.then_inc(s_ready, 1)
                        elif step == "z":
                            pe.wait_ge(at_ready, BT * (t + 1))
                            for g in range(2):
                                if g == 0 and t:
                                    pe.wait_ge(z_act, t)
                                if g == 1 and t >= 2:
                                    pe.wait_ge(acc_dve, 4 * (t - 1))
                                nc.tensor.matmul(z_ps[g][:, :], xtm[:, t, :], at[:, t % 2, g * HALF:(g + 1) * HALF],
                                                 start=True, stop=True).then_inc(z_ready, 1)
                        elif step == "o":
                            pe.wait_ge(z_act, t + 1)
                            pe.wait_ge(z_dve, t + 1)
                            for h in range(HD):
                                if t or h >= 4:
                                    pe.wait_ge(ssq_ready, HD * t + h // 2 * 2 - 2)
                                mm = nc.tensor.matmul(o_ps[h // 2 % 2][:, h % 2 * 256:h % 2 * 256 + 256],
                                                      z_sb[:, t % 2, h * 128:(h + 1) * 128], wvt[:, h * 256:(h + 1) * 256],
                                                      start=True, stop=True)
                                if h % 2:
                                    mm.then_inc(o_ready, 1)
                        elif step == "y":
                            for g in range(2):
                                if g == 0:
                                    pe.wait_ge(z_dve, min(t + 2, NT))
                                    if t:
                                        pe.wait_ge(acc_dve, 4 * t)
                                elif t:
                                    pe.wait_ge(part_ready, t)
                                for j in range(4):
                                    h = 4 * g + j
                                    mm = nc.tensor.matmul(y_ps[g][:, j * 128:(j + 1) * 128],
                                                          z_sb[:, t % 2, h * 128:(h + 1) * 128], wvo[:, h, :],
                                                          start=True, stop=True)
                                mm.then_inc(y_ready, 1)

            @block.scalar
            def _(act):
                for turn in steps():
                    for step, t in turn:
                        if step == "r":
                            for g in (0, 2):
                                act.wait_ge(r_ready, 4 * t + g + 1)
                                if t >= 2:
                                    act.wait_ge(s_ready, t - 1)
                                nc.scalar.copy(r_sb[:, t % 2, g * HALF:(g + 1) * HALF], r_ps[0][:, :]).then_inc(r_act, 1)
                        elif step == "score":
                            act.wait_ge(sub_ready, t + 1)
                            nc.scalar.activation(e_sb[:, :, :], e_sb[:, :, :], ACT.Exp, scale=DHD ** -0.5).then_inc(e_ready, 1)
                        elif step == "z":
                            act.wait_ge(z_ready, 2 * t + 1)
                            if t >= 2:
                                act.wait_ge(y_ready, 2 * t - 2)
                            nc.scalar.copy(z_sb[:, t % 2, 0:HALF], z_ps[0][:, :]).then_inc(z_act, 1)
                        elif step == "y":
                            act.wait_ge(y_ready, 2 * t + 2)
                            act.wait_ge(rms_ready, t + 1)
                            if t:
                                act.wait_ge(acc_pool, 2 * t)
                            for h in range(4):
                                mm = nc.scalar.activation(part[:, h, :], y_ps[1][:, h * 128:(h + 1) * 128], ACT.Identity,
                                                          scale=rms[:, t % 2, 4 + h:5 + h])
                            mm.then_inc(part_ready, 1)
                        elif step == "o":
                            if t >= 2:
                                act.wait_ge(rms_ready, t - 1)
                            for h in range(HD):
                                if h % 2 == 0:
                                    act.wait_ge(o_ready, 4 * t + h // 2 + 1)
                                nc.scalar.activation(junk[:, h, :], o_ps[h // 2 % 2][:, h % 2 * 256:h % 2 * 256 + 256], ACT.Square,
                                                     accum_out=ssq[:, t % 2, h:h + 1]).then_inc(ssq_ready, 1)
                            act.wait_ge(ssq_ready, HD * (t + 1))
                            if t >= 2:
                                act.wait_ge(acc_dve, 4 * (t - 1))
                                act.wait_ge(part_ready, t - 1)
                            nc.scalar.activation(rms[:, t % 2, :], ssq[:, t % 2, :], ACT.Ln, scale=1.0 / (2 * DHD),
                                                 bias=S.eps(1e-5)).then_inc(rlog, 1)
                            act.wait_ge(rlog, t + 1)
                            nc.scalar.activation(rms[:, t % 2, :], rms[:, t % 2, :], ACT.Exp, scale=-0.5).then_inc(rms_ready, 1)

            @block.vector
            def _(dve):
                for turn in steps():
                    for step, t in turn:
                        if step == "r":
                            for g in (1, 3):
                                dve.wait_ge(r_ready, 4 * t + g + 1)
                                if t >= 2:
                                    dve.wait_ge(s_ready, t - 1)
                                nc.vector.tensor_copy(r_sb[:, t % 2, g * HALF:(g + 1) * HALF], r_ps[1][:, :]).then_inc(r_dve, 1)
                        elif step == "score":
                            dve.wait_ge(s_ready, t + 1)
                            s = s_ps[:, :].rearrange("p (h k) -> p h k", k=NQ)
                            nc.vector.tensor_reduce(nmax[:, :], s, AX.X, ALU.max).then_inc(max_ready, 1)
                            dve.wait_ge(max_ready, t + 1)
                            if t:
                                dve.wait_ge(a_ready, t)
                            nc.vector.tensor_tensor(e_sb[:, :, :], s, nmax[:, :].unsqueeze(2).to_broadcast([128, HH, NQ]),
                                                    ALU.subtract).then_inc(sub_ready, 1)
                            dve.wait_ge(e_ready, t + 1)
                            nc.vector.tensor_reduce(sums[:, :], e_sb[:, :, :], AX.X, ALU.add).then_inc(sum_ready, 1)
                            dve.wait_ge(sum_ready, t + 1)
                            nc.vector.reciprocal(rsum[:, :], sums[:, :]).then_inc(rsum_ready, 1)
                            dve.wait_ge(rsum_ready, t + 1)
                            nc.vector.tensor_tensor(by_half(rsum)[:, :, 1], by_half(rsum)[:, :, 1], nlam[:, :],
                                                    ALU.mult).then_inc(nl_ready, 1)
                        elif step == "at":
                            dve.wait_ge(a_ready, t + 1)
                            if t >= 2:
                                dve.wait_ge(z_ready, 2 * t - 2)
                            for b in range(BT):
                                p = slice(b * NQ, (b + 1) * NQ)
                                nc.vector.transpose(
                                    at[p, t % 2, :].rearrange("p (h q) -> p h q", h=HD)[:, :, b * NQ:(b + 1) * NQ],
                                    attn[p, :, :]).then_inc(at_ready, 1)
                        elif step == "z":
                            dve.wait_ge(z_ready, 2 * t + 2)
                            if t >= 2:
                                dve.wait_ge(y_ready, 2 * t - 2)
                            nc.vector.tensor_copy(z_sb[:, t % 2, HALF:2 * HALF], z_ps[1][:, :]).then_inc(z_dve, 1)
                        elif step == "y":
                            dve.wait_ge(rms_ready, t + 1)
                            dve.wait_ge(y_ready, 2 * t + 1)
                            for h in range(4):
                                y, out = y_ps[0][:, h * 128:(h + 1) * 128], acc[:, 0, t, :]
                                if h == 0:
                                    nc.vector.tensor_scalar(out, y, rms[:, t % 2, h:h + 1], None,
                                                            ALU.mult).then_inc(acc_dve, 1)
                                else:
                                    dve.wait_ge(acc_dve, 4 * t + h)
                                    nc.vector.scalar_tensor_tensor(out=out, in0=y, scalar=rms[:, t % 2, h:h + 1], in1=out,
                                                                   op0=ALU.mult, op1=ALU.add).then_inc(acc_dve, 1)

            @block.gpsimd
            def _(pool):
                for turn in steps():
                    for step, t in turn:
                        if step == "score":
                            pool.wait_ge(nl_ready, t + 1)
                            nc.gpsimd.tensor_tensor(e_sb[:, :, :], e_sb[:, :, :],
                                                    rsum[:, :].unsqueeze(2).to_broadcast([128, HH, NQ]),
                                                    ALU.mult).then_inc(p_ready, 1)
                            pool.wait_ge(p_ready, t + 1)
                            if t:
                                pool.wait_ge(at_ready, BT * t)
                            both = e_sb[:, :, :].rearrange("p (h s) k -> p h s k", s=2)
                            nc.gpsimd.tensor_tensor(attn[:, :, :], both[:, :, 0, :], both[:, :, 1, :], ALU.add).then_inc(a_ready, 1)
                        elif step == "y":
                            pool.wait_ge(part_ready, t + 1)
                            nc.gpsimd.tensor_tensor(part[:, 0:2, :], part[:, 0:2, :], part[:, 2:4, :],
                                                    ALU.add).then_inc(acc_pool, 1)
                            pool.wait_ge(acc_pool, 2 * t + 1)
                            nc.gpsimd.tensor_tensor(acc[:, 1, t, :], part[:, 0, :], part[:, 1, :],
                                                    ALU.add).then_inc(acc_pool, 1)

        with ExitStack() as inner:
            x_ps = inner.enter_context(nc.psum_tensor("d1c_x", [128, NH2, HALF], F32))
            x_ready, added = sem("x"), sem("added")
            block = inner.enter_context(nc.Block())

            @block.tensor
            def _(pe):
                for t in range(NT):
                    x = x_ps[:, t // 4, t % 4 * 128:(t % 4 + 1) * 128]
                    nc.tensor.matmul(x, acc[:, 0, t, :], C("ident"), start=True, stop=False)
                    nc.tensor.matmul(x, acc[:, 1, t, :], C("ident"), start=False, stop=True).then_inc(x_ready, 1)

            @block.vector
            def _(dve):
                for h in range(NH2):
                    dve.wait_ge(x_ready, 4 * h + 4)
                    x = S.xT[:, h * HALF:(h + 1) * HALF]
                    nc.vector.tensor_tensor(x, x_ps[:, h, :], x, ALU.add).then_inc(added, 1)

            norm_stage(nc, S, "n2", S.xT, S.xn, 1e-5, centre=C("c128"), mean=C("j128"),
                       within=(inner, block), ready=added)


class Chain:

    def __init__(self, engine, semaphore):
        self.engine, self.semaphore, self.count = engine, semaphore, 0

    def __call__(self, instruction):
        self.count += 1
        instruction.then_inc(self.semaphore, 1)
        self.engine.wait_ge(self.semaphore, self.count)


def top_two(nc, S, name, logits, gates, sb, logits_ready, bias=None):
    sem = lambda n: S.sem(f"{name}_{n}")
    shape = [128, NT, EXPERTS]
    p, key, first, second, rest = (sb(n, shape) for n in ("p", "key", "first", "second", "rest"))
    top, row = sb("top", [128, NT]), sb("row", [128, NT])
    chain_sem, shifted, exp_ready, gates_ready = sem("chain"), sem("shifted"), sem("exp"), sem("gates")
    wide = lambda t: t[:, :].unsqueeze(2).to_broadcast(shape)
    rank = block_of(S, "rank").rearrange("p (t e) -> p t e", e=EXPERTS)

    def exponents(act):
        act.wait_ge(shifted, 1)
        nc.scalar.activation(p[:, :, :], p[:, :, :], ACT.Exp).then_inc(exp_ready, 1)

    def choice(dve):
        step = Chain(dve, chain_sem)
        tt = lambda *a: step(nc.vector.tensor_tensor(*a))
        dve.wait_ge(logits_ready, 1)
        source = logits
        if bias is not None:
            tt(key[:, :, :], logits, bias, ALU.add)
            source = key[:, :, :]
        step(nc.vector.tensor_reduce(top[:, :], source, AX.X, ALU.max))
        nc.vector.tensor_tensor(p[:, :, :], source, wide(top), ALU.subtract).then_inc(shifted, 1)
        dve.wait_ge(exp_ready, 1)
        step(nc.vector.tensor_reduce(row[:, :], p[:, :, :], AX.X, ALU.add))
        step(nc.vector.reciprocal(row[:, :], row[:, :]))
        tt(p[:, :, :], p[:, :, :], wide(row), ALU.mult)

        def select(out, src):
            step(nc.vector.tensor_reduce(top[:, :], src[:, :, :], AX.X, ALU.max))
            tt(key[:, :, :], src[:, :, :], wide(top), ALU.is_ge)
            tt(key[:, :, :], key[:, :, :], rank, ALU.mult)
            step(nc.vector.tensor_reduce(top[:, :], key[:, :, :], AX.X, ALU.max))
            tt(out[:, :, :], key[:, :, :], wide(top), ALU.is_equal)

        select(first, p)
        step(nc.vector.scalar_tensor_tensor(out=rest[:, :, :], in0=first[:, :, :], scalar=-2.0, in1=p[:, :, :],
                                            op0=ALU.mult, op1=ALU.add))
        select(second, rest)
        tt(first[:, :, :], first[:, :, :], second[:, :, :], ALU.add)
        tt(p[:, :, :], p[:, :, :], first[:, :, :], ALU.mult)
        step(nc.vector.tensor_reduce(row[:, :], p[:, :, :], AX.X, ALU.add))
        step(nc.vector.reciprocal(row[:, :], row[:, :]))
        nc.vector.tensor_tensor(gates[:, :, :], p[:, :, :], wide(row), ALU.mult).then_inc(gates_ready, 1)

    return exponents, choice, gates_ready


def ffn_stage(nc, S, dram):
    with ExitStack() as ctx:
        sb = lambda n, s: ctx.enter_context(nc.sbuf_tensor("f2_" + n, s, F32))
        sem = lambda n: S.sem("f2_" + n)
        C = lambda n: block_of(S, n)
        xr = sb("xr", [128, TOK])
        gates = sb("gates", [128, NT, EXPERTS])
        acc = sb("acc", [128, NT, 128])
        gu_w, down_w = sb("gu_w", [128, 2, 2 * HID]), sb("down_w", [128, 2, 3 * 128])
        w_in = [sem("w_in0"), sem("w_in1")]
        with ExitStack() as inner:
            block = inner.enter_context(nc.Block())

            @block.sync
            def _(sp):
                for k in range(2):
                    sp.dma_start(gu_w[:, k, :], dram["gate_up"][k, :, :]).then_inc(w_in[k], 16)
                    sp.dma_start(down_w[:, k, :], dram["down"][k, :, :]).then_inc(w_in[k], 16)
                sp.dma_start(S.yT[:, :], dram["y_t"]).then_inc(S.yt_in, 16)
                sp.dma_start(S.ytm[:, :], dram["y_tm"]).then_inc(S.ytm_in, 16)

            norm_stage(nc, S, "f2n", S.xn, xr, 1e-6, mean=C("j128"), gain=C("ffn_w"), within=(inner, block))

        with ExitStack() as inner:
            isb = lambda n, s: inner.enter_context(nc.sbuf_tensor("f2b_" + n, s, F32))
            ips = lambda n: inner.enter_context(nc.psum_tensor(f"f2b_{n}_ps", [128, HALF], F32))
            sil, hid = isb("sil", [128, 2, HALF]), isb("hid", [128, NH2, 3, HALF])
            g_ps, u_ps, d_ps = [ips("g0"), ips("g1")], [ips("u0"), ips("u1")], [ips("d0"), ips("d1")]
            gu_ready, sil_ready, hid_ready, d_ready, acc_ready = (sem(n) for n in ("gu", "sil", "hid", "d", "acc"))
            l_ps = inner.enter_context(nc.psum_tensor("f2a_l", [128, NT, EXPERTS], F32))
            l_ready = sem("l")
            block = inner.enter_context(nc.Block())

            @block.tensor
            def _(pe):
                for t in range(NT):
                    mm = nc.tensor.matmul(l_ps[:, t, :], xr[:, t * 128:(t + 1) * 128], C("router2"), start=True, stop=True)
                mm.then_inc(l_ready, 1)

            exponents, choice, gates_ready = top_two(nc, S, "f2t", l_ps[:, :, :], gates, isb, l_ready)
            UNITS = 3 * NH2
            FREE = 2

            @block.sync
            def _(sp):
                with sp.Fori(1, EXPERTS // 2) as i:
                    for k in range(2):
                        sp.wait_ge(d_ready, i * 4 + (2 * k - 2))
                        load_at = i * 2 + k
                        sp.dma_start(gu_w[:, k, :], dram["gate_up"][bass.ds(load_at, 1), :, :]).then_inc(w_in[k], 16)
                        sp.dma_start(down_w[:, k, :], dram["down"][bass.ds(load_at, 1), :, :]).then_inc(w_in[k], 16)

            @block.tensor
            def _(pe):
                with pe.Fori(0, EXPERTS // 2) as i:
                    for k in range(2):
                        pe.wait_ge(w_in[k], i * 32 + 32)
                        for h in range(NH2):
                            for c, m in enumerate(HCH):
                                u = UNITS * k + 3 * h + c
                                pe.wait_ge(hid_ready, i * (2 * UNITS) + (u - 1 + FREE))
                                x = xr[:, h * HALF:(h + 1) * HALF]
                                nc.tensor.matmul(g_ps[u % 2][0:m, :], gu_w[:, k, c * 128:c * 128 + m], x, start=True, stop=True)
                                nc.tensor.matmul(u_ps[u % 2][0:m, :], gu_w[:, k, HID + c * 128:HID + c * 128 + m], x,
                                                 start=True, stop=True).then_inc(gu_ready, 1)
                        for h in range(NH2):
                            pe.wait_ge(hid_ready, i * (2 * UNITS) + (UNITS * k + 3 * h + 3 + FREE))
                            pe.wait_ge(acc_ready, i * (2 * NT) + (NT * k + 4 * h + 4))
                            for j in range(4):
                                for c, m in enumerate(HCH):
                                    mm = nc.tensor.matmul(d_ps[h][:, j * 128:(j + 1) * 128],
                                                          hid[0:m, h, c, j * 128:(j + 1) * 128],
                                                          down_w[0:m, k, c * 128:(c + 1) * 128],
                                                          start=(c == 0), stop=(c == 2))
                            mm.then_inc(d_ready, 1)

            @block.scalar
            def _(act):
                def pair(i, units):
                    for u in units:
                        m = HCH[u % 3]
                        act.wait_ge(gu_ready, i * (2 * UNITS) + (u + 1))
                        nc.scalar.activation(sil[0:m, u % 2, :], g_ps[u % 2][0:m, :], ACT.Silu).then_inc(sil_ready, 1)

                pair(0, range(UNITS))
                exponents(act)
                pair(0, range(UNITS, 2 * UNITS))
                with act.Fori(1, EXPERTS // 2) as i:
                    pair(i, range(2 * UNITS))

            @block.vector
            def _(dve):
                nc.vector.memset(acc[:, 0:4, :], 0.0).then_inc(hid_ready, 1)
                nc.vector.memset(acc[:, 4:8, :], 0.0).then_inc(hid_ready, 1)
                dve.wait_ge(hid_ready, FREE)
                for t in range(NT):
                    nc.vector.memset(acc[:, t, 0:1], 0.0).then_inc(acc_ready, 1)

                def multiply(i, k):
                    for h in range(NH2):
                        for c, m in enumerate(HCH):
                            u = UNITS * k + 3 * h + c
                            dve.wait_ge(sil_ready, i * (2 * UNITS) + (u + 1))
                            nc.vector.tensor_tensor(hid[0:m, h, c, :], sil[0:m, u % 2, :], u_ps[u % 2][0:m, :],
                                                    ALU.mult).then_inc(hid_ready, 1)

                def add(i, k):
                    gate = slice(k, k + 1) if isinstance(i, int) else bass.ds(i * 2 + k, 1)
                    for t in range(NT):
                        h, j = t // 4, t % 4
                        if j == 0:
                            dve.wait_ge(d_ready, i * 4 + (2 * k + h + 1))
                        dve.wait_ge(acc_ready, i * (2 * NT) + (NT * k + t + 1))
                        nc.vector.scalar_tensor_tensor(
                            out=acc[:, t, :], in0=d_ps[h][:, j * 128:(j + 1) * 128], scalar=gates[:, t, gate],
                            in1=acc[:, t, :], op0=ALU.mult, op1=ALU.add).then_inc(acc_ready, 1)

                multiply(0, 0)
                choice(dve)
                dve.wait_ge(gates_ready, 1)
                add(0, 0)
                multiply(0, 1)
                add(0, 1)
                with dve.Fori(1, EXPERTS // 2) as i:
                    for k in range(2):
                        multiply(i, k)
                        add(i, k)

        with ExitStack() as inner:
            t_ps = inner.enter_context(nc.psum_tensor("f2c_t", [128, NH2, HALF], F32))
            moe = inner.enter_context(nc.sbuf_tensor("f2c_moe", [128, TOK], F32))
            alpha = inner.enter_context(nc.sbuf_tensor("f2c_alpha", [128, 1], F32))
            turned, alpha_ready, moe_ready, added = sem("turned"), sem("alpha"), sem("moe"), sem("added")
            block = inner.enter_context(nc.Block())

            @block.tensor
            def _(pe):
                for h in range(NH2):
                    for j in range(4):
                        mm = nc.tensor.transpose(t_ps[:, h, j * 128:(j + 1) * 128], acc[:, 4 * h + j, :], C("ident"))
                    mm.then_inc(turned, 1)

            @block.vector
            def _(dve):
                nc.vector.tensor_scalar(alpha[:, :], C("alpha"), -0.5, 2.0, ALU.max, ALU.min).then_inc(alpha_ready, 1)
                dve.wait_ge(alpha_ready, 1)
                for h in range(NH2):
                    t = slice(h * HALF, (h + 1) * HALF)
                    dve.wait_ge(turned, h + 1)
                    nc.vector.scalar_tensor_tensor(out=moe[:, t], in0=t_ps[:, h, :], scalar=alpha[:, 0:1],
                                                   in1=S.xn[:, t], op0=ALU.mult, op1=ALU.add).then_inc(moe_ready, 1)
                    dve.wait_ge(moe_ready, h + 1)
                    nc.vector.tensor_tensor(S.xT[:, t], S.xT[:, t], moe[:, t], ALU.add).then_inc(added, 1)

            norm_stage(nc, S, "n3", S.xT, S.xn, 1e-5, centre=C("c128"), mean=C("j128"), tables=True,
                       within=(inner, block), ready=added)


def context_stage(nc, S):
    DA = DC + 1
    with ExitStack() as ctx:
        sb = lambda n, s: ctx.enter_context(nc.sbuf_tensor("x3_" + n, s, F32))
        sem = lambda n: S.sem("x3_" + n)
        C = lambda n: block_of(S, n)
        q, qk = sb("q", [128, TOK]), sb("qk", [DA, TOK])
        vo = sb("vo", [DA, 128])
        z = sb("z", [DA, TOK])

        with ExitStack() as inner:
            ips = lambda n, s: inner.enter_context(nc.psum_tensor("x3a_" + n, s, F32))
            q_ps, k_ps, v_ps = ips("q_ps", [128, NH2, HALF]), ips("k_ps", [128, NH2, HALF]), ips("v_ps", [128, 128])
            q_ready, q_saved, k_ready, k_saved, v_ready, v_saved = (
                sem(n) for n in ("q", "qs", "k", "ks", "v", "vs"))
            block = inner.enter_context(nc.Block())

            @block.tensor
            def _(pe):
                for h in range(NH2):
                    nc.tensor.matmul(q_ps[:, h, :], C("wq3"), S.xn[:, h * HALF:(h + 1) * HALF],
                                     start=True, stop=True).then_inc(q_ready, 1)
                nc.tensor.matmul(v_ps[0:DA, :], C("wv3"), C("wo3"), start=True, stop=True).then_inc(v_ready, 1)
                for h in range(NH2):
                    pe.wait_ge(q_saved, h + 1)
                    nc.tensor.matmul(k_ps[0:DA, h, :], C("wk3"), q[:, h * HALF:(h + 1) * HALF],
                                     start=True, stop=True).then_inc(k_ready, 1)

            @block.scalar
            def _(act):
                act.wait_ge(v_ready, 1)
                nc.scalar.copy(vo[:, :], v_ps[0:DA, :]).then_inc(v_saved, 1)
                act.wait_ge(k_ready, 1)
                nc.scalar.copy(qk[:, 0:HALF], k_ps[0:DA, 0, :]).then_inc(k_saved, 1)

            @block.vector
            def _(dve):
                for h in range(NH2):
                    dve.wait_ge(q_ready, h + 1)
                    nc.vector.tensor_scalar(q[:, h * HALF:(h + 1) * HALF], q_ps[:, h, :], C("bq3"), (D // 8) ** -0.5,
                                            ALU.add, ALU.mult).then_inc(q_saved, 1)
                dve.wait_ge(k_ready, 2)
                nc.vector.tensor_copy(qk[:, HALF:TOK], k_ps[0:DA, 1, :]).then_inc(k_saved, 1)

        with ExitStack() as inner:
            isb = lambda n, s: inner.enter_context(nc.sbuf_tensor("x3b_" + n, s, F32))
            ips = lambda n: inner.enter_context(nc.psum_tensor(f"x3b_{n}_ps", [128, HALF], F32))
            p, pt = isb("p", [128, 2, NKC * KC]), isb("pt", [KC, 2, NKC * 128])
            nmax, total, rtotal = isb("nmax", [128, 2]), isb("total", [128, 2]), isb("rtotal", [128, 2])
            zt = isb("zt", [128, 2, DA])
            s_ps, t_ps, z_ps, w_ps = (
                [ips("s0"), ips("s1")], [ips("t0"), ips("t1")], [ips("z0"), ips("z1")], [ips("w0"), ips("w1")])
            (s_ready, max_ready, e_ready, r_ready, t_ready, pt_ready, z_ready, zt_ready, w_ready, z_saved, padded) = (
                sem(n) for n in ("s", "max", "e", "r", "t", "pt", "z", "zt", "w", "zs", "pad"))
            block = inner.enter_context(nc.Block())

            def steps():
                for n in range(NT + 3):
                    yield [(s, n - lag) for s, lag in (("untwist", 3), ("z", 2), ("score", 0), ("turn", 1))
                           if 0 <= n - lag < NT]

            @block.tensor
            def _(pe):
                for turn in steps():
                    for step, t in turn:
                        if step == "score":
                            if t == 0:
                                pe.wait_ge(S.yt_in, 16)
                                pe.wait_ge(S.ytm_in, 32)
                            if t >= 2:
                                pe.wait_ge(e_ready, t - 1)
                            for j in range(BT):
                                b = BT * t + j
                                mm = nc.tensor.matmul(s_ps[t % 2][j * NQ:(j + 1) * NQ, 0:SC], qk[:, b * NQ:(b + 1) * NQ],
                                                      S.yT[:, b * SC:(b + 1) * SC], start=True, stop=True)
                            mm.then_inc(s_ready, 1)
                        elif step == "turn":
                            pe.wait_ge(e_ready, t + 1)
                            if t == 0:
                                pe.wait_ge(padded, 2)
                            if t >= 2:
                                pe.wait_ge(pt_ready, t - 1)
                            for c in range(NKC):
                                mm = nc.tensor.transpose(t_ps[t % 2][0:KC, c * 128:(c + 1) * 128],
                                                         p[:, t % 2, c * KC:(c + 1) * KC], C("ident"))
                            mm.then_inc(t_ready, 1)
                        elif step == "z":
                            pe.wait_ge(pt_ready, t + 1)
                            if t >= 2:
                                pe.wait_ge(zt_ready, t - 1)
                            for c in range(NKC):
                                for j in range(BT):
                                    at = ((BT * t + j) * NKC + c) * DA
                                    mm = nc.tensor.matmul(z_ps[t % 2][j * NQ:(j + 1) * NQ, 0:DA],
                                                          pt[:, t % 2, c * 128 + j * NQ:c * 128 + (j + 1) * NQ],
                                                          S.ytm[:, at:at + DA], start=(c == 0), stop=(c == NKC - 1))
                            mm.then_inc(z_ready, 1)
                        else:
                            pe.wait_ge(zt_ready, t + 1)
                            if t >= 2:
                                pe.wait_ge(z_saved, t - 1)
                            nc.tensor.transpose(w_ps[t % 2][0:DA, 0:128], zt[:, t % 2, :], C("ident")).then_inc(w_ready, 1)

            @block.scalar
            def _(act):
                for turn in steps():
                    for step, t in turn:
                        if step == "score":
                            act.wait_ge(max_ready, t + 1)
                            if t >= 2:
                                act.wait_ge(t_ready, t - 1)
                            nc.scalar.activation(p[:, t % 2, 0:SC], s_ps[t % 2][:, 0:SC], ACT.Exp,
                                                 bias=nmax[:, t % 2:t % 2 + 1],
                                                 accum_out=total[:, t % 2:t % 2 + 1]).then_inc(e_ready, 1)
                        elif step == "z":
                            act.wait_ge(z_ready, t + 1)
                            act.wait_ge(r_ready, t + 1)
                            if t >= 2:
                                act.wait_ge(w_ready, t - 1)
                            nc.scalar.activation(zt[:, t % 2, :], z_ps[t % 2][:, 0:DA], ACT.Identity,
                                                 scale=rtotal[:, t % 2:t % 2 + 1]).then_inc(zt_ready, 1)

            @block.vector
            def _(dve):
                for k in range(2):
                    nc.vector.memset(p[:, k, SC:NKC * KC], 0.0).then_inc(padded, 1)
                for turn in steps():
                    for step, t in turn:
                        if step == "score":
                            dve.wait_ge(s_ready, t + 1)
                            nc.vector.tensor_reduce(nmax[:, t % 2:t % 2 + 1], s_ps[t % 2][:, 0:SC], AX.X, ALU.max,
                                                    negate=True).then_inc(max_ready, 1)
                        elif step == "untwist":
                            dve.wait_ge(w_ready, t + 1)
                            nc.vector.tensor_copy(z[:, t * 128:(t + 1) * 128], w_ps[t % 2][0:DA, 0:128]).then_inc(z_saved, 1)
                        elif step == "turn":
                            dve.wait_ge(e_ready, t + 1)
                            if t >= 2:
                                dve.wait_ge(zt_ready, t - 1)
                            nc.vector.reciprocal(rtotal[:, t % 2:t % 2 + 1],
                                                 total[:, t % 2:t % 2 + 1]).then_inc(r_ready, 1)
                            dve.wait_ge(t_ready, t + 1)
                            if t >= 2:
                                dve.wait_ge(z_ready, t - 1)
                            nc.vector.tensor_copy(pt[:, t % 2, :], t_ps[t % 2][0:KC, 0:NKC * 128]).then_inc(pt_ready, 1)

        with ExitStack() as inner:
            y_ps = inner.enter_context(nc.psum_tensor("x3c_y", [128, NH2, HALF], F32))
            y_ready, added = sem("y"), sem("added")
            block = inner.enter_context(nc.Block())

            @block.tensor
            def _(pe):
                for h in range(NH2):
                    nc.tensor.matmul(y_ps[:, h, :], vo[:, :], z[:, h * HALF:(h + 1) * HALF],
                                     start=True, stop=True).then_inc(y_ready, 1)

            @block.vector
            def _(dve):
                for h in range(NH2):
                    dve.wait_ge(y_ready, h + 1)
                    x = S.xT[:, h * HALF:(h + 1) * HALF]
                    nc.vector.scalar_tensor_tensor(out=x, in0=y_ps[:, h, :], scalar=C("bo3"), in1=x,
                                                   op0=ALU.add, op1=ALU.add).then_inc(added, 1)

            norm_stage(nc, S, "n4", S.xT, S.xn, 1e-5, centre=C("c128"), mean=C("j128"),
                       within=(inner, block), ready=added)


def delta_stage(nc, S, dram):
    with ExitStack() as ctx:
        sb = lambda n, s: ctx.enter_context(nc.sbuf_tensor("r4_" + n, s, F32))
        sem = lambda n: S.sem("r4_" + n)
        C = lambda n: block_of(S, n)
        half = lambda t, h: t[:, h * HALF:(h + 1) * HALF]
        x1, h1 = sb("x1", [128, TOK]), sb("h1", [128, TOK])
        q, k, v, beta = (sb(n, [128, TOK]) for n in ("q", "k", "v", "beta"))
        norm_stage(nc, S, "r4n", S.xn, h1, 1e-6, mean=C("j128"), gain=C("norm1"))

        with ExitStack() as inner:
            isb = lambda n, s: inner.enter_context(nc.sbuf_tensor("r4a_" + n, s, F32))
            p_ps = [inner.enter_context(nc.psum_tensor(f"r4a_p{n}", [128, HALF], F32)) for n in range(8)]
            keep = isb("keep", [128, 3])
            decay, ksq, kinv = isb("decay", [128, B, NQ]), isb("ksq", [128, TOK]), isb("kinv", [128, TOK])
            p_ready, k_saved, v_saved, q_saved, sq_ready, ss_ready = (
                sem(n) for n in ("p", "ks", "vs", "qs", "sq", "ss"))
            clipped, logged, kinv_ready, e_ready, ea_ready = (sem(n) for n in ("clip", "log", "kinv", "e", "ea"))
            chain_sem, done, raised, beta_ready = sem("chain"), sem("done"), sem("raised"), sem("betar")
            block = inner.enter_context(nc.Block())
            ORDER = ("wk4", "wb4", "wv4", "wq4")

            @block.tensor
            def _(pe):
                for n, w in enumerate(ORDER):
                    if n == 2:
                        for h in range(NH2):
                            pe.wait_ge(sq_ready, h + 1)
                            nc.tensor.matmul(p_ps[h][:, :], C("ones"), half(ksq, h), start=True, stop=True).then_inc(ss_ready, 1)
                    for h in range(NH2):
                        nc.tensor.matmul(p_ps[2 * n + h][:, :], C(w), half(h1, h), start=True, stop=True).then_inc(p_ready, 1)

            @block.scalar
            def _(act):
                nc.scalar.activation(keep[:, 0:1], C("decay"), ACT.Exp, scale=-1.0).then_inc(ea_ready, 1)
                for h in range(NH2):
                    act.wait_ge(p_ready, h + 1)
                    nc.scalar.copy(half(k, h), p_ps[h][:, :]).then_inc(k_saved, 1)
                    nc.scalar.activation(half(ksq, h), p_ps[h][:, :], ACT.Square).then_inc(sq_ready, 1)
                act.wait_ge(ea_ready, 3)
                for h in range(NH2):
                    act.wait_ge(p_ready, 2 + h + 1)
                    nc.scalar.activation(half(beta, h), p_ps[2 + h][:, :], ACT.Exp, scale=-1.0,
                                         bias=keep[:, 2:3]).then_inc(e_ready, 1)
                for h in range(NH2):
                    act.wait_ge(clipped, h + 1)
                    nc.scalar.activation(half(kinv, h), half(kinv, h), ACT.Ln).then_inc(logged, 1)
                    act.wait_ge(logged, h + 1)
                    nc.scalar.activation(half(kinv, h), half(kinv, h), ACT.Exp, scale=-0.5).then_inc(kinv_ready, 1)
                for h in range(NH2):
                    act.wait_ge(raised, h + 1)
                    nc.scalar.activation(half(beta, h), half(beta, h), ACT.Ln).then_inc(logged, 1)
                    act.wait_ge(logged, NH2 + h + 1)
                    nc.scalar.activation(half(beta, h), half(beta, h), ACT.Exp, scale=-1.0).then_inc(beta_ready, 1)
                for h in range(NH2):
                    act.wait_ge(p_ready, 6 + h + 1)
                    nc.scalar.copy(half(q, h), p_ps[6 + h][:, :]).then_inc(q_saved, 1)

            @block.vector
            def _(dve):
                step = Chain(dve, chain_sem)
                nc.vector.tensor_scalar(keep[:, 2:3], C("beta_b"), -1.0, None, ALU.mult).then_inc(ea_ready, 1)
                dve.wait_ge(ea_ready, 2)
                step(nc.vector.tensor_scalar(keep[:, 1:2], keep[:, 0:1], 1.0, None, ALU.add))
                step(nc.vector.reciprocal(keep[:, 1:2], keep[:, 1:2]))
                nc.vector.tensor_scalar(keep[:, 0:1], keep[:, 1:2], -1.0, 1.0, ALU.mult, ALU.add).then_inc(ea_ready, 1)
                step(nc.vector.memset(decay[:, :, :], 1.0))
                dve.wait_ge(ea_ready, 3)
                step(nc.vector.tensor_scalar(decay[:, :, :], decay[:, :, :], keep[:, 0:1], None, ALU.mult))
                step(nc.vector.memset(decay[:, :, 0:1], 0.0))
                for h in range(NH2):
                    dve.wait_ge(e_ready, h + 1)
                    nc.vector.tensor_scalar(half(beta, h), half(beta, h), 1.0, 2.0 ** 62, ALU.add, ALU.min).then_inc(raised, 1)
                for h in range(NH2):
                    dve.wait_ge(ss_ready, h + 1)
                    nc.vector.tensor_scalar(half(kinv, h), p_ps[h][:, :], 1e-24, LNS, ALU.max, ALU.mult).then_inc(clipped, 1)
                for h in range(NH2):
                    dve.wait_ge(p_ready, 4 + h + 1)
                    step(nc.vector.tensor_scalar(half(v, h), p_ps[4 + h][:, :], keep[:, 1:2], None, ALU.mult))
                    flat = decay[:, :, :].rearrange("p b t -> p (b t)")
                    step(nc.vector.tensor_tensor_scan(half(v, h), half(flat, h), half(v, h), 0.0, ALU.mult, ALU.add))
                for h in range(NH2):
                    dve.wait_ge(kinv_ready, h + 1)
                    nc.vector.scalar_tensor_tensor(out=half(k, h), in0=half(kinv, h), scalar=LNS ** 0.5, in1=half(k, h),
                                                   op0=ALU.mult, op1=ALU.mult).then_inc(done, 1)
                for h in range(NH2):
                    dve.wait_ge(beta_ready, h + 1)
                    step(nc.vector.tensor_tensor(half(v, h), half(v, h), half(beta, h), ALU.mult))

        o = sb("o", [128, TOK])
        with ExitStack() as inner:
            isb = lambda n: inner.enter_context(nc.sbuf_tensor(f"r4b_{n}", [128, TOK], F32))
            bt, qk, vt, inv, invt, x, u, low = (isb(n) for n in ("bt", "qk", "vt", "inv", "invt", "x", "u", "low"))
            LEVELS = (2, 4, 8, 16)
            m = [isb(f"m{n}") for n in LEVELS]
            a_ps, b_ps, c_ps, d_ps = ([inner.enter_context(nc.psum_tensor(f"r4b_{n}{h}", [128, HALF], F32))
                                       for h in range(NH2)] for n in "abcd")
            mm_done, dve_done, m_ready = ([sem(f"{n}{h}") for h in range(NH2)] for n in ("mm", "dv", "mr"))
            o_saved = sem("os")
            block = inner.enter_context(nc.Block())
            wide = lambda n: C(n).unsqueeze(1).to_broadcast([128, 4, 128])
            four = lambda t, h: half(t, h).rearrange("p (t n) -> p t n", t=4)
            bank = lambda p: p[:, :].rearrange("p (t n) -> p t n", t=4)
            MM_GRAM, MM_QK, MM_V, MM_TURN = 1, 2, 3, 4
            MM_X = lambda l: 5 + 3 * l
            MM_NEXT = lambda l: 7 + 3 * l if l < 3 else 15
            MM_U, MM_O = 16, 17
            DV_BT, DV_QK, DV_V, DV_INVT, DV_INV = 2, 3, 4, 6, 7
            DV_X = lambda l: 8 + 3 * l
            DV_LEVEL = lambda l: 10 + 3 * l if l < 3 else 18
            DV_U = 19

            def products(h, out, left, right):
                for j in range(4):
                    t = slice((4 * h + j) * 128, (4 * h + j + 1) * 128)
                    mm = nc.tensor.matmul(out[:, j * 128:(j + 1) * 128], left[:, t], right[:, t], start=True, stop=True)
                mm.then_inc(mm_done[h], 1)

            def turns(h, out, src):
                for j in range(4):
                    t = slice((4 * h + j) * 128, (4 * h + j + 1) * 128)
                    mm = nc.tensor.transpose(out[:, j * 128:(j + 1) * 128], src[:, t], C("ident"))
                mm.then_inc(mm_done[h], 1)

            @block.tensor
            def _(pe):
                for h in range(NH2):
                    products(h, a_ps[h], k, k)
                    products(h, b_ps[h], k, q)
                    turns(h, c_ps[h], v)
                for h in range(NH2):
                    pe.wait_ge(dve_done[h], DV_INVT)
                    turns(h, d_ps[h], invt)
                for l in range(len(LEVELS)):
                    for h in range(NH2):
                        pe.wait_ge(dve_done[h], DV_INV if l == 0 else DV_LEVEL(l - 1))
                        pe.wait_ge(m_ready[h], l + 1)
                        products(h, a_ps[h], m[l], inv)
                    for h in range(NH2):
                        pe.wait_ge(dve_done[h], DV_X(l))
                        products(h, b_ps[h], x, invt)
                        if l < 3:
                            products(h, c_ps[h], invt, x)
                for h in range(NH2):
                    pe.wait_ge(dve_done[h], DV_LEVEL(3))
                    products(h, a_ps[h], invt, vt)
                for h in range(NH2):
                    pe.wait_ge(dve_done[h], DV_U)
                    products(h, d_ps[h], u, qk)

            @block.scalar
            def _(act):
                for h in range(NH2):
                    act.wait_ge(mm_done[h], MM_O)
                    nc.scalar.copy(half(o, h), d_ps[h][:, :]).then_inc(o_saved, 1)

            @block.gpsimd
            def _(pool):
                for l, n in enumerate(LEVELS):
                    for h in range(NH2):
                        pool.wait_ge(dve_done[h], DV_BT)
                        nc.gpsimd.tensor_tensor(four(m[l], h), four(bt, h), wide(f"pair{n}"), ALU.mult).then_inc(m_ready[h], 1)
                nc.gpsimd.memset(S.kblk[:, :, :], 0.0).then_inc(S.blocks_set, 1)
                nc.gpsimd.memset(S.vblk[:, :, :, :], 0.0).then_inc(S.blocks_set, 1)
                pool.wait_ge(S.blocks_set, 2)
                for j in range(4):
                    nc.gpsimd.memset(S.vblk[j * NQ:(j + 1) * NQ, j, :, 4 * DHS:], 1.0).then_inc(S.blocks_set, 1)

            @block.vector
            def _(dve):
                count = [0, 0]

                def step(h, instruction):
                    count[h] += 1
                    instruction.then_inc(dve_done[h], 1)

                def after(h, products_done=None):
                    if products_done:
                        dve.wait_ge(mm_done[h], products_done)
                    if count[h]:
                        dve.wait_ge(dve_done[h], count[h])

                for h in range(NH2):
                    after(h, MM_GRAM)
                    step(h, nc.vector.tensor_tensor(four(low, h), bank(a_ps[h]), wide("before"), ALU.mult))
                    after(h)
                    step(h, nc.vector.tensor_tensor(half(bt, h), half(low, h), half(beta, h), ALU.mult))
                    after(h, MM_QK)
                    step(h, nc.vector.tensor_tensor(four(qk, h), bank(b_ps[h]), wide("upto"), ALU.mult))
                    after(h, MM_V)
                    step(h, nc.vector.tensor_copy(half(vt, h), c_ps[h][:, :]))
                    step(h, nc.vector.tensor_tensor(four(x, h), four(bt, h), wide("pair1"), ALU.mult))
                    after(h)
                    step(h, nc.vector.tensor_tensor(four(invt, h), wide("ident"), four(x, h), ALU.subtract))
                for h in range(NH2):
                    after(h, MM_TURN)
                    step(h, nc.vector.tensor_copy(half(inv, h), d_ps[h][:, :]))
                for l in range(len(LEVELS)):
                    for h in range(NH2):
                        after(h, MM_X(l))
                        step(h, nc.vector.tensor_copy(half(x, h), a_ps[h][:, :]))
                    for h in range(NH2):
                        after(h, MM_NEXT(l))
                        step(h, nc.vector.tensor_tensor(half(invt, h), half(invt, h), b_ps[h][:, :], ALU.subtract))
                        if l < 3:
                            step(h, nc.vector.tensor_tensor(half(inv, h), half(inv, h), c_ps[h][:, :], ALU.subtract))
                for h in range(NH2):
                    after(h, MM_U)
                    step(h, nc.vector.tensor_copy(half(u, h), a_ps[h][:, :]))

        with ExitStack() as inner:
            y_ps = inner.enter_context(nc.psum_tensor("r4c_y", [128, NH2, HALF], F32))
            y_ready, x1_ready = sem("y"), sem("x1r")
            block = inner.enter_context(nc.Block())

            @block.tensor
            def _(pe):
                for h in range(NH2):
                    nc.tensor.matmul(y_ps[:, h, :], C("wo4"), half(o, h), start=True, stop=True).then_inc(y_ready, 1)

            @block.gpsimd
            def _(pool):
                nc.gpsimd.dma_start(S.w_k[:, :], dram["qkvo"][0, :, 0:129]).then_inc(S.k_in, 16)
                nc.gpsimd.dma_start(S.w_qv[:, :], dram["qkvo"][0, :, 129:386]).then_inc(S.qv_in, 16)
                nc.gpsimd.dma_start(S.w_next[:, :], dram["qkvo"][0, :, 386:515]).then_inc(S.next_in, 16)

            @block.vector
            def _(dve):
                for h in range(NH2):
                    dve.wait_ge(y_ready, h + 1)
                    nc.vector.tensor_tensor(half(x1, h), half(S.xn, h), y_ps[:, h, :], ALU.add).then_inc(x1_ready, 1)

            norm_stage(nc, S, "r4m", x1, h1, 1e-6, mean=C("j128"), gain=C("norm2"), within=(inner, block), ready=x1_ready)

        with ExitStack() as inner:
            isb = lambda n, s: inner.enter_context(nc.sbuf_tensor("r4d_" + n, s, F32))
            ips = lambda n: inner.enter_context(nc.psum_tensor(f"r4d_{n}_ps", [128, HALF], F32))
            sil, hid = isb("sil", [128, 4, HALF]), isb("hid", [128, 4, HALF])
            g_ps, u_ps, d_ps = [ips("g0"), ips("g1")], [ips("u0"), ips("u1")], [ips("d0"), ips("d1")]
            gu_ready, sil_ready, hid_ready, d_ready, res_ready, added = (
                sem(n) for n in ("gu", "sil", "hid", "d", "res", "add"))
            block = inner.enter_context(nc.Block())

            @block.tensor
            def _(pe):
                for n in range(4):
                    h, c = n // 2, n % 2
                    if n >= 2:
                        pe.wait_ge(hid_ready, n - 1)
                    w = slice(c * 128, (c + 1) * 128)
                    nc.tensor.matmul(g_ps[c][:, :], C("gate4")[:, w], half(h1, h), start=True, stop=True)
                    nc.tensor.matmul(u_ps[c][:, :], C("up4")[:, w], half(h1, h), start=True, stop=True).then_inc(gu_ready, 1)
                for h in range(NH2):
                    pe.wait_ge(hid_ready, 2 * h + 2)
                    for c in range(2):
                        mm = nc.tensor.matmul(d_ps[h][:, :], C("down4")[:, c * 128:(c + 1) * 128], hid[:, 2 * h + c, :],
                                              start=(c == 0), stop=(c == 1))
                    mm.then_inc(d_ready, 1)

            @block.scalar
            def _(act):
                for n in range(4):
                    act.wait_ge(gu_ready, n + 1)
                    nc.scalar.activation(sil[:, n, :], g_ps[n % 2][:, :], ACT.Silu).then_inc(sil_ready, 1)

            @block.vector
            def _(dve):
                for n in range(4):
                    dve.wait_ge(sil_ready, n + 1)
                    nc.vector.tensor_tensor(hid[:, n, :], sil[:, n, :], u_ps[n % 2][:, :], ALU.mult).then_inc(hid_ready, 1)
                for h in range(NH2):
                    nc.vector.tensor_tensor(half(S.xT, h), half(S.xT, h), half(x1, h), ALU.add).then_inc(res_ready, 1)
                for h in range(NH2):
                    dve.wait_ge(d_ready, h + 1)
                    dve.wait_ge(res_ready, h + 1)
                    nc.vector.tensor_tensor(half(S.xT, h), half(S.xT, h), d_ps[h][:, :], ALU.add).then_inc(added, 1)


def experts_stage(nc, S, dram):
    with ExitStack() as ctx:
        sb = lambda n, s: ctx.enter_context(nc.sbuf_tensor("e5_" + n, s, F32))
        sem = lambda n: S.sem("e5_" + n)
        C = lambda n: block_of(S, n)
        half = lambda t, h: t[:, h * HALF:(h + 1) * HALF]
        NR = D // 2
        gates, gates_t = sb("gates", [128, NT, EXPERTS]), sb("gates_t", [EXPERTS, TOK])
        acc = sb("acc", [128, NT, 128])
        vblk, kblk, w_k, w_qv, w_next = S.vblk, S.kblk, S.w_k, S.w_qv, S.w_next
        k_in, qv_in, next_in = S.k_in, S.qv_in, S.next_in
        kt = sb("kt", [128, TOK])
        k_ready, k_saved, k_spread = sem("k"), sem("ks"), [sem("kspread0"), sem("kspread1")]

        def spread_keys(sp, e, h):
            k = slice(h * HALF, (h + 1) * HALF)
            sp.wait_ge(k_saved, e * 2 + (h + 1))
            for head in range(HS):
                r = slice(head * DHS, (head + 1) * DHS)
                sp.dma_start(kblk[r, head, k], kt[r, k]).then_inc(k_spread[h], 16)

        by_group = vblk[:, :, :, :].rearrange("p j n (d g) -> p j n d g", g=4)

        def values(j, b, h):
            return vblk[j * NQ:(j + 1) * NQ, j, :, 0:4 * DHS].rearrange(
                "p (h t b) c -> p h t b c", h=2, b=BT)[:, h, :, b, :]


        with ExitStack() as inner:
            isb = lambda n, s: inner.enter_context(nc.sbuf_tensor("e5d_" + n, s, F32))
            ips = lambda n: inner.enter_context(nc.psum_tensor(f"e5d_{n}_ps", [128, NH2, HALF], F32))
            hr, hn = isb("hr", [NR, TOK]), isb("hn", [NR, TOK])
            w_o, qt = isb("w_o", [128, 129]), isb("qt", [128, TOK])
            p, pt = isb("p", [128, 2, HS, NQ]), isb("pt", [128, 2, 4, 128])
            nmax, rsum = isb("nmax", [128, 2, HS]), isb("rsum", [128, HS])
            on, ot = isb("on", [128, 2, 128]), isb("ot", [128, 2, 128])
            h_ps, k_ps, centred_ps, var_ps = ips("qk_v"), ips("s"), ips("t_o"), ips("ot_y")
            bank = lambda pair, n: pair[:, n, :]
            qk_ps, v_ps, s_ps = bank(h_ps, 0), bank(h_ps, 1), [bank(k_ps, 0), bank(k_ps, 1)]
            t_ps, o_ps, ot_ps, y_ps = bank(centred_ps, 0), bank(centred_ps, 1), bank(var_ps, 0), bank(var_ps, 1)
            l_ps = o_ps[:, 0:NT * EXPERTS].rearrange("p (t e) -> p t e", t=NT)
            h_ready, h_saved, l_ready, g_ready, g_saved = sem("h"), sem("hs"), sem("l"), sem("g"), sem("gs")
            wo_ready, q_ready, q_saved = sem("wo"), sem("q"), sem("qs")
            v_ready, v_spread_dve, v_spread_act = sem("v"), sem("vsd"), sem("vsa")
            s_ready, max_ready, sub_ready, e_ready = sem("s"), sem("max"), sem("sub"), sem("e")
            t_ready, pt_saved, o_ready, rsum_ready = sem("t"), sem("pts"), sem("o"), sem("rsum")
            on_ready, ot_ready, ot_saved, y_ready, acc_ready = sem("on"), sem("ot"), sem("ots"), sem("y"), sem("acc")
            x_ready, x_saved, ob_ready = sem("x"), sem("xs"), sem("ob")
            block = inner.enter_context(nc.Block())
            ROUND = range(NT // 2, NT + NT // 2)

            def reach(engine, semaphore, value):
                if not isinstance(value, int) or value > 0:
                    engine.wait_ge(semaphore, value)

            def live(e, t):
                return not isinstance(e, int) or 0 <= e * NT + t < EXPERTS * NT

            def coming(e):
                return not isinstance(e, int) or e + 1 < EXPERTS

            def second_keys(e):
                return not isinstance(e, int) or 0 <= e < EXPERTS - 1

            def first_keys(e):
                return not isinstance(e, int) or e < EXPERTS - 2

            @block.tensor
            def _(pe):
                for h in range(NH2):
                    nc.tensor.matmul(h_ps[0:NR, h, :], C("rw1"), half(S.xn, h), start=True, stop=True).then_inc(h_ready, 1)
                pe.wait_ge(k_in, 16)
                for h in range(NH2):
                    nc.tensor.matmul(k_ps[:, h, :], w_k[:, 0:128], half(S.xn, h), start=True, stop=True).then_inc(k_ready, 1)

            @block.scalar
            def _(act):
                for h in range(NH2):
                    act.wait_ge(k_ready, h + 1)
                    nc.scalar.activation(half(kt, h), k_ps[:, h, :], ACT.Identity,
                                         bias=w_k[:, 128:129]).then_inc(k_saved, 1)

            @block.vector
            def _(dve):
                for h in range(NH2):
                    dve.wait_ge(h_ready, h + 1)
                    nc.vector.tensor_scalar(half(hr, h), h_ps[0:NR, h, :], C("rb1")[0:NR, :], None,
                                            ALU.add).then_inc(h_saved, 1)

            hn_ready = norm_stage(nc, S, "e5n", hr, hn, 1e-5, feats=NR, centre=C("c64")[0:NR, :],
                                  mean=C("j64")[0:NR, :], gain=C("ln_g")[0:NR, :], shift=C("ln_b")[0:NR, :],
                                  relu=True, within=(inner, block), ready=h_saved, banks=(centred_ps, var_ps))
            exponents, choice, gates_ready = top_two(nc, S, "e5t", l_ps, gates, lambda n, s: isb("t_" + n, s), l_ready,
                                                     bias=C("rb2").unsqueeze(1).to_broadcast([128, NT, EXPERTS]))

            @block.gpsimd
            def _(pool):
                with pool.Fori(1, EXPERTS) as e:
                    pool.wait_ge(k_saved, e * 2)
                    nc.gpsimd.dma_start(w_k[:, :], dram["qkvo"][bass.ds(e, 1), :, 0:129]).then_inc(k_in, 16)
                    pool.wait_ge(q_saved, e * 2)
                    pool.wait_ge(v_ready, e * 2)
                    nc.gpsimd.dma_start(w_qv[:, :], dram["qkvo"][bass.ds(e, 1), :, 129:386]).then_inc(qv_in, 16)
                    pool.wait_ge(wo_ready, e * 1)
                    nc.gpsimd.dma_start(w_next[:, :], dram["qkvo"][bass.ds(e, 1), :, 386:515]).then_inc(next_in, 16)

            @block.sync
            def _(sp):
                spread_keys(sp, 0, 0)
                spread_keys(sp, 0, 1)
                with sp.Fori(1, EXPERTS) as e:
                    for h in range(2):
                        spread_keys(sp, e, h)
                out = dram["out"].rearrange("(t p) d -> p t d", p=128)
                for h in range(2):
                    sp.wait_ge(acc_ready, 1 + (EXPERTS - 1) * NT + 4 * h + 4)
                    sp.dma_start(out[:, 4 * h:4 * h + 4, :], acc[:, 4 * h:4 * h + 4, :]).then_inc(S.stored, 16)
                sp.wait_ge(S.stored, 32)

            @block.tensor
            def _(pe):

                def turn_gates():
                    pe.wait_ge(gates_ready, 1)
                    for t in range(NT):
                        mm = nc.tensor.transpose(centred_ps[0:EXPERTS, t // 4, t % 4 * 128:(t % 4 + 1) * 128],
                                                 gates[:, t, :], C("ident"))
                    mm.then_inc(g_ready, 1)

                def output_biases():
                    for t in range(NT):
                        nc.tensor.matmul(var_ps[:, t // 4, t % 4 * 128:(t % 4 + 1) * 128], gates_t[:, t * 128:(t + 1) * 128],
                                         C("ob")[0:EXPERTS, :], start=True, stop=True).then_inc(ob_ready, 1)

                def rounds(e):
                    for n in ROUND:
                        h = n // 4 - 1
                        if live(e, n):
                            t = n
                            if t % 4 == 0:
                                pe.wait_ge(q_saved, e * 2 + (t // 4 + 1))
                                pe.wait_ge(k_spread[t // 4 % 2], e * (16 * HS) + 16 * HS * (t // NT + 1))
                            reach(pe, sub_ready, e * NT + (t - 1))
                            for b in range(BT):
                                at = t % NT * 128 + b * NQ
                                mm = nc.tensor.matmul(s_ps[t % 2][b * NQ:(b + 1) * NQ, :], qt[:, at:at + NQ],
                                                      kblk[:, :, at:at + NQ], start=True, stop=True)
                            mm.then_inc(s_ready, 1)
                        if isinstance(e, int) and e < 0 and n == 8:
                            turn_gates()
                        if isinstance(e, int) and e < 0 and n == 10:
                            output_biases()
                        if isinstance(e, int) and e < 0 and n == 9:
                            pe.wait_ge(g_saved, NH2)
                        if n == 7 and second_keys(e):
                            pe.wait_ge(q_saved, e * 2 + 3)
                            nc.tensor.matmul(qk_ps[:, :], w_k[:, 0:128], half(S.xn, 1),
                                             start=True, stop=True).then_inc(k_ready, 1)
                        if n == 11 and first_keys(e):
                            pe.wait_ge(k_in, e * 16 + 48)
                            pe.wait_ge(q_saved, e * 2 + 4)
                            nc.tensor.matmul(qk_ps[:, :], w_k[:, 0:128], half(S.xn, 0),
                                             start=True, stop=True).then_inc(k_ready, 1)
                        if live(e, n - 4):
                            t = n - 4
                            if t % NT == 0:
                                pe.wait_ge(wo_ready, e + (t // NT + 1))
                            pe.wait_ge(ot_saved, e * NT + (t + 1))
                            pe.wait_ge(acc_ready, e * NT + (t + 1))
                            nc.tensor.matmul(y_ps[:, 0:128], ot[:, t % 2, :], w_o[:, 0:128],
                                             start=True, stop=True).then_inc(y_ready, 1)
                        if live(e, n - 3):
                            t = n - 3
                            pe.wait_ge(on_ready, e * NT + (t + 1))
                            reach(pe, ot_saved, e * NT + t)
                            nc.tensor.transpose(ot_ps[:, 0:128], on[:, t % 2, :], C("ident")).then_inc(ot_ready, 1)
                        if live(e, n - 2):
                            t = n - 2
                            if t % 4 == 0:
                                pe.wait_ge(v_spread_dve, e * 2 + (t // 4 + 1))
                                pe.wait_ge(v_spread_act, e * 2 + (t // 4 + 1))
                            pe.wait_ge(pt_saved, e * NT + (t + 1))
                            reach(pe, on_ready, e * NT + t)
                            for g in range(4):
                                for b in range(BT):
                                    mm = nc.tensor.matmul(
                                        o_ps[b * NQ:(b + 1) * NQ, g * 36:(g + 1) * 36],
                                        pt[:, t % 2, g, b * NQ:(b + 1) * NQ],
                                        by_group[:, :, t % NT * BT + b, :, g], start=True, stop=True)
                            mm.then_inc(o_ready, 1)
                        if coming(e) and n % 4 == 1:
                            if h == 0:
                                pe.wait_ge(qv_in, e * 16 + 32)
                            pe.wait_ge(k_saved, e * 2 + (h + 3))
                            nc.tensor.matmul(qk_ps[:, :], w_qv[:, 0:128], half(S.xn, h),
                                             start=True, stop=True).then_inc(q_ready, 1)
                            reach(pe, v_spread_dve, e * 2 + (h + 2))
                            reach(pe, v_spread_act, e * 2 + (h + 2))
                            for t in range(4):
                                at = h * HALF + t * 128
                                mm = nc.tensor.matmul(v_ps[:, t * 128:(t + 1) * 128], S.xn[:, at:at + 128],
                                                      w_qv[:, 128:256], start=True, stop=True)
                            mm.then_inc(v_ready, 1)
                        if live(e, n - 1):
                            t = n - 1
                            pe.wait_ge(e_ready, e * NT + (t + 1))
                            reach(pe, pt_saved, e * NT + t)
                            for g in range(4):
                                mm = nc.tensor.transpose(t_ps[:, g * 128:(g + 1) * 128],
                                                         p[:, t % 2, 4 * g:4 * g + 4, :].rearrange("p h k -> p (h k)"),
                                                         C("ident"))
                            mm.then_inc(t_ready, 1)

                pe.wait_ge(k_saved, NH2)
                for t in range(NT):
                    nc.tensor.transpose(k_ps[:, t // 4, t % 4 * 128:(t % 4 + 1) * 128], S.xT[:, t * 128:(t + 1) * 128],
                                        C("ident")).then_inc(x_ready, 1)
                pe.wait_ge(hn_ready, NH2)
                for t in range(NT):
                    mm = nc.tensor.matmul(l_ps[:, t, :], hn[:, t * 128:(t + 1) * 128], C("rw2")[0:NR, :], start=True, stop=True)
                mm.then_inc(l_ready, 1)
                rounds(-1)
                with pe.Fori(0, EXPERTS - 2) as e:
                    rounds(e)
                rounds(EXPERTS - 2)
                rounds(EXPERTS - 1)

            @block.scalar
            def _(act):

                def rounds(e):
                    for n in ROUND:
                        h = n // 4 - 1
                        if live(e, n - 3):
                            t = n - 3
                            if t % NT == 0:
                                act.wait_ge(next_in, e * 16 + 16 * (t // NT + 1))
                                reach(act, y_ready, e * NT + t)
                                nc.scalar.copy(w_o[:, :], w_next[:, :]).then_inc(wo_ready, 1)
                                act.wait_ge(wo_ready, e + (t // NT + 1))
                            act.wait_ge(ot_ready, e * NT + (t + 1))
                            reach(act, acc_ready, e * NT + t)
                            nc.scalar.activation(ot[:, t % 2, :], ot_ps[:, 0:128], ACT.Identity,
                                                 bias=w_o[:, 128:129]).then_inc(ot_saved, 1)
                        if live(e, n):
                            t = n
                            act.wait_ge(sub_ready, e * NT + (t + 1))
                            nc.scalar.activation(p[:, t % 2, :, :], p[:, t % 2, :, :], ACT.Exp,
                                                 scale=DHS ** -0.5).then_inc(e_ready, 1)
                        if coming(e) and n % 4 == 1:
                            act.wait_ge(q_ready, e * 2 + (h + 3))
                            nc.scalar.activation(half(qt, h), qk_ps[:, :], ACT.Identity,
                                                 bias=w_qv[:, 256:257]).then_inc(q_saved, 1)
                        if n == 7 and second_keys(e):
                            act.wait_ge(k_ready, e * 2 + 4)
                            reach(act, k_spread[1], e * (16 * HS) + 16 * HS)
                            nc.scalar.activation(half(kt, 1), qk_ps[:, :], ACT.Identity,
                                                 bias=w_k[:, 128:129]).then_inc(k_saved, 1)
                        if n == 11 and first_keys(e):
                            act.wait_ge(k_ready, e * 2 + 5)
                            act.wait_ge(k_spread[0], e * (16 * HS) + 32 * HS)
                            nc.scalar.activation(half(kt, 0), qk_ps[:, :], ACT.Identity,
                                                 bias=w_k[:, 128:129]).then_inc(k_saved, 1)
                        if live(e, n - 1):
                            t = n - 1
                            act.wait_ge(t_ready, e * NT + (t + 1))
                            reach(act, o_ready, e * NT + (t - 1))
                            nc.scalar.copy(pt[:, t % 2, :, :].rearrange("p g q -> p (g q)"), t_ps[:, :]).then_inc(pt_saved, 1)
                        if coming(e) and n % 4 >= 2:
                            if n % 4 == 2:
                                act.wait_ge(v_ready, e * 2 + (h + 3))
                            for j in (0, 1) if n % 4 == 2 else (2, 3):
                                for b in (2, 3):
                                    mm = nc.scalar.copy(values(j, b, h), v_ps[b * NQ:(b + 1) * NQ, :].rearrange(
                                        "p (t j c) -> p t j c", t=4, j=4)[:, :, j, :])
                            if n % 4 == 3:
                                mm.then_inc(v_spread_act, 1)

                for h in range(NH2):
                    act.wait_ge(x_ready, 4 * h + 4)
                    nc.scalar.copy(acc[:, 4 * h:4 * h + 4, :].rearrange("p t d -> p (t d)"),
                                   k_ps[:, h, :]).then_inc(x_saved, 1)
                exponents(act)
                rounds(-1)
                with act.Fori(0, EXPERTS - 2) as e:
                    rounds(e)
                rounds(EXPERTS - 2)
                rounds(EXPERTS - 1)

            @block.vector
            def _(dve):
                def rounds(e):
                    for n in ROUND:
                        h = n // 4 - 1
                        if live(e, n):
                            t = n
                            dve.wait_ge(s_ready, e * NT + (t + 1))
                            s = s_ps[t % 2][:, :].rearrange("p (h k) -> p h k", h=HS)
                            nc.vector.tensor_reduce(nmax[:, t % 2, :], s, AX.X, ALU.max).then_inc(max_ready, 1)
                            dve.wait_ge(max_ready, e * NT + (t + 1))
                            reach(dve, t_ready, e * NT + (t - 1))
                            nc.vector.tensor_tensor(p[:, t % 2, :, :], s,
                                                    nmax[:, t % 2, :].unsqueeze(2).to_broadcast([128, HS, NQ]),
                                                    ALU.subtract).then_inc(sub_ready, 1)
                        if isinstance(e, int) and e < 0 and n == 8:
                            dve.wait_ge(g_ready, 1)
                            for k in range(NH2):
                                nc.vector.tensor_copy(half(gates_t, k), centred_ps[0:EXPERTS, k, :]).then_inc(g_saved, 1)
                        if isinstance(e, int) and e < 0 and n == 10:
                            dve.wait_ge(x_saved, NH2)
                            for k in range(NH2):
                                dve.wait_ge(ob_ready, 4 * k + 4)
                                a = acc[:, 4 * k:4 * k + 4, :].rearrange("p t d -> p (t d)")
                                mm = nc.vector.tensor_tensor(a, a, var_ps[:, k, :], ALU.add)
                            mm.then_inc(acc_ready, 1)
                        if live(e, n - 4):
                            t = n - 4
                            dve.wait_ge(y_ready, e * NT + (t + 1))
                            dve.wait_ge(acc_ready, e * NT + (t + 1))
                            gate = e if t < NT else e + 1
                            gate = slice(gate, gate + 1) if isinstance(e, int) else bass.ds(gate, 1)
                            nc.vector.scalar_tensor_tensor(
                                out=acc[:, t % NT, :], in0=y_ps[:, 0:128], scalar=gates[:, t % NT, gate],
                                in1=acc[:, t % NT, :], op0=ALU.mult, op1=ALU.add).then_inc(acc_ready, 1)
                        if live(e, n - 2):
                            t = n - 2
                            dve.wait_ge(o_ready, e * NT + (t + 1))
                            o = o_ps[:, 0:HS * (DHS + 1)].rearrange("p (h d) -> p h d", h=HS)
                            nc.vector.reciprocal(rsum[:, :], o[:, :, DHS]).then_inc(rsum_ready, 1)
                            dve.wait_ge(rsum_ready, e * NT + (t + 1))
                            reach(dve, ot_ready, e * NT + (t - 1))
                            nc.vector.tensor_tensor(on[:, t % 2, :].rearrange("p (h d) -> p h d", h=HS), o[:, :, 0:DHS],
                                                    rsum[:, :].unsqueeze(2).to_broadcast([128, HS, DHS]),
                                                    ALU.mult).then_inc(on_ready, 1)
                        if coming(e) and n % 4 >= 2:
                            if n % 4 == 2:
                                dve.wait_ge(v_ready, e * 2 + (h + 3))
                            for j in (0, 1) if n % 4 == 2 else (2, 3):
                                for b in (0, 1):
                                    mm = nc.vector.tensor_copy(values(j, b, h), v_ps[b * NQ:(b + 1) * NQ, :].rearrange(
                                        "p (t j c) -> p t j c", t=4, j=4)[:, :, j, :])
                            if n % 4 == 3:
                                mm.then_inc(v_spread_dve, 1)

                choice(dve)
                rounds(-1)
                with dve.Fori(0, EXPERTS - 2) as e:
                    rounds(e)
                rounds(EXPERTS - 2)
                rounds(EXPERTS - 1)


EPS = (1e-5, 1e-6)


def program(nc, dram):
    with ExitStack() as ctx:
        S = Shared()
        sb = lambda n, s, dt=F32: ctx.enter_context(nc.sbuf_tensor(n, s, dt))
        S.sem = lambda n: ctx.enter_context(nc.semaphore(n))
        S.xT, S.xn = sb("xT", [D, TOK]), sb("xn", [D, TOK])
        S.const, S.vec, S.wts = sb("const", [128, N_CONST]), sb("vec", [128, N_VEC]), sb("wts", [128, N_WTS])
        S.epst = sb("epst", [128, len(EPS)])
        S.eps = lambda e: S.epst[:, EPS.index(e):EPS.index(e) + 1]
        S.x_in, S.const_in, S.wts_in = S.sem("x_in"), S.sem("const_in"), S.sem("wts_in")
        S.yt_in, S.ytm_in, S.mask_in = S.sem("yt_in"), S.sem("ytm_in"), S.sem("mask_in")
        S.ytm_rest_in = S.sem("ytm_rest_in")
        S.blocks_set, S.k_in, S.qv_in, S.next_in = (S.sem(n) for n in ("blocks_set", "k_in", "qv_in", "next_in"))
        S.wd_in, S.stored = S.sem("wd_in"), S.sem("stored")
        context = ExitStack()
        csb = lambda n, s, dt=F32: context.enter_context(nc.sbuf_tensor(n, s, dt))
        S.ytm = csb("ytm", [KC, B * NKC * (DC + 1)])
        S.mask = csb("mask", [128, B // 2 * MASK_WORDS], I32)
        diff_weights = ExitStack()
        S.wd = diff_weights.enter_context(nc.sbuf_tensor("wd", [128, 5 * 2048], F32))
        eps_set = S.sem("eps_set")
        with nc.Block() as block:

            @block.scalar
            def _(act):
                nc.scalar.preload_act_table_set("natural_log_exp_and_others")

            @block.vector
            def _(dve):
                for n, e in enumerate(EPS):
                    nc.vector.memset(S.epst[:, n:n + 1], e).then_inc(eps_set, 1)

            @block.gpsimd
            def _(pool):
                pool.wait_ge(eps_set, len(EPS))
        load_stage(nc, S, dram)
        stage_sems = []

        def stage_sem(name):
            stage_sems.append(nc.alloc_semaphore(name=name))
            return stage_sems[-1]

        def recycle():
            nc.clear_and_free_semaphores(list(stage_sems))
            nc.all_engine_barrier()
            stage_sems.clear()

        S.sem = stage_sem
        C = lambda n: block_of(S, n)
        cross_stage(nc, S)
        diff_stage(nc, S, dram)
        recycle()
        diff_weights.close()
        S.yT = csb("yT", [DC + 1, B * SC])
        ffn_stage(nc, S, dram)
        context_stage(nc, S)
        recycle()
        context.close()
        S.vblk = sb("vblk", [128, 4, B, (DHS + 1) * 4])
        S.kblk = sb("kblk", [128, HS, TOK])
        S.w_k = sb("w_k", [128, 129])
        S.w_qv = sb("w_qv", [128, 257])
        S.w_next = sb("w_next", [128, 129])
        delta_stage(nc, S, dram)
        norm_stage(nc, S, "n5", S.xT, S.xn, 1e-5, centre=C("c128"), mean=C("j128"), tables=True)
        experts_stage(nc, S, dram)


def constants():
    p = np.arange(128)
    c = np.zeros((128, N_CONST), np.float32)

    def put(name, a):
        at, width = CONST[name]
        c[:a.shape[0], at:at + width] = a

    same = p[:, None] // NQ == p[None, :] // NQ
    put("ident", np.eye(128))
    for n in (128, 96, 64):
        put(f"c{n}", np.eye(n) - 1.0 / n)
    put("j128", np.full((128, 128), 1 / 128))
    put("j96", np.full((96, 128), 1 / 96))
    put("j64", np.full((64, 64), 1 / 64))
    put("heads64", (p[:, None] // 64 == p[None, :] // 64) / 64)
    put("headq", (p[:, None] // 64 == np.arange(64)[None, :] // NQ) / 64)
    put("ones", np.ones((128, 128)))
    put("before", same & (p[:, None] < p[None, :]))
    put("upto", same & (p[:, None] <= p[None, :]))
    for n in (1, 2, 4, 8, 16):
        put(f"pair{n}", (p[:, None] // (2 * n) == p[None, :] // (2 * n))
            & (p[:, None] // n % 2 == 0) & (p[None, :] // n % 2 == 1))
    put("rank", np.broadcast_to(8.0 - np.arange(64) % 8, (128, 64)))
    return c


def laid_out(i):
    i = {k: np.asarray(v) for k, v in i.items()}
    f = np.float32

    def pack(where, total, items):
        a = np.zeros((128, total), f)
        for name, v in items.items():
            at, width = where[name]
            a[:v.shape[0], at:at + width] = v
        return a

    col = lambda v: v.reshape(-1, 1)
    rep = lambda v: np.broadcast_to(v.reshape(1, -1), (128, v.size))
    ctx = i["ctx_768"]
    vec = pack(VEC, N_VEC, {
        "x_g": col(i["L0_xattn_ln_x_g"]), "x_b": col(i["L0_xattn_ln_x_b"]),
        "l_g": col(i["L0_xattn_ln_l_g"]), "l_b": col(i["L0_xattn_ln_l_b"]),
        "qn_g": col(np.tile(i["L0_xattn_qn_g"], HC)), "kn_g": col(np.tile(i["L0_xattn_kn_g"], HC)),
        "bo0": col(i["L0_xattn_bo"]), "ffn_w": col(i["L0_ffn_norm_weight"]),
        "alpha": rep(i["L0_ffn_residual_alpha"]), "bq3": col(i["L1_xattn_bq"]), "bo3": col(i["L1_xattn_bo"]),
        "norm1": col(i["L1_attn_norm1_w"]), "norm2": col(i["L1_attn_norm2_w"]),
        "decay": col(i["L1_attn_alpha_logit"]), "beta_b": rep(i["L1_attn_beta_b"]),
        "rb1": col(i["L1_ffn_rb1"]), "ln_g": col(i["L1_ffn_ln_g"]), "ln_b": col(i["L1_ffn_ln_b"]),
        "rs": i["L0_attn_rms_scale"].reshape(2, 128).T, "rb2": rep(i["L1_ffn_rb2"]),
    })
    wkv, wlkv = i["L0_xattn_Wkv"], i["L0_xattn_Wlkv"]
    wts = pack(WTS, N_WTS, {
        "wq0": i["L0_xattn_Wq"].T, "wk0": wkv[:128].T, "wv0": wkv[128:].T,
        "wlk0": wlkv[:128].T, "wlv0": wlkv[128:].T, "wo0": i["L0_xattn_Wo"].T,
        "lq1": i["L0_attn_lambda_q1"].T, "lk1": i["L0_attn_lambda_k1"].T,
        "lq2": i["L0_attn_lambda_q2"].T, "lk2": i["L0_attn_lambda_k2"].T,
        "router2": i["L0_ffn_router_weight"].T,
        "wq3": i["L1_xattn_Wq"],
        "wk3": np.concatenate([i["L1_xattn_Wk"].T, col(i["L1_xattn_bk"])], 1),
        "wv3": np.concatenate([i["L1_xattn_Wv"].T, col(i["L1_xattn_bv"])], 1),
        "wo3": i["L1_xattn_Wo"],
        "wq4": i["L1_attn_Wq"], "wk4": i["L1_attn_Wk"], "wv4": i["L1_attn_Wv"], "wo4": i["L1_attn_Wo"],
        "wb4": np.broadcast_to(i["L1_attn_beta_w"], (128, 128)),
        "gate4": i["L1_attn_w_gate"], "up4": i["L1_attn_w_up"],
        "down4": i["L1_attn_w_down"].reshape(2, 128, 128).transpose(1, 0, 2).reshape(128, 256),
        "rw1": i["L1_ffn_rW1"].T, "rw2": i["L1_ffn_rW2"].T, "ob": i["L1_ffn_ob"],
    })
    y_tm = np.zeros((B, NKC * KC, DC + 1), f)
    y_tm[:, :SC, :DC] = ctx
    y_tm[:, :SC, DC] = 1.0
    y_t = np.ones((DC + 1, B * SC), f)
    y_t[:DC] = ctx.reshape(B * SC, DC).T
    rows = lambda w: w.reshape(16, 128, 128).transpose(1, 0, 2).reshape(128, 2048)
    wd = np.concatenate([
        rows(i["L0_attn_Wq"]), rows(i["L0_attn_Wk"]), i["L0_attn_Wv"].T, rows(i["L0_attn_Wv"]),
        rows(np.ascontiguousarray(i["L0_attn_Wo"].T))], 1)
    down = np.zeros((EXPERTS, 3 * 128, 128), f)
    down[:, :HID] = i["L0_ffn_down_weight"].transpose(0, 2, 1)
    w = {n: i[f"L1_ffn_{n}W"].transpose(0, 2, 1) for n in "qkvo"}
    w["v"] = w["v"].reshape(EXPERTS, 128, 4, 4, DHS).transpose(0, 1, 3, 4, 2).reshape(EXPERTS, 128, 128)
    bias = {n: i[f"L1_ffn_{n}b"][:, :, None] for n in "qkv"}
    qkvo = np.concatenate([w["k"], bias["k"], w["q"], w["v"], bias["q"], w["o"], bias["v"]], 2)
    mask = np.zeros((B, 4 * MASK_WORDS), bool)
    mask[:, :SC] = i["mask_BxS2_bk0"]
    return {
        "x_t": i["x"].reshape(TOK, D).T, "y_t": y_t,
        "y_tm": y_tm.reshape(B, NKC, KC, DC + 1).transpose(2, 0, 1, 3).reshape(KC, -1),
        "mask": mask.view(np.int32), "const": constants(), "vec": vec, "wts": wts,
        "wd": wd, "gate_up": i["L0_ffn_gate_up_weight"].transpose(0, 2, 1),
        "down": down.reshape(EXPERTS, 3, 128, 128).transpose(0, 2, 1, 3).reshape(EXPERTS, 128, 384),
        "qkvo": qkvo,
    }


def kernel(**inputs):
    import numpy as _np
    import concourse.bacc as _bacc
    from concourse.bass_utils import run_bass_kernel_spmd as _run

    nc = _bacc.Bacc("TRN2", target_bir_lowering=False, num_devices=1)
    arrays, dram = {}, {}
    for name, a in laid_out(inputs).items():
        a = _np.ascontiguousarray(a)
        arrays[f"in_{name}"] = a
        dram[name] = nc.dram_tensor(f"in_{name}", a.shape, mybir.dt.from_np(a.dtype), kind="ExternalInput").ap()
    dram["out"] = nc.dram_tensor("out_0", (TOK, D), F32, kind="ExternalOutput").ap()
    program(nc, dram)
    r = _run(nc, [arrays], core_ids=[0])
    return r.results[0]["out_0"].reshape(B, NQ, D)
```
